# Optimizing a Trainium2 kernel written in Bass

```python
import numpy as np
import jax
import jax.numpy as jnp

def _softmax(x, axis=-1):
    return jax.nn.softmax(x, axis=axis)

def _gelu(x):
    return jax.nn.gelu(x, approximate=True)

def _silu(x):
    return jax.nn.silu(x)

def _sigmoid(x):
    return jax.nn.sigmoid(x)

def _layernorm(x, axis=-1, eps=1e-05):
    m = jnp.mean(x, axis=axis, keepdims=True)
    v = jnp.var(x, axis=axis, keepdims=True)
    return (x - m) / jnp.sqrt(v + eps)

def _scatter_add(tgt, idx, src, axis=0):
    return tgt.at[idx].add(src)

def _segment_sum(src, seg, n):
    return jax.ops.segment_sum(src, seg, n)
kernel_name = 'mk_recurrent_d2_jaxref_r8_da6baa'

def setup_inputs(seed: int=0):
    np.random.seed(seed)
    _w = jnp.asarray

    def _L0_attn_setup():
        import jax, jax.numpy as jnp
        import numpy as np
        B, T, D = (4, 256, 128)
        H, Kd = (4, 32)
        Vd = 64
        KEY_DIM, VAL_DIM = (H * Kd, H * Vd)
        CONV = 4
        EPS = 1e-06
        LN_EPS = 1e-05

        def _layernorm(x, g, b):
            m = jnp.mean(x, -1, keepdims=True)
            v = jnp.mean((x - m) ** 2, -1, keepdims=True)
            return (x - m) * jax.lax.rsqrt(v + LN_EPS) * g + b

        def _rmsnorm(x, w):
            return x * jax.lax.rsqrt(jnp.mean(x * x, -1, keepdims=True) + EPS) * w

        def _l2norm(x):
            return x * jax.lax.rsqrt(jnp.sum(x * x, -1, keepdims=True) + EPS)

        def _causal_conv_silu(x, w):
            t = x.shape[1]
            xp = jnp.pad(x, ((0, 0), (CONV - 1, 0), (0, 0)))
            y = xp[:, 0:t, :] * w[:, 0]
            for i in range(1, CONV):
                y = y + xp[:, i:i + t, :] * w[:, i]
            return jax.nn.silu(y)

        def _gated_delta_rule(q, k, v, g, beta):
            qT = jnp.moveaxis(q, 1, 0)
            kT = jnp.moveaxis(k, 1, 0)
            vT = jnp.moveaxis(v, 1, 0)
            gT = jnp.moveaxis(g, 1, 0)
            bT = jnp.moveaxis(beta, 1, 0)
            S0 = jnp.zeros((q.shape[0], H, Kd, Vd), q.dtype)

            def step(S, inp):
                q_t, k_t, v_t, g_t, b_t = inp
                S = S * jnp.exp(g_t)[..., None, None]
                kv = jnp.einsum('bhk,bhkv->bhv', k_t, S)
                delta = (v_t - kv) * b_t[..., None]
                S = S + k_t[..., :, None] * delta[..., None, :]
                o = jnp.einsum('bhk,bhkv->bhv', q_t, S)
                return (S, o)
            _, o = jax.lax.scan(step, S0, (qT, kT, vT, gT, bT))
            return jnp.moveaxis(o, 0, 1)

        def _forward(x, ln1_g, ln1_b, ln2_g, ln2_b, rms_in_w, Wq, Wk, Wv, conv_q_w, conv_k_w, conv_v_w, Wa, dt_bias, A_log, Wb, Wg, o_norm_w, Wo, W2, b2):
            b, t, _ = x.shape
            h = _layernorm(x, ln1_g, ln1_b)
            h = _rmsnorm(h, rms_in_w)
            q = _causal_conv_silu(h @ Wq, conv_q_w).reshape(b, t, H, Kd)
            k = _causal_conv_silu(h @ Wk, conv_k_w).reshape(b, t, H, Kd)
            v = _causal_conv_silu(h @ Wv, conv_v_w).reshape(b, t, H, Vd)
            q = _l2norm(q) * Kd ** (-0.5)
            k = _l2norm(k)
            g = -jnp.exp(A_log) * jax.nn.softplus(h @ Wa + dt_bias)
            beta = jax.nn.sigmoid(h @ Wb)
            o = _gated_delta_rule(q, k, v, g, beta)
            gate = (h @ Wg).reshape(b, t, H, Vd)
            o = _rmsnorm(o, o_norm_w) * jax.nn.silu(gate)
            enc = o.reshape(b, t, VAL_DIM) @ Wo
            x = x + enc
            h2 = _layernorm(x, ln2_g, ln2_b)
            x_out = jax.nn.gelu(h2 @ W2 + b2, approximate=False) + x
            return x_out
        key = jax.random.key(seed)
        ks = jax.random.split(key, 16)
        r = lambda k, shp, s=0.02: jax.random.normal(k, shp, dtype=jnp.float32) * s
        return {'x': jax.random.normal(ks[0], (B, T, D), dtype=jnp.float32), 'ln1_g': jnp.ones((D,), jnp.float32), 'ln1_b': jnp.zeros((D,), jnp.float32), 'ln2_g': jnp.ones((D,), jnp.float32), 'ln2_b': jnp.zeros((D,), jnp.float32), 'rms_in_w': jnp.ones((D,), jnp.float32), 'Wq': r(ks[1], (D, KEY_DIM)), 'Wk': r(ks[2], (D, KEY_DIM)), 'Wv': r(ks[3], (D, VAL_DIM)), 'conv_q_w': r(ks[4], (KEY_DIM, CONV), 0.3), 'conv_k_w': r(ks[5], (KEY_DIM, CONV), 0.3), 'conv_v_w': r(ks[6], (VAL_DIM, CONV), 0.3), 'Wa': r(ks[7], (D, H)), 'dt_bias': r(ks[8], (H,), 0.5), 'A_log': jnp.log(jax.random.uniform(ks[9], (H,), minval=1.0, maxval=16.0)), 'Wb': r(ks[10], (D, H)), 'Wg': r(ks[11], (D, VAL_DIM)), 'o_norm_w': jnp.ones((Vd,), jnp.float32), 'Wo': r(ks[12], (VAL_DIM, D)), 'W2': r(ks[13], (D, D)), 'b2': jnp.zeros((D,), jnp.float32)}
    _L0_attn_in = _L0_attn_setup()

    def _L0_ffn_setup():
        import jax, jax.numpy as jnp
        import numpy as np
        B, S, D, F, E, TOP_K = (4, 256, 128, 512, 8, 2)
        LN_EPS = 1e-05
        key = jax.random.key(seed)
        ks = jax.random.split(key, 4)
        sc = lambda fan_in: 1.0 / np.sqrt(fan_in)
        return {'x': jax.random.normal(ks[0], (B, S, D), jnp.float32), 'W1': jax.random.normal(ks[1], (E, D, F), jnp.float32) * sc(D), 'b1': jnp.zeros((E, F), jnp.float32), 'W2': jax.random.normal(ks[2], (E, F, D), jnp.float32) * sc(F), 'b2': jnp.zeros((E, D), jnp.float32), 'Wr': jax.random.normal(ks[3], (D, E), jnp.float32) * sc(D), 'br': jnp.zeros((E,), jnp.float32), 'gamma': jnp.ones((D,), jnp.float32), 'beta': jnp.zeros((D,), jnp.float32)}
    _L0_ffn_in = _L0_ffn_setup()

    def _L1_attn_setup():
        import jax, jax.numpy as jnp
        import numpy as np
        B, T, D_MODEL, NH, HD = (2, 256, 128, 16, 64)
        INNER = NH * HD
        SPIKE_ALPHA, THR_MIN, THR_MAX = (1.0, 0.01, 10.0)
        ROPE_BASE = 10000.0

        def _ternary_ste(x):
            thr = jax.lax.stop_gradient(jnp.clip(SPIKE_ALPHA * jnp.mean(jnp.abs(x)), THR_MIN, THR_MAX))
            q = jnp.where(x > thr, 1.0, jnp.where(x < -thr, -1.0, 0.0)).astype(x.dtype)
            return x + jax.lax.stop_gradient(q - x)

        def _rope_tables(t_len, dim, dtype):
            inv_freq = 1.0 / ROPE_BASE ** (jnp.arange(0, dim, 2, dtype=jnp.float32) / dim)
            freqs = jnp.arange(t_len, dtype=jnp.float32)[:, None] * inv_freq[None, :]
            return (jnp.cos(freqs).astype(dtype), jnp.sin(freqs).astype(dtype))

        def _rotary(x, cos, sin):
            d2 = x.shape[-1] // 2
            x1, x2 = (x[..., :d2], x[..., d2:])
            c = cos[None, :, None, :]
            s = sin[None, :, None, :]
            return jnp.concatenate([x1 * c - x2 * s, x2 * c + x1 * s], axis=-1)
        key = jax.random.key(seed)
        ks = jax.random.split(key, 8)
        x = jax.random.normal(ks[0], (B, T, D_MODEL), dtype=jnp.float32)
        Wq = jax.random.normal(ks[1], (INNER, D_MODEL), dtype=jnp.float32) * 0.02
        Wk = jax.random.normal(ks[2], (INNER, D_MODEL), dtype=jnp.float32) * 0.02
        Wv = jax.random.normal(ks[3], (INNER, D_MODEL), dtype=jnp.float32) * 0.02
        Wo = jax.random.normal(ks[4], (D_MODEL, INNER), dtype=jnp.float32) * 0.02
        Wb = jax.random.normal(ks[5], (NH, D_MODEL), dtype=jnp.float32) * 0.02
        bb = jnp.zeros((NH,), dtype=jnp.float32)
        alpha_log = -2.0 + 0.5 * jax.random.normal(ks[6], (NH, 1), dtype=jnp.float32)
        return {'x': x, 'Wq': Wq, 'Wk': Wk, 'Wv': Wv, 'Wo': Wo, 'Wb': Wb, 'bb': bb, 'alpha_log': alpha_log}
    _L1_attn_in = _L1_attn_setup()

    def _L1_ffn_setup():
        import jax, jax.numpy as jnp
        import numpy as np
        H = 8
        KD = 128
        TOPK = 8
        NUM_KEYS = 32
        N_EXPERTS = NUM_KEYS * NUM_KEYS
        N_DIM = 128
        BN_EPS = 1e-05

        def gelu_new(x):
            c = jnp.sqrt(jnp.asarray(2.0 / jnp.pi, x.dtype))
            return 0.5 * x * (1.0 + jnp.tanh(c * (x + 0.044715 * x * x * x)))
        key = jax.random.key(seed)
        ks = jax.random.split(key, 5)
        b, s = (2, 128)
        x = jax.random.normal(ks[0], (b, s, N_DIM), dtype=jnp.float32)
        w_q = jax.random.normal(ks[1], (N_DIM, 2 * H * KD), dtype=jnp.float32) * 0.02
        bn_gamma = jnp.ones((2 * H * KD,), dtype=jnp.float32)
        bn_beta = jnp.zeros((2 * H * KD,), dtype=jnp.float32)
        keys = jax.random.normal(ks[2], (H, NUM_KEYS, 2, KD), dtype=jnp.float32) * 0.02
        down_embed = jax.random.normal(ks[3], (N_EXPERTS, N_DIM), dtype=jnp.float32) * 0.02
        up_embed = jax.random.normal(ks[4], (N_EXPERTS, N_DIM), dtype=jnp.float32) * 0.02
        return {'x': x, 'w_q': w_q, 'bn_gamma': bn_gamma, 'bn_beta': bn_beta, 'keys': keys, 'down_embed': down_embed, 'up_embed': up_embed}
    _L1_ffn_in = _L1_ffn_setup()
    _d = {'L0_attn_x': _L0_attn_in['x'], 'L0_attn_ln1_g': _L0_attn_in['ln1_g'], 'L0_attn_ln1_b': _L0_attn_in['ln1_b'], 'L0_attn_ln2_g': _L0_attn_in['ln2_g'], 'L0_attn_ln2_b': _L0_attn_in['ln2_b'], 'L0_attn_rms_in_w': _L0_attn_in['rms_in_w'], 'L0_attn_Wq': _L0_attn_in['Wq'], 'L0_attn_Wk': _L0_attn_in['Wk'], 'L0_attn_Wv': _L0_attn_in['Wv'], 'L0_attn_conv_q_w': _L0_attn_in['conv_q_w'], 'L0_attn_conv_k_w': _L0_attn_in['conv_k_w'], 'L0_attn_conv_v_w': _L0_attn_in['conv_v_w'], 'L0_attn_Wa': _L0_attn_in['Wa'], 'L0_attn_dt_bias': _L0_attn_in['dt_bias'], 'L0_attn_A_log': _L0_attn_in['A_log'], 'L0_attn_Wb': _L0_attn_in['Wb'], 'L0_attn_Wg': _L0_attn_in['Wg'], 'L0_attn_o_norm_w': _L0_attn_in['o_norm_w'], 'L0_attn_Wo': _L0_attn_in['Wo'], 'L0_attn_W2': _L0_attn_in['W2'], 'L0_attn_b2': _L0_attn_in['b2'], 'L0_ffn_W1': _L0_ffn_in['W1'], 'L0_ffn_b1': _L0_ffn_in['b1'], 'L0_ffn_W2': _L0_ffn_in['W2'], 'L0_ffn_b2': _L0_ffn_in['b2'], 'L0_ffn_Wr': _L0_ffn_in['Wr'], 'L0_ffn_br': _L0_ffn_in['br'], 'L0_ffn_gamma': _L0_ffn_in['gamma'], 'L0_ffn_beta': _L0_ffn_in['beta'], 'L1_attn_Wq': _L1_attn_in['Wq'], 'L1_attn_Wk': _L1_attn_in['Wk'], 'L1_attn_Wv': _L1_attn_in['Wv'], 'L1_attn_Wo': _L1_attn_in['Wo'], 'L1_attn_Wb': _L1_attn_in['Wb'], 'L1_attn_bb': _L1_attn_in['bb'], 'L1_attn_alpha_log': _L1_attn_in['alpha_log'], 'L1_ffn_w_q': _L1_ffn_in['w_q'], 'L1_ffn_bn_gamma': _L1_ffn_in['bn_gamma'], 'L1_ffn_bn_beta': _L1_ffn_in['bn_beta'], 'L1_ffn_keys': _L1_ffn_in['keys'], 'L1_ffn_down_embed': _L1_ffn_in['down_embed'], 'L1_ffn_up_embed': _L1_ffn_in['up_embed']}
    _x0 = _d['L0_attn_x']
    _d['L0_attn_x'] = jax.random.normal(jax.random.fold_in(jax.random.key(seed), 1), (2, 1024, 128), dtype=_x0.dtype)
    del _x0
    return _d

def reference(L0_attn_x, L0_attn_ln1_g, L0_attn_ln1_b, L0_attn_ln2_g, L0_attn_ln2_b, L0_attn_rms_in_w, L0_attn_Wq, L0_attn_Wk, L0_attn_Wv, L0_attn_conv_q_w, L0_attn_conv_k_w, L0_attn_conv_v_w, L0_attn_Wa, L0_attn_dt_bias, L0_attn_A_log, L0_attn_Wb, L0_attn_Wg, L0_attn_o_norm_w, L0_attn_Wo, L0_attn_W2, L0_attn_b2, L0_ffn_W1, L0_ffn_b1, L0_ffn_W2, L0_ffn_b2, L0_ffn_Wr, L0_ffn_br, L0_ffn_gamma, L0_ffn_beta, L1_attn_Wq, L1_attn_Wk, L1_attn_Wv, L1_attn_Wo, L1_attn_Wb, L1_attn_bb, L1_attn_alpha_log, L1_ffn_w_q, L1_ffn_bn_gamma, L1_ffn_bn_beta, L1_ffn_keys, L1_ffn_down_embed, L1_ffn_up_embed):

    def _L0_attn_ref(x, ln1_g, ln1_b, ln2_g, ln2_b, rms_in_w, Wq, Wk, Wv, conv_q_w, conv_k_w, conv_v_w, Wa, dt_bias, A_log, Wb, Wg, o_norm_w, Wo, W2, b2):
        import jax, jax.numpy as jnp
        import numpy as np
        B, T, D = (4, 256, 128)
        H, Kd = (4, 32)
        Vd = 64
        KEY_DIM, VAL_DIM = (H * Kd, H * Vd)
        CONV = 4
        EPS = 1e-06
        LN_EPS = 1e-05

        def _layernorm(x, g, b):
            m = jnp.mean(x, -1, keepdims=True)
            v = jnp.mean((x - m) ** 2, -1, keepdims=True)
            return (x - m) * jax.lax.rsqrt(v + LN_EPS) * g + b

        def _rmsnorm(x, w):
            return x * jax.lax.rsqrt(jnp.mean(x * x, -1, keepdims=True) + EPS) * w

        def _l2norm(x):
            return x * jax.lax.rsqrt(jnp.sum(x * x, -1, keepdims=True) + EPS)

        def _causal_conv_silu(x, w):
            t = x.shape[1]
            xp = jnp.pad(x, ((0, 0), (CONV - 1, 0), (0, 0)))
            y = xp[:, 0:t, :] * w[:, 0]
            for i in range(1, CONV):
                y = y + xp[:, i:i + t, :] * w[:, i]
            return jax.nn.silu(y)

        def _gated_delta_rule(q, k, v, g, beta):
            qT = jnp.moveaxis(q, 1, 0)
            kT = jnp.moveaxis(k, 1, 0)
            vT = jnp.moveaxis(v, 1, 0)
            gT = jnp.moveaxis(g, 1, 0)
            bT = jnp.moveaxis(beta, 1, 0)
            S0 = jnp.zeros((q.shape[0], H, Kd, Vd), q.dtype)

            def step(S, inp):
                q_t, k_t, v_t, g_t, b_t = inp
                S = S * jnp.exp(g_t)[..., None, None]
                kv = jnp.einsum('bhk,bhkv->bhv', k_t, S)
                delta = (v_t - kv) * b_t[..., None]
                S = S + k_t[..., :, None] * delta[..., None, :]
                o = jnp.einsum('bhk,bhkv->bhv', q_t, S)
                return (S, o)
            _, o = jax.lax.scan(step, S0, (qT, kT, vT, gT, bT))
            return jnp.moveaxis(o, 0, 1)

        def _forward(x, ln1_g, ln1_b, ln2_g, ln2_b, rms_in_w, Wq, Wk, Wv, conv_q_w, conv_k_w, conv_v_w, Wa, dt_bias, A_log, Wb, Wg, o_norm_w, Wo, W2, b2):
            b, t, _ = x.shape
            h = _layernorm(x, ln1_g, ln1_b)
            h = _rmsnorm(h, rms_in_w)
            q = _causal_conv_silu(h @ Wq, conv_q_w).reshape(b, t, H, Kd)
            k = _causal_conv_silu(h @ Wk, conv_k_w).reshape(b, t, H, Kd)
            v = _causal_conv_silu(h @ Wv, conv_v_w).reshape(b, t, H, Vd)
            q = _l2norm(q) * Kd ** (-0.5)
            k = _l2norm(k)
            g = -jnp.exp(A_log) * jax.nn.softplus(h @ Wa + dt_bias)
            beta = jax.nn.sigmoid(h @ Wb)
            o = _gated_delta_rule(q, k, v, g, beta)
            gate = (h @ Wg).reshape(b, t, H, Vd)
            o = _rmsnorm(o, o_norm_w) * jax.nn.silu(gate)
            enc = o.reshape(b, t, VAL_DIM) @ Wo
            x = x + enc
            h2 = _layernorm(x, ln2_g, ln2_b)
            x_out = jax.nn.gelu(h2 @ W2 + b2, approximate=False) + x
            return x_out
        return _forward(x, ln1_g, ln1_b, ln2_g, ln2_b, rms_in_w, Wq, Wk, Wv, conv_q_w, conv_k_w, conv_v_w, Wa, dt_bias, A_log, Wb, Wg, o_norm_w, Wo, W2, b2)

    def _L0_ffn_ref(x, W1, b1, W2, b2, Wr, br, gamma, beta):
        import jax, jax.numpy as jnp
        import numpy as np
        B, S, D, F, E, TOP_K = (4, 256, 128, 512, 8, 2)
        LN_EPS = 1e-05
        b, s, d = x.shape
        e = Wr.shape[1]
        rw = jax.nn.softmax(x.mean(axis=1) @ Wr + br, axis=-1)
        x_flat = x.reshape(-1, d)
        rw_tok = jnp.repeat(rw, s, axis=0)
        tk_w, tk_i = jax.lax.top_k(rw_tok, TOP_K)
        tk_w = jax.nn.softmax(tk_w, axis=-1)
        h = jax.nn.gelu(jnp.einsum('nd,edf->enf', x_flat, W1) + b1[:, None, :], approximate=False)
        expert_out = jnp.einsum('enf,efd->end', h, W2) + b2[:, None, :]
        onehot = jax.nn.one_hot(tk_i, e, dtype=x.dtype)
        cw = jnp.einsum('nk,nke->ne', tk_w, onehot)
        out = jnp.einsum('ne,end->nd', cw, expert_out).reshape(b, s, d)
        y = out + x
        mu = y.mean(axis=-1, keepdims=True)
        var = y.var(axis=-1, keepdims=True)
        return (y - mu) / jnp.sqrt(var + LN_EPS) * gamma + beta

    def _L1_attn_ref(x, Wq, Wk, Wv, Wo, Wb, bb, alpha_log):
        import jax, jax.numpy as jnp
        import numpy as np
        B, T, D_MODEL, NH, HD = (2, 256, 128, 16, 64)
        INNER = NH * HD
        SPIKE_ALPHA, THR_MIN, THR_MAX = (1.0, 0.01, 10.0)
        ROPE_BASE = 10000.0

        def _ternary_ste(x):
            thr = jax.lax.stop_gradient(jnp.clip(SPIKE_ALPHA * jnp.mean(jnp.abs(x)), THR_MIN, THR_MAX))
            q = jnp.where(x > thr, 1.0, jnp.where(x < -thr, -1.0, 0.0)).astype(x.dtype)
            return x + jax.lax.stop_gradient(q - x)

        def _rope_tables(t_len, dim, dtype):
            inv_freq = 1.0 / ROPE_BASE ** (jnp.arange(0, dim, 2, dtype=jnp.float32) / dim)
            freqs = jnp.arange(t_len, dtype=jnp.float32)[:, None] * inv_freq[None, :]
            return (jnp.cos(freqs).astype(dtype), jnp.sin(freqs).astype(dtype))

        def _rotary(x, cos, sin):
            d2 = x.shape[-1] // 2
            x1, x2 = (x[..., :d2], x[..., d2:])
            c = cos[None, :, None, :]
            s = sin[None, :, None, :]
            return jnp.concatenate([x1 * c - x2 * s, x2 * c + x1 * s], axis=-1)
        b, t, _ = x.shape
        q = (x @ Wq.T).reshape(b, t, NH, HD)
        k = (x @ Wk.T).reshape(b, t, NH, HD)
        v = (x @ Wv.T).reshape(b, t, NH, HD)
        cos, sin = _rope_tables(t, HD, x.dtype)
        q = _rotary(q, cos, sin)
        k = _rotary(k, cos, sin)
        k = _ternary_ste(k.reshape(b, t, INNER)).reshape(b, t, NH, HD)
        v = _ternary_ste(v.reshape(b, t, INNER)).reshape(b, t, NH, HD)
        alpha = jax.nn.sigmoid(alpha_log)
        beta = jax.nn.sigmoid(x @ Wb.T + bb)
        log_alpha = jnp.log(jnp.clip(alpha[:, 0], 1e-06, None))
        pos = jnp.arange(t, dtype=jnp.float32)
        time_diff = pos[:, None] - pos[None, :]
        decay_exp = time_diff[None, :, :] * log_alpha[:, None, None]
        causal = jnp.triu(jnp.ones((t, t), dtype=bool), k=1)
        decay = jnp.exp(jnp.where(causal[None], -jnp.inf, decay_exp)).astype(q.dtype)
        qk = jnp.einsum('bihd,bjhd->bhij', q, k)
        beta_k = jnp.transpose(beta, (0, 2, 1))[:, :, None, :]
        weights = qk * decay[None] * beta_k
        out = jnp.einsum('bhij,bjhd->bihd', weights, v)
        out = out.reshape(b, t, INNER) @ Wo.T
        return out

    def _L1_ffn_ref(x, w_q, bn_gamma, bn_beta, keys, down_embed, up_embed):
        import jax, jax.numpy as jnp
        import numpy as np
        H = 8
        KD = 128
        TOPK = 8
        NUM_KEYS = 32
        N_EXPERTS = NUM_KEYS * NUM_KEYS
        N_DIM = 128
        BN_EPS = 1e-05

        def gelu_new(x):
            c = jnp.sqrt(jnp.asarray(2.0 / jnp.pi, x.dtype))
            return 0.5 * x * (1.0 + jnp.tanh(c * (x + 0.044715 * x * x * x)))
        b, n, d = x.shape
        q = jnp.einsum('bnd,de->bne', x, w_q)
        mean = jnp.mean(q, axis=(0, 1))
        var = jnp.var(q, axis=(0, 1))
        q = (q - mean) * jax.lax.rsqrt(var + BN_EPS) * bn_gamma + bn_beta
        q = q.reshape(b, n, 2, H, KD).transpose(2, 0, 1, 3, 4)
        sim = jnp.einsum('pbnhd,hkpd->pbnhk', q, keys)
        sx, ix = jax.lax.top_k(sim[0], TOPK)
        sy, iy = jax.lax.top_k(sim[1], TOPK)
        all_scores = (sx[..., :, None] + sy[..., None, :]).reshape(b, n, H, TOPK * TOPK)
        all_indices = (ix[..., :, None] * NUM_KEYS + iy[..., None, :]).reshape(b, n, H, TOPK * TOPK)
        scores, pk = jax.lax.top_k(all_scores, TOPK)
        indices = jnp.take_along_axis(all_indices, pk, axis=-1)
        wd = down_embed[indices]
        wu = up_embed[indices]
        h = jnp.einsum('bnd,bnhkd->bnhk', x, wd)
        h = gelu_new(h)
        h = jax.nn.softmax(scores, axis=-1) * h
        out = jnp.einsum('bnhk,bnhkd->bnd', h, wu)
        return out
    x = L0_attn_x
    xn = _layernorm(x, axis=-1)
    s = _L0_attn_ref(xn, L0_attn_ln1_g, L0_attn_ln1_b, L0_attn_ln2_g, L0_attn_ln2_b, L0_attn_rms_in_w, L0_attn_Wq, L0_attn_Wk, L0_attn_Wv, L0_attn_conv_q_w, L0_attn_conv_k_w, L0_attn_conv_v_w, L0_attn_Wa, L0_attn_dt_bias, L0_attn_A_log, L0_attn_Wb, L0_attn_Wg, L0_attn_o_norm_w, L0_attn_Wo, L0_attn_W2, L0_attn_b2)
    g = _silu(_L0_ffn_ref(xn, L0_ffn_W1, L0_ffn_b1, L0_ffn_W2, L0_ffn_b2, L0_ffn_Wr, L0_ffn_br, L0_ffn_gamma, L0_ffn_beta))
    x = x + s * g
    xn = _layernorm(x, axis=-1)
    s = _L1_attn_ref(xn, L1_attn_Wq, L1_attn_Wk, L1_attn_Wv, L1_attn_Wo, L1_attn_Wb, L1_attn_bb, L1_attn_alpha_log)
    g = _silu(_L1_ffn_ref(xn, L1_ffn_w_q, L1_ffn_bn_gamma, L1_ffn_bn_beta, L1_ffn_keys, L1_ffn_down_embed, L1_ffn_up_embed))
    x = x + s * g
    return x

_drawn_inputs = setup_inputs


def setup_inputs(seed=0):
    import zlib

    import numpy as np

    out = dict(_drawn_inputs(seed))
    spreads = {'L0_attn_ln1_g': (1.0, 0.6),
     'L0_attn_ln1_b': (0.0, 0.8),
     'L0_attn_ln2_g': (1.0, 0.6),
     'L0_attn_ln2_b': (0.0, 0.8),
     'L0_attn_rms_in_w': (1.0, 0.6),
     'L0_attn_o_norm_w': (1.0, 0.6),
     'L0_attn_b2': (0.0, 0.432),
     'L0_ffn_b1': (0.0, 0.432),
     'L0_ffn_b2': (0.0, 0.349),
     'L0_ffn_br': (0.0, 0.1),
     'L0_ffn_gamma': (1.0, 0.2),
     'L0_ffn_beta': (0.0, 0.1),
     'L1_attn_bb': (0.0, 0.8),
     'L1_ffn_bn_gamma': (1.0, 0.6),
     'L1_ffn_bn_beta': (0.0, 0.8)}
    factors = {'L0_attn_Wq': 6.225,
     'L0_attn_Wk': 6.188,
     'L0_attn_Wv': 6.143,
     'L0_attn_conv_q_w': 6.217,
     'L0_attn_conv_k_w': 6.007,
     'L0_attn_conv_v_w': 5.944,
     'L0_attn_Wa': 8.0,
     'L0_attn_dt_bias': 8.0,
     'L0_attn_A_log': 8.0,
     'L0_attn_Wb': 8.0,
     'L0_attn_Wg': 6.177,
     'L0_attn_Wo': 6.164,
     'L0_ffn_Wr': 8.0,
     'L1_attn_Wq': 8.0,
     'L1_attn_Wk': 8.0,
     'L1_attn_Wv': 8.0,
     'L1_attn_Wo': 8.0,
     'L1_attn_Wb': 8.0,
     'L1_attn_alpha_log': 64.0,
     'L1_ffn_w_q': 8.0,
     'L1_ffn_keys': 8.0,
     'L1_ffn_down_embed': 8.0,
     'L1_ffn_up_embed': 8.0}
    for name, (base, spread) in spreads.items():
        noise = np.random.default_rng([zlib.crc32(name.encode()), seed]).standard_normal(out[name].shape)
        drawn = base * np.exp(spread * noise) if base else spread * noise
        out[name] = jnp.asarray(drawn.astype(out[name].dtype))
    for name, factor in factors.items():
        out[name] = (out[name] * factor).astype(out[name].dtype)
    return out
```

```python
from contextlib import ExitStack

import numpy as np
import concourse.bass as bass
from concourse import mybir

ALU = mybir.AluOpType
ACT = mybir.ActivationFunctionType
F32 = mybir.dt.float32
BF16 = mybir.dt.bfloat16
U32 = mybir.dt.uint32
AX_X = mybir.AxisListType.X

P = 128
B, T, D = 2, 1024, 128
N = B * T
NT = N // P
TB = T // P
W = 512
NW = N // W
LN_EPS = 1e-5
EPS = 1e-6
H, KD, VD, CONV = 4, 32, 64, 4
C = 64
LEVELS = 6
E, F, TOPK = 8, 512, 2
FB = F // P
NH, HD = 16, 64
INNER = NH * HD
IB = INNER // P
PH, NK = 8, 32
NE = NK * NK
PK = 8


class Link:

    def __init__(self, eng, sem, base=0):
        self.eng, self.sem, self.base, self.n = eng, sem, base, 0

    def __call__(self, ins):
        self.n += 1
        ins.then_inc(self.sem, 1)
        self.eng.wait_ge(self.sem, self.base + self.n)


class Memory:

    def __init__(self, nc, ctx, program=None):
        self.nc, self.ctx = nc, ctx
        self.program, self.used = (program.ctx, program.used) if program else (ctx, [])

    def sb(self, name, shape, dt=F32):
        return self.ctx.enter_context(self.nc.sbuf_tensor(name, shape, dt))

    def ps(self, name, shape, dt=F32):
        return self.ctx.enter_context(self.nc.psum_tensor(name, shape, dt))

    def sem(self, name):
        self.used.append(self.program.enter_context(self.nc.semaphore(name)))
        return self.used[-1]


def bc(ap, axis, n):
    v = ap.unsqueeze(axis)
    return v.broadcast_to([*v.shape[:axis], n, *v.shape[axis + 1:]])


def root(a, var_ready, n, var, std_ready):
    a.wait_ge(var_ready, n)
    a.activation(var, var, ACT.Sqrt).then_inc(std_ready, 1)


def layer_norm(v, link, out, x, tmp, stat, var_ready, std_ready, n, gb=None):
    mean, var = stat[:, 0, :], stat[:, 1, :]
    link(v.tensor_reduce(mean, x, AX_X, ALU.add))
    link(v.tensor_scalar(mean, mean, 1.0 / D, None, ALU.mult))
    link(v.tensor_tensor(out, x, bc(mean, 2, D), ALU.subtract))
    link(v.tensor_tensor(tmp, out, out, ALU.mult))
    link(v.tensor_reduce(var, tmp, AX_X, ALU.add))
    v.tensor_scalar(var, var, 1.0 / D, LN_EPS, ALU.mult, ALU.add).then_inc(var_ready, 1)
    v.wait_ge(std_ready, n)
    link(v.reciprocal(var, var))
    link(v.tensor_tensor(out, out, bc(var, 2, D), ALU.mult))
    if gb is not None:
        g, b = gb
        link(v.tensor_tensor(out, out, bc(g, 1, NT), ALU.mult))
        link(v.tensor_tensor(out, out, bc(b, 1, NT), ALU.add))


def phase_norm(nc, m, io, s):
    ctx = ExitStack()
    with ctx:
        mm = Memory(nc, ctx, m)
        g1 = mm.sb("ln1_g", [P, D])
        b1 = mm.sb("ln1_b", [P, D])
        rw = mm.sb("rms_w", [P, 1])
        hid = mm.sb("hid", [P, NT, D])
        tmp = mm.sb("sq_tmp", [P, NT, D])
        stat = mm.sb("stat", [P, 2, NT])
        x_in = mm.sem("x_in")
        ln_in = mm.sem("ln_in")
        chain = mm.sem("norm_chain")
        var_ready = mm.sem("var_ready")
        std_ready = mm.sem("std_ready")
        xn_ready = mm.sem("xn_ready")
        h_ready = mm.sem("h_ready")
        turned = mm.sem("turned")
        copied = mm.sem("copied")
        with nc.Block() as block:
            @block.sync
            def _(sp):
                sp.dma_start(s.x[:], io["L0_attn_x"].rearrange("b (c p) d -> p (b c) d", p=P)).then_inc(x_in, 16)
                sp.dma_start(s.ident[:], io["c_ident"]).then_inc(ln_in, 16)
                sp.dma_start(g1[:], io["L0_attn_ln1_g"].partition_broadcast(P)).then_inc(ln_in, 16)
                sp.dma_start(b1[:], io["L0_attn_ln1_b"].partition_broadcast(P)).then_inc(ln_in, 16)
                sp.dma_start(rw[:], io["L0_attn_rms_in_w"].rearrange("(d a) -> d a", a=1)).then_inc(ln_in, 16)

            @block.vector
            def _(v):
                link = Link(v, chain)
                v.wait_ge(x_in, 16)
                layer_norm(v, link, s.xn[:], s.x[:], tmp[:], stat, var_ready, std_ready, 1)
                v.engine_nop().then_inc(xn_ready, 1)
                v.wait_ge(ln_in, 64)
                layer_norm(v, link, hid[:], s.xn[:], tmp[:], stat, var_ready, std_ready, 2, (g1[:], b1[:]))
                link(v.tensor_tensor(tmp[:], hid[:], hid[:], ALU.mult))
                link(v.tensor_reduce(stat[:, 0, :], tmp[:], AX_X, ALU.add))
                v.tensor_scalar(stat[:, 1, :], stat[:, 0, :], 1.0 / D, EPS, ALU.mult, ALU.add).then_inc(var_ready, 1)
                v.wait_ge(std_ready, 3)
                link(v.reciprocal(stat[:, 1, :], stat[:, 1, :]))
                v.tensor_tensor(hid[:], hid[:], bc(stat[:, 1, :], 2, D), ALU.mult).then_inc(h_ready, 1)

            @block.tensor
            def _(pe):
                pe.wait_ge(ln_in, 64)
                for k, (src, ready) in enumerate(((s.xn, xn_ready), (hid, h_ready))):
                    pe.wait_ge(ready, 1)
                    for t in range(NT):
                        last = pe.transpose(s.bank[4 * k + t // 4][:, P * (t % 4):P * (t % 4 + 1)], src[:, t, :], s.ident[:])
                        if t % 4 == 3:
                            last.then_inc(turned, 1)

            @block.scalar
            def _(a):
                for n in range(3):
                    root(a, var_ready, n + 1, stat[:, 1, :], std_ready)
                for w in range(NW):
                    a.wait_ge(turned, w + 1)
                    a.activation(s.xnT[:, W * w:W * (w + 1)], s.bank[w][:], ACT.Copy).then_inc(copied, 1)
                for w in range(NW):
                    a.wait_ge(turned, NW + w + 1)
                    a.activation(s.hT[:, W * w:W * (w + 1)], s.bank[4 + w][:], ACT.Copy, scale=rw[:]).then_inc(copied, 1)


def phase_project(nc, m, io, s):
    ctx = ExitStack()
    with ctx:
        mm = Memory(nc, ctx, m)
        w = mm.sb("kqv_w", [P, 4 * P])
        gw = mm.sb("gate_w", [P, H * VD + 2 * H])
        cw = mm.sb("conv_w", [P, 4, CONV])
        group = mm.sb("head_ones", [P, P])
        padded = [mm.sb(f"padded{j}", [P, B, CONV - 1 + T]) for j in range(4)]
        dtb = mm.sb("dt_bias", [P, H])
        alog = mm.sb("a_log", [P, H])
        ab = mm.sb("ab", [P, NT, 2 * H])
        az = mm.sb("az", [P, NT, 2 * H])
        ez = mm.sb("ez", [P, NT, 2 * H])
        lp = mm.sb("log1p", [P, NT, 2 * H])
        eps = mm.sb("eps", [P, 2])
        w_in = mm.sem("w_in")
        small_in = mm.sem("small_in")
        pads = mm.sem("pads")
        chain = mm.sem("conv_chain")
        achain = mm.sem("act_chain")
        projected = mm.sem("projected")
        evacuated = mm.sem("evacuated")
        conved = mm.sem("conved")
        silued = mm.sem("silued")
        gated = mm.sem("gated")
        gate_out = mm.sem("gate_out")
        ab_out = mm.sem("ab_out")
        squared = mm.sem("squared")
        summed = mm.sem("summed")
        z_ready = mm.sem("z_ready")
        e_ready = mm.sem("e_ready")
        with nc.Block() as block:
            @block.sync
            def _(sp):
                sp.dma_start(w[:, 0:P], io["L0_attn_Wk"]).then_inc(w_in, 16)
                sp.dma_start(w[:, P:2 * P], io["L0_attn_Wq"]).then_inc(w_in, 16)
                sp.dma_start(w[:, 2 * P:4 * P], io["L0_attn_Wv"]).then_inc(w_in, 16)
                sp.dma_start(cw[:, 0, :], io["L0_attn_conv_k_w"]).then_inc(w_in, 16)
                sp.dma_start(cw[:, 1, :], io["L0_attn_conv_q_w"]).then_inc(w_in, 16)
                sp.dma_start(cw[:, 2:4, :], io["L0_attn_conv_v_w"].rearrange("(j p) i -> p j i", p=P)).then_inc(w_in, 16)
                sp.dma_start(gw[:, 0:H * VD], io["L0_attn_Wg"]).then_inc(small_in, 16)
                sp.dma_start(gw[:, H * VD:H * VD + H], io["L0_attn_Wa"]).then_inc(small_in, 16)
                sp.dma_start(gw[:, H * VD + H:], io["L0_attn_Wb"]).then_inc(small_in, 16)
                sp.dma_start(dtb[:], io["L0_attn_dt_bias"].partition_broadcast(P)).then_inc(small_in, 16)
                sp.dma_start(alog[:], io["L0_attn_A_log"].partition_broadcast(P)).then_inc(small_in, 16)
                sp.dma_start(group[:], io["c_head_ones"]).then_inc(small_in, 16)

            @block.tensor
            def _(pe):
                pe.wait_ge(w_in, 96)
                for j in range(4):
                    for c in range(NW):
                        if j >= 2:
                            pe.wait_ge(evacuated, NW * (j - 2) + c + 1)
                        pe.matmul(s.bank[4 * (j % 2) + c][:], w[:, P * j:P * (j + 1)], s.hT[:, W * c:W * (c + 1)],
                                  start=True, stop=True).then_inc(projected, 1)
                pe.wait_ge(small_in, 96)
                for t in range(NT):
                    pe.wait_ge(evacuated, NW * 2 + t + 1 if t < 8 else NW * 4)
                    if t >= 8:
                        pe.wait_ge(gate_out, t - 7)
                        pe.wait_ge(ab_out, t - 7)
                    pe.matmul(s.bank[t % 8][:, 0:H * VD + 2 * H], s.hT[:, P * t:P * (t + 1)], gw[:],
                              start=True, stop=True).then_inc(gated, 1)
                for j in range(2):
                    pe.wait_ge(squared, j + 1)
                    for c in range(NW):
                        pe.wait_ge(gate_out, 8 + 4 * j + c + 1)
                        pe.wait_ge(ab_out, 8 + 4 * j + c + 1)
                        pe.matmul(s.bank[4 * j + c][:], group[:], s.rs[j][:, W * c:W * (c + 1)],
                                  start=True, stop=True).then_inc(summed, 1)

            @block.vector
            def _(v):
                link = Link(v, chain)
                for j in range(4):
                    v.memset(padded[j][:, :, 0:CONV - 1], 0.0).then_inc(pads, 1)
                v.memset(eps[:, 0:1], EPS).then_inc(pads, 1)
                v.memset(eps[:, 1:2], KD * EPS).then_inc(pads, 1)
                v.wait_ge(pads, 6)
                v.wait_ge(w_in, 96)
                for j in range(4):
                    v.wait_ge(evacuated, NW * (j + 1))
                    y = s.kqv[j][:].rearrange("p (b t) -> p b t", b=B)
                    link(v.tensor_scalar(y, padded[j][:, :, 0:T], cw[:, j, 0:1], None, ALU.mult))
                    for i in range(1, CONV):
                        link(v.scalar_tensor_tensor(y, padded[j][:, :, i:i + T], cw[:, j, i:i + 1], y, ALU.mult, ALU.add))
                    v.engine_nop().then_inc(conved, 1)
                v.wait_ge(ab_out, NT)
                za, zb = ab[:, :, 0:H], ab[:, :, H:2 * H]
                link(v.tensor_tensor(za, za, bc(dtb[:], 1, NT), ALU.add))
                link(v.tensor_scalar(az[:, :, 0:H], za, -1.0, None, ALU.mult))
                link(v.tensor_tensor(az[:, :, 0:H], az[:, :, 0:H], za, ALU.max))
                v.tensor_scalar(az[:, :, H:2 * H], zb, -87.0, None, ALU.max).then_inc(z_ready, 1)
                e, u, d, is0 = ez[:, :, 0:H], az[:, :, 0:H], az[:, :, H:2 * H], lp[:, :, 0:H]
                v.wait_ge(e_ready, 1)
                v.tensor_scalar(u, e, 1.0, None, ALU.add).then_inc(z_ready, 1)
                v.wait_ge(z_ready, 2)
                link(v.tensor_scalar(d, u, -1.0, None, ALU.add))
                link(v.tensor_scalar(is0, d, 0.0, None, ALU.is_equal))
                link(v.tensor_tensor(d, d, is0, ALU.add))
                link(v.reciprocal(d, d))
                link(v.tensor_tensor(d, d, e, ALU.mult))
                v.wait_ge(e_ready, 2)
                link(v.tensor_tensor(is0, lp[:, :, H:2 * H], is0, ALU.add))
                link(v.tensor_tensor(d, d, is0, ALU.mult))
                link(v.tensor_scalar(za, za, 0.0, None, ALU.max))
                link(v.tensor_tensor(za, za, d, ALU.add))
                link(v.tensor_tensor(za, za, bc(alog[:], 1, NT), ALU.mult))
                v.tensor_scalar(s.g[:], za, -1.0, -104.0, ALU.mult, ALU.max).then_inc(z_ready, 1)
                link(v.tensor_scalar(ez[:, :, H:2 * H], ez[:, :, H:2 * H], 1.0, None, ALU.add))
                link(v.reciprocal(s.beta[:], ez[:, :, H:2 * H]))

            @block.scalar
            def _(a):
                link = Link(a, achain)
                def evacuate(j):
                    for c in range(NW):
                        a.wait_ge(projected, NW * j + c + 1)
                        a.activation(padded[j][:, c // 2, CONV - 1 + W * (c % 2):CONV - 1 + W * (c % 2 + 1)],
                                     s.bank[4 * (j % 2) + c][:], ACT.Copy).then_inc(evacuated, 1)

                def silu(j):
                    a.wait_ge(conved, j + 1)
                    a.activation(s.kqv[j][:], s.kqv[j][:], ACT.Silu).then_inc(silued, 1)

                for j in range(4):
                    evacuate(j)
                for t in range(NT):
                    a.wait_ge(gated, t + 1)
                    a.activation(s.gate[:, t, :], s.bank[t % 8][:, 0:H * VD], ACT.Silu).then_inc(gate_out, 1)
                    a.activation(ab[:, t, :], s.bank[t % 8][:, H * VD:H * VD + 2 * H], ACT.Copy).then_inc(ab_out, 1)
                for j in range(4):
                    silu(j)
                for j in range(2):
                    a.wait_ge(silued, j + 1)
                    a.activation(s.rs[j][:], s.kqv[j][:], ACT.Square).then_inc(squared, 1)
                a.wait_ge(small_in, 96)
                link(a.activation(alog[:], alog[:], ACT.Exp))
                a.wait_ge(z_ready, 1)
                a.activation(ez[:], az[:], ACT.Exp, scale=-1.0).then_inc(e_ready, 1)
                a.wait_ge(z_ready, 2)
                a.activation(lp[:, :, H:2 * H], az[:, :, 0:H], ACT.Ln).then_inc(e_ready, 1)
                for j in range(2):
                    for c in range(NW):
                        a.wait_ge(summed, NW * j + c + 1)
                        link(a.activation(s.rs[j][:, W * c:W * (c + 1)], s.bank[4 * j + c][:], ACT.Ln,
                                          bias=eps[:, j:j + 1], scale=float(KD if j else 1)))
                for j in range(2):
                    a.activation(s.rs[j][:], s.rs[j][:], ACT.Exp, scale=-0.5)


def phase_delta(nc, m, io, s):
    LINKS_V = 2 * (3 + 1 + LEVELS - 2 + P // C)
    ctx = ExitStack()
    with ctx:
        mm = Memory(nc, ctx, m)
        le = mm.sb("le", [P, P])
        gt = mm.sb("gt", [P, P])
        lvl = mm.sb("lvl", [P, LEVELS, P])
        own = mm.sb("own", [P, H])

        def pair(name, shape):
            return [mm.sb(f"{name}{b}", shape) for b in range(B)]

        kt = pair("kt", [P, P])
        qt = pair("qt", [P, P])
        kbd = pair("kbd", [P, H, P])
        qbd = pair("qbd", [P, H, P])
        vt = pair("vt", [P, 2, P])
        gm = pair("gm", [P, H, P])
        gch = pair("gch", [P, H, KD])
        dmb = pair("dmb", [P, H, P])
        expd = pair("expd", [P, P + 2 * H])
        eb = pair("eb", [P, H])
        at = pair("at", [P, H, P])
        pt = pair("pt", [P, H, P])
        qg = pair("qg", [P, P])
        tok = pair("tok", [P, 3 * P])
        kend = pair("kend", [P, P])
        kg = pair("kg", [P, P])
        off = pair("off", [P, H, P])
        xx = pair("xx", [P, H, P])
        tt = pair("tt", [P, H, P])
        rr = pair("rr", [P, H, P])
        wt = pair("wt", [P, P])
        uu = pair("uu", [P, H * VD])
        yy = pair("yy", [P, H * VD])
        st = pair("st", [P, H, VD])
        sown = pair("sown", [P, H, VD])

        def sems(name):
            return [mm.sem(f"{name}{b}") for b in range(B)]

        const_in = mm.sem("const_in")
        chain = mm.sem("delta_chain")
        start = mm.sem("delta_start")
        staged = sems("staged")
        v_staged = sems("v_staged")
        spread = sems("spread")
        masks_g = sems("masks_g")
        decays = sems("decays")
        products = sems("products")
        expd_done = sems("expd_done")
        at_done = sems("at_done")
        turned = sems("turned")
        tok_done = sems("tok_done")
        kscaled = sems("kscaled")
        x_done = sems("x_done")
        t_turned = sems("t_turned")
        t_done = sems("t_done")
        off_done = sems("off_done")
        r_ready = sems("r_ready")
        r_done = sems("r_done")
        dx_ready = sems("dx_ready")
        wu_ready = sems("wu_ready")
        wu_done = sems("wu_done")
        z_ready = sems("z_ready")
        y_done = sems("y_done")
        s_ready = sems("s_ready")
        o_ready = sems("o_ready")
        s_done = sems("s_done")
        o_done = sems("o_done")
        L1 = LEVELS - 1
        NC = P // C
        with nc.Block() as block:
            @block.sync
            def _(sp):
                sp.dma_start(le[:], io["c_le"]).then_inc(const_in, 16)
                sp.dma_start(gt[:], io["c_gt"]).then_inc(const_in, 16)
                sp.dma_start(lvl[:], io["c_levels"]).then_inc(const_in, 16)
                sp.dma_start(own[:], io["c_own"]).then_inc(const_in, 16)

            @block.gpsimd
            def _(g):
                g.wait_ge(const_in, 64)
                with g.Fori(0, TB) as i:
                    for b in range(B):
                        for flat, wide in ((kt, kbd), (qt, qbd)):
                            g.wait_ge(staged[b], 2 * i + (1 if wide is kbd else 2))
                            g.tensor_tensor(wide[b][:], bc(flat[b][:], 1, H), bc(own[:], 2, P), ALU.mult).then_inc(spread[b], 1)

            @block.vector
            def _(v):
                for b in range(B):
                    v.memset(st[b][:], 0.0).then_inc(start, 1)
                v.wait_ge(start, B)
                v.wait_ge(const_in, 64)
                with v.Fori(0, TB) as i:
                    link = Link(v, chain, i * LINKS_V)
                    for b in range(B):
                        v.wait_ge(o_done[b], i)
                        cols = bass.ds(i * P + b * T, P)
                        v.tensor_tensor(kt[b][:], s.kqv[0][:, cols], s.rs[0][:, cols], ALU.mult).then_inc(staged[b], 1)
                        v.tensor_tensor(qt[b][:], s.kqv[1][:, cols], s.rs[1][:, cols], ALU.mult).then_inc(staged[b], 1)
                        gi = s.g[:, bass.ds(i + b * TB, 1), :].rearrange("p a h -> p (a h)")
                        v.tensor_tensor(gm[b][:], bc(gt[:], 1, H), bc(gi, 2, P), ALU.mult).then_inc(masks_g[b], 1)
                        v.tensor_copy(gch[b][:], bc(gi, 2, KD)).then_inc(masks_g[b], 1)
                    for b in range(B):
                        bi = s.beta[:, bass.ds(i + b * TB, 1), :].rearrange("p a h -> p (a h)")
                        v.wait_ge(expd_done[b], 2 * i + 2)
                        link(v.tensor_tensor(dmb[b][:], dmb[b][:], bc(le[:], 1, H), ALU.mult))
                        link(v.tensor_tensor(dmb[b][:], dmb[b][:], bc(bi, 2, P), ALU.mult))
                        link(v.tensor_tensor(eb[b][:], expd[b][:, P + H:], bi, ALU.mult))
                        v.wait_ge(products[b], i + 1)
                        v.tensor_tensor(at[b][:], s.bank[4 * b + 2][:].rearrange("p (h t) -> p h t", h=H), dmb[b][:],
                                        ALU.mult).then_inc(at_done[b], 1)
                        v.tensor_tensor(pt[b][:], s.bank[4 * b + 3][:].rearrange("p (h t) -> p h t", h=H), dmb[b][:],
                                        ALU.mult).then_inc(at_done[b], 1)
                    for b in range(B):
                        v.wait_ge(at_done[b], 2 * i + 2)
                        link(v.tensor_tensor(off[b][:], at[b][:], bc(lvl[:, 0, :], 1, H), ALU.mult))
                        v.tensor_tensor(xx[b][:], bc(s.ident[:], 1, H), off[b][:], ALU.subtract).then_inc(x_done[b], 1)
                    for b in range(B):
                        v.wait_ge(tok_done[b], i + 1)
                        kk = tok[b][:, 0:P].rearrange("p (h c) -> p h c", h=H)
                        v.tensor_tensor(kend[b][:].rearrange("p (h c) -> p h c", h=H), kk, bc(eb[b][:], 2, KD),
                                        ALU.mult).then_inc(kscaled[b], 1)
                        v.tensor_tensor(kg[b][:].rearrange("p (h c) -> p h c", h=H), kk, bc(expd[b][:, P:P + H], 2, KD),
                                        ALU.mult).then_inc(kscaled[b], 1)
                        v.tensor_tensor(qg[b][:], qt[b][:], expd[b][:, 0:P], ALU.mult).then_inc(kscaled[b], 1)
                    for l in range(1, LEVELS):
                        for b in range(B):
                            if l == 1:
                                v.wait_ge(x_done[b], i * LEVELS + 1)
                            else:
                                v.wait_ge(r_ready[b], i * L1 + l - 1)
                            v.tensor_tensor(off[b][:], at[b][:], bc(lvl[:, l, :], 1, H), ALU.mult).then_inc(off_done[b], 1)
                        for b in range(B):
                            v.wait_ge(dx_ready[b], i * L1 + l)
                            x = xx[b][:].rearrange("p h t -> p (h t)")
                            t = tt[b][:].rearrange("p h t -> p (h t)")
                            if l < L1:
                                link(v.tensor_tensor(t, t, s.bank[4 * b][:], ALU.subtract))
                            v.tensor_tensor(x, x, s.bank[4 * b + 3][:], ALU.subtract).then_inc(x_done[b], 1)
                    for c in range(NC):
                        rows = slice(C * c, C * (c + 1))
                        for b in range(B):
                            v.wait_ge(wu_done[b], 2 * i + 2)
                            v.wait_ge(z_ready[b], i * NC + c + 1)
                            v.tensor_tensor(yy[b][rows, :], uu[b][rows, :], s.bank[4 * b + 3][rows, 0:H * VD],
                                            ALU.subtract).then_inc(y_done[b], 1)
                        for b in range(B):
                            last = C * (c + 1) - 1
                            v.wait_ge(s_ready[b], i * NC + c + 1)
                            link(v.tensor_tensor(sown[b][:], s.bank[4 * b + 1][:, 0:H * VD].rearrange("p (h v) -> p h v", h=H),
                                                 bc(own[:], 2, VD), ALU.mult))
                            v.scalar_tensor_tensor(st[b][:], st[b][:], expd[b][:, last:last + 1], sown[b][:],
                                                   ALU.mult, ALU.add).then_inc(s_done[b], 1)
                    assert link.n == LINKS_V, link.n

            @block.scalar
            def _(a):
                with a.Fori(0, TB) as i:
                    for b in range(B):
                        a.wait_ge(turned[b], i)
                        for j in range(2):
                            a.activation(vt[b][:, j, :], s.kqv[2 + j][:, bass.ds(i * P + b * T, P)], ACT.Copy).then_inc(v_staged[b], 1)
                    for b in range(B):
                        a.wait_ge(decays[b], i + 1)
                        a.activation(dmb[b][:].rearrange("p h t -> p (h t)"), s.bank[4 * b][:], ACT.Exp).then_inc(expd_done[b], 1)
                        a.activation(expd[b][:], s.bank[4 * b + 1][:, 0:P + 2 * H], ACT.Exp).then_inc(expd_done[b], 1)
                    for b in range(B):
                        a.wait_ge(turned[b], i + 1)
                        a.activation(tok[b][:], s.bank[4 * b + 1][:, 0:3 * P], ACT.Copy).then_inc(tok_done[b], 1)
                    for b in range(B):
                        a.wait_ge(t_turned[b], i + 1)
                        a.activation(tt[b][:].rearrange("p h t -> p (h t)"), s.bank[4 * b][:], ACT.Copy).then_inc(t_done[b], 1)
                    for l in range(1, LEVELS):
                        for b in range(B):
                            a.wait_ge(r_ready[b], i * L1 + l)
                            a.activation(rr[b][:].rearrange("p h t -> p (h t)"), s.bank[4 * b + 2][:], ACT.Copy).then_inc(r_done[b], 1)
                    for b in range(B):
                        a.wait_ge(wu_ready[b], i + 1)
                        a.activation(wt[b][:], s.bank[4 * b + 1][:, 0:P], ACT.Copy).then_inc(wu_done[b], 1)
                        a.activation(uu[b][:], s.bank[4 * b + 2][:, 0:H * VD], ACT.Copy).then_inc(wu_done[b], 1)
                    for b in range(B):
                        a.wait_ge(o_ready[b], (i + 1) * NC)
                        a.activation(s.o[:, bass.ds(i + b * TB, 1), :].rearrange("p a c -> p (a c)"), s.bank[4 * b][:, 0:H * VD],
                                     ACT.Copy).then_inc(o_done[b], 1)

            @block.tensor
            def _(pe):
                pe.wait_ge(const_in, 64)
                pe.wait_ge(start, B)
                with pe.Fori(0, TB) as i:
                    for b in range(B):
                        p0, p1, p2, p3 = s.bank[4 * b:4 * b + 4]
                        pe.wait_ge(o_done[b], i)
                        pe.wait_ge(s_done[b], i * NC)
                        pe.wait_ge(masks_g[b], 2 * i + 2)
                        gi = s.g[:, bass.ds(i + b * TB, 1), :].rearrange("p a h -> p (a h)")
                        for h in range(H):
                            pe.matmul(p0[:, P * h:P * (h + 1)], gm[b][:, h, :], le[:], start=True, stop=True)
                        pe.matmul(p1[:, 0:P], gch[b][:].rearrange("p h c -> p (h c)"), le[:], start=True, stop=True)
                        pe.matmul(p1[:, P:P + H], le[:], gi, start=True, stop=True)
                        pe.matmul(p1[:, P + H:P + 2 * H], gt[:], gi, start=True, stop=True).then_inc(decays[b], 1)
                        pe.wait_ge(staged[b], 2 * i + 1)
                        pe.wait_ge(spread[b], 2 * i + 1)
                        pe.matmul(p2[:], kt[b][:], kbd[b][:].rearrange("p h t -> p (h t)"), start=True, stop=True)
                        pe.wait_ge(spread[b], 2 * i + 2)
                        pe.matmul(p3[:], kt[b][:], qbd[b][:].rearrange("p h t -> p (h t)"), start=True,
                                  stop=True).then_inc(products[b], 1)
                    for b in range(B):
                        p1 = s.bank[4 * b + 1]
                        pe.wait_ge(expd_done[b], 2 * i + 2)
                        pe.wait_ge(v_staged[b], 2 * i + 2)
                        pe.transpose(p1[:, 0:P], kt[b][:], s.ident[:])
                        pe.transpose(p1[:, P:2 * P], vt[b][:, 0, :], s.ident[:])
                        pe.transpose(p1[:, 2 * P:3 * P], vt[b][:, 1, :], s.ident[:]).then_inc(turned[b], 1)
                    for b in range(B):
                        pe.wait_ge(x_done[b], i * LEVELS + 1)
                        for h in range(H):
                            last = pe.transpose(s.bank[4 * b][:, P * h:P * (h + 1)], xx[b][:, h, :], s.ident[:])
                        last.then_inc(t_turned[b], 1)
                    for l in range(1, LEVELS):
                        for b in range(B):
                            if l == 1:
                                pe.wait_ge(t_done[b], i + 1)
                                pe.wait_ge(at_done[b], 2 * i + 2)
                            pe.wait_ge(x_done[b], i * LEVELS + l)
                            pe.wait_ge(off_done[b], i * L1 + l)
                            for h in range(H):
                                last = pe.matmul(s.bank[4 * b + 2][:, P * h:P * (h + 1)], off[b][:, h, :], tt[b][:, h, :], start=True, stop=True)
                            last.then_inc(r_ready[b], 1)
                        for b in range(B):
                            pe.wait_ge(r_done[b], i * L1 + l)
                            for h in range(H):
                                last = pe.matmul(s.bank[4 * b + 3][:, P * h:P * (h + 1)], rr[b][:, h, :], xx[b][:, h, :], start=True, stop=True)
                            if l < L1:
                                for h in range(H):
                                    last = pe.matmul(s.bank[4 * b][:, P * h:P * (h + 1)], xx[b][:, h, :], rr[b][:, h, :], start=True, stop=True)
                            last.then_inc(dx_ready[b], 1)
                    for b in range(B):
                        pe.wait_ge(x_done[b], (i + 1) * LEVELS)
                        pe.wait_ge(kscaled[b], 3 * i + 3)
                        pe.wait_ge(tok_done[b], i + 1)
                        for h in range(H):
                            pe.matmul(s.bank[4 * b + 1][KD * h:KD * (h + 1), 0:P], kg[b][:, KD * h:KD * (h + 1)], xx[b][:, h, :],
                                      start=True, stop=True)
                        for h in range(H):
                            last = pe.matmul(s.bank[4 * b + 2][:, VD * h:VD * (h + 1)], xx[b][:, h, :],
                                             tok[b][:, P + VD * h:P + VD * (h + 1)], start=True, stop=True)
                        last.then_inc(wu_ready[b], 1)
                    for c in range(NC):
                        cols = slice(C * c, C * (c + 1))
                        for b in range(B):
                            p0, p1, p2, p3 = s.bank[4 * b:4 * b + 4]
                            pe.wait_ge(wu_done[b], 2 * i + 2)
                            pe.wait_ge(s_done[b], i * NC + c)
                            state = st[b][:].rearrange("p h v -> p (h v)")
                            pe.matmul(p3[cols, 0:H * VD], wt[b][:, cols], state, start=True, stop=True).then_inc(z_ready[b], 1)
                            pe.matmul(p0[cols, 0:H * VD], qg[b][:, cols], state, start=True, stop=False, skip_group_check=True)
                        for b in range(B):
                            p0, p1, p2, p3 = s.bank[4 * b:4 * b + 4]
                            pe.wait_ge(y_done[b], i * NC + c + 1)
                            pe.matmul(p1[:, 0:H * VD], kend[b][cols, :], yy[b][cols, :], start=True, stop=True).then_inc(s_ready[b], 1)
                            for h in range(H):
                                last = pe.matmul(p0[cols, VD * h:VD * (h + 1)], pt[b][cols, h, cols], yy[b][cols, VD * h:VD * (h + 1)],
                                                 start=False, stop=h == H - 1, skip_group_check=True)
                            last.then_inc(o_ready[b], 1)


def phase_encode(nc, m, io, s):
    ctx = ExitStack()
    with ctx:
        mm = Memory(nc, ctx, m)
        nw = mm.sb("o_norm_w", [P, VD])
        wo = mm.sb("wo", [P, 2, D])
        w2 = mm.sb("w2", [P, D])
        b2 = mm.sb("b2", [1, D])
        ones = mm.sb("ones", [1, P])
        g2 = mm.sb("ln2_g", [P, D])
        bb2 = mm.sb("ln2_b", [P, D])
        osq = mm.sb("osq", [P, NT * H, VD])
        ost = mm.sb("ost", [P, NT * H])
        oT = mm.sb("oT", [P, 2, N])
        xe = mm.sb("xe", [P, NT, D])
        h2 = mm.sb("h2", [P, NT, D])
        h2T = mm.sb("h2T", [P, N])
        stat = mm.sb("enc_stat", [P, 2, NT])
        w_in = mm.sem("enc_w_in")
        chain = mm.sem("enc_chain")
        squared = mm.sem("o_squared")
        gate_done = mm.sem("gate_done")
        var_ready = mm.sem("enc_var")
        std_ready = mm.sem("enc_std")
        o_ready = mm.sem("o_ready")
        turned = mm.sem("enc_turned")
        copied = mm.sem("enc_copied")
        encoded = mm.sem("encoded")
        xe_done = mm.sem("xe_done")
        h2_ready = mm.sem("h2_ready")
        h2_out = mm.sem("h2_out")
        gelued = mm.sem("gelued")
        ov = s.o[:].rearrange("p t (h v) -> p (t h) v", v=VD)
        with nc.Block() as block:
            @block.sync
            def _(sp):
                sp.dma_start(nw[:], io["L0_attn_o_norm_w"].partition_broadcast(P)).then_inc(w_in, 16)
                sp.dma_start(wo[:], io["L0_attn_Wo"].rearrange("(j p) d -> p j d", p=P)).then_inc(w_in, 16)
                sp.dma_start(w2[:], io["L0_attn_W2"]).then_inc(w_in, 16)
                sp.dma_start(b2[:], io["L0_attn_b2"].rearrange("(a d) -> a d", a=1)).then_inc(w_in, 16)
                sp.dma_start(g2[:], io["L0_attn_ln2_g"].partition_broadcast(P)).then_inc(w_in, 16)
                sp.dma_start(bb2[:], io["L0_attn_ln2_b"].partition_broadcast(P)).then_inc(w_in, 16)

            @block.gpsimd
            def _(g):
                g.memset(ones[:], 1.0).then_inc(gate_done, 1)
                g.wait_ge(w_in, 96)
                gv = s.gate[:].rearrange("p t (h v) -> p (t h) v", v=VD)
                g.tensor_tensor(gv, gv, bc(nw[:], 1, NT * H), ALU.mult).then_inc(gate_done, 1)

            @block.vector
            def _(v):
                link = Link(v, chain)
                v.wait_ge(squared, 1)
                link(v.tensor_reduce(ost[:], osq[:], AX_X, ALU.add))
                v.tensor_scalar(ost[:], ost[:], 1.0 / VD, EPS, ALU.mult, ALU.add).then_inc(var_ready, 1)
                v.wait_ge(std_ready, 1)
                link(v.reciprocal(ost[:], ost[:]))
                link(v.tensor_tensor(ov, ov, bc(ost[:], 2, VD), ALU.mult))
                v.wait_ge(gate_done, 2)
                v.tensor_tensor(s.o[:], s.o[:], s.gate[:], ALU.mult).then_inc(o_ready, 1)
                for w in range(NW):
                    v.wait_ge(encoded, w + 1)
                    v.tensor_tensor(xe[:, 4 * w:4 * w + 4, :], s.xn[:, 4 * w:4 * w + 4, :],
                                    s.bank[w][:].rearrange("p (t d) -> p t d", d=D), ALU.add).then_inc(xe_done, 1)
                v.wait_ge(xe_done, NW)
                v.wait_ge(w_in, 96)
                layer_norm(v, link, h2[:], xe[:], s.s0[:], stat, var_ready, std_ready, 2, (g2[:], bb2[:]))
                v.engine_nop().then_inc(h2_ready, 1)
                for w in range(NW):
                    v.wait_ge(gelued, w + 1)
                    v.tensor_tensor(s.s0[:, 4 * w:4 * w + 4, :], s.s0[:, 4 * w:4 * w + 4, :], xe[:, 4 * w:4 * w + 4, :], ALU.add)

            @block.tensor
            def _(pe):
                pe.wait_ge(w_in, 96)
                pe.wait_ge(gate_done, 1)
                pe.wait_ge(o_ready, 1)
                for j in range(2):
                    for t in range(NT):
                        last = pe.transpose(s.bank[4 * j + t // 4][:, P * (t % 4):P * (t % 4 + 1)],
                                            s.o[:, t, P * j:P * (j + 1)], s.ident[:])
                        if t % 4 == 3:
                            last.then_inc(turned, 1)
                pe.wait_ge(copied, 2 * NW)
                for t in range(NT):
                    for j in range(2):
                        last = pe.matmul(s.bank[t // 4][:, P * (t % 4):P * (t % 4 + 1)], oT[:, j, P * t:P * (t + 1)], wo[:, j, :],
                                         start=j == 0, stop=j == 1)
                    if t % 4 == 3:
                        last.then_inc(encoded, 1)
                pe.wait_ge(h2_ready, 1)
                for t in range(NT):
                    last = pe.transpose(s.bank[4 + t // 4][:, P * (t % 4):P * (t % 4 + 1)], h2[:, t, :], s.ident[:])
                    if t % 4 == 3:
                        last.then_inc(turned, 1)
                for t in range(NT):
                    pe.wait_ge(copied, 2 * NW + t // 4 + 1)
                    out = s.bank[t // 4][:, P * (t % 4):P * (t % 4 + 1)]
                    pe.matmul(out, h2T[:, P * t:P * (t + 1)], w2[:], start=True, stop=False)
                    last = pe.matmul(out, ones[:], b2[:], start=False, stop=True)
                    if t % 4 == 3:
                        last.then_inc(h2_out, 1)

            @block.scalar
            def _(a):
                a.activation(osq[:], ov, ACT.Square).then_inc(squared, 1)
                root(a, var_ready, 1, ost[:], std_ready)
                for n in range(2 * NW):
                    a.wait_ge(turned, n + 1)
                    a.activation(oT[:, n // NW, W * (n % NW):W * (n % NW + 1)], s.bank[n][:], ACT.Copy).then_inc(copied, 1)
                root(a, var_ready, 2, stat[:, 1, :], std_ready)
                for n in range(NW):
                    a.wait_ge(turned, 2 * NW + n + 1)
                    a.activation(h2T[:, W * n:W * (n + 1)], s.bank[4 + n][:], ACT.Copy).then_inc(copied, 1)
                for n in range(NW):
                    a.wait_ge(h2_out, n + 1)
                    a.activation(s.s0[:, 4 * n:4 * n + 4, :].rearrange("p t d -> p (t d)"), s.bank[n][:],
                                 ACT.Gelu).then_inc(gelued, 1)


def phase_experts(nc, m, io, s):
    NJ = B * TOPK
    ctx = ExitStack()
    with ctx:
        mm = Memory(nc, ctx, m)
        wr = mm.sb("wr", [P, E])
        br = mm.sb("br", [1, E])
        ones = mm.sb("ones_row", [1, P])
        mean = mm.sb("mean_x", [P, B])
        lg = mm.sb("logits", [1, B, E])
        st = mm.sb("router_stat", [1, B, 2])
        top = mm.sb("top", [1, B, 8])
        idx = mm.sb("expert", [1, B, 8], U32)
        cw = mm.sb("mix", [1, B, TOPK])
        cwb = mm.sb("mix_b", [P, NJ])
        w1 = [mm.sb(f"w1_{j}", [P, F]) for j in range(NJ)]
        w2 = [mm.sb(f"w2_{j}", [P, FB, D]) for j in range(NJ)]
        b1 = [mm.sb(f"b1_{j}", [P, FB]) for j in range(NJ)]
        b2 = [mm.sb(f"b2_{j}", [1, D]) for j in range(NJ)]
        hh = [mm.sb(f"hidden{n}", [P, TOPK * FB, W]) for n in range(2)]
        y = mm.sb("y_moe", [P, NT, D])
        tmp = mm.sb("moe_tmp", [P, NT, D])
        stat = mm.sb("moe_stat", [P, 2, NT])
        gam = mm.sb("gamma", [P, D])
        bet = mm.sb("beta_ln", [P, D])
        in_ = mm.sem("router_in")
        chain = mm.sem("moe_chain")
        mean_done = mm.sem("mean_done")
        logit_ready = mm.sem("logit_ready")
        sub_done = mm.sem("sub_done")
        exp_done = mm.sem("exp_done")
        picked = mm.sem("picked")
        mixed = mm.sem("mixed")
        mix_out = mm.sem("mix_out")
        mix_done = mm.sem("mix_done")
        w_in = [mm.sem(f"expert_in{j}") for j in range(NJ)]
        scaled = mm.sem("scaled")
        up = mm.sem("up")
        act = mm.sem("act")
        down = mm.sem("down")
        summed = mm.sem("y_summed")
        var_ready = mm.sem("moe_var")
        std_ready = mm.sem("moe_std")
        normed = mm.sem("y_normed")
        NU = TOPK * FB
        with nc.Block() as block:
            @block.sync
            def _(sp):
                sp.dma_start(wr[:], io["L0_ffn_Wr"]).then_inc(in_, 16)
                sp.dma_start(br[:], io["L0_ffn_br"].rearrange("(a e) -> a e", a=1)).then_inc(in_, 16)
                sp.dma_start(gam[:], io["L0_ffn_gamma"].partition_broadcast(P)).then_inc(in_, 16)
                sp.dma_start(bet[:], io["L0_ffn_beta"].partition_broadcast(P)).then_inc(in_, 16)
                sp.wait_ge(picked, B)
                for j in range(NJ):
                    e = sp.value_load(idx[0:1, j // TOPK, j % TOPK:j % TOPK + 1], min_val=0, max_val=E - 1)
                    pick = bass.ds(e, 1)
                    sp.dma_start(w1[j][:], io["L0_ffn_W1"][pick].rearrange("a p f -> p (a f)")).then_inc(w_in[j], 16)
                    sp.dma_start(b1[j][:], io["b1_by_feature"][pick].rearrange("a p f -> p (a f)")).then_inc(w_in[j], 16)
                    sp.dma_start(w2[j][:], io["L0_ffn_W2"][pick].rearrange("a (f p) d -> p (a f) d", p=P)).then_inc(w_in[j], 16)
                    sp.dma_start(b2[j][:], io["L0_ffn_b2"][pick]).then_inc(w_in[j], 16)

            @block.vector
            def _(v):
                link = Link(v, chain)
                link(v.memset(ones[:], 1.0))
                link(v.tensor_reduce(mean[:], s.xnT[:].rearrange("p (b t) -> p b t", b=B), AX_X, ALU.add))
                v.tensor_scalar(mean[:], mean[:], 1.0 / T, None, ALU.mult).then_inc(mean_done, 1)
                v.wait_ge(in_, 64)
                v.wait_ge(logit_ready, 1)
                link(v.tensor_tensor(lg[:], s.bank[0][0:1, 0:B * E].rearrange("p (b e) -> p b e", b=B), bc(br[:], 1, B), ALU.add))
                link(v.tensor_reduce(st[:, :, 0], lg[:], AX_X, ALU.max))
                v.tensor_tensor(lg[:], lg[:], bc(st[:, :, 0], 2, E), ALU.subtract).then_inc(sub_done, 1)
                v.wait_ge(exp_done, 1)
                link(v.tensor_reduce(st[:, :, 1], lg[:], AX_X, ALU.add))
                link(v.reciprocal(st[:, :, 1], st[:, :, 1]))
                link(v.tensor_tensor(lg[:], lg[:], bc(st[:, :, 1], 2, E), ALU.mult))
                for b in range(B):
                    link(v.max(top[:, b, :], lg[:, b, :]))
                    v.max_index(idx[:, b, :], top[:, b, :], lg[:, b, :]).then_inc(picked, 1)
                v.tensor_tensor(cw[:], top[:, :, 0:TOPK], bc(top[:, :, 0], 2, TOPK), ALU.subtract).then_inc(sub_done, 1)
                v.wait_ge(exp_done, 2)
                link(v.tensor_reduce(st[:, :, 1], cw[:], AX_X, ALU.add))
                link(v.reciprocal(st[:, :, 1], st[:, :, 1]))
                v.tensor_tensor(cw[:], cw[:], bc(st[:, :, 1], 2, TOPK), ALU.mult).then_inc(mixed, 1)
                v.wait_ge(mixed, 1)
                v.wait_ge(mix_done, 1)
                for j in range(NJ):
                    v.wait_ge(w_in[j], 64)
                    v.tensor_scalar(w2[j][:], w2[j][:], cwb[:, j:j + 1], None, ALU.mult).then_inc(scaled, 1)
                    v.tensor_scalar(b2[j][:], b2[j][:], cw[0:1, j // TOPK, j % TOPK:j % TOPK + 1], None, ALU.mult).then_inc(scaled, 1)
                for t in range(NT):
                    v.wait_ge(down, t + 1)
                    v.tensor_tensor(y[:, t, :], s.bank[4 + t % 4][:, 0:D], s.xn[:, t, :], ALU.add).then_inc(summed, 1)
                v.wait_ge(summed, NT)
                layer_norm(v, link, tmp[:], y[:], s.g0[:], stat, var_ready, std_ready, 1, (gam[:], bet[:]))
                v.engine_nop().then_inc(normed, 1)

            @block.scalar
            def _(a):
                a.wait_ge(sub_done, 1)
                a.activation(lg[:], lg[:], ACT.Exp).then_inc(exp_done, 1)
                a.wait_ge(sub_done, 2)
                a.activation(cw[:], cw[:], ACT.Exp).then_inc(exp_done, 1)
                a.wait_ge(mix_out, 1)
                a.activation(cwb[:], s.bank[1][:, 0:NJ], ACT.Copy).then_inc(mix_done, 1)
                for w in range(NW):
                    if w >= 2:
                        a.wait_ge(down, 4 * (w - 1))
                    for n in range(NU):
                        j = TOPK * (w // 2) + n // FB
                        a.wait_ge(up, NU * w + n + 1)
                        if w % 2 == 0:
                            a.wait_ge(w_in[j], 64)
                        a.activation(hh[w % 2][:, n, :], s.bank[n % 4][:], ACT.Gelu, bias=b1[j][:, n % FB:n % FB + 1]).then_inc(act, 1)
                root(a, var_ready, 1, stat[:, 1, :], std_ready)
                a.wait_ge(normed, 1)
                a.activation(s.g0[:], tmp[:], ACT.Silu)

            @block.tensor
            def _(pe):
                pe.wait_ge(mean_done, 1)
                pe.wait_ge(in_, 64)
                for b in range(B):
                    last = pe.matmul(s.bank[0][0:1, E * b:E * (b + 1)], mean[:, b:b + 1], wr[:], start=True, stop=True)
                last.then_inc(logit_ready, 1)
                pe.wait_ge(mixed, 1)
                pe.matmul(s.bank[1][:, 0:NJ], ones[:], cw[:].rearrange("p b k -> p (b k)"), start=True, stop=True).then_inc(mix_out, 1)
                pe.wait_ge(mix_done, 1)

                def ups(w):
                    for n in range(NU):
                        j = TOPK * (w // 2) + n // FB
                        if w % 2 == 0:
                            pe.wait_ge(w_in[j], 64)
                        if NU * w + n >= 4:
                            pe.wait_ge(act, NU * w + n - 3)
                        f = n % FB
                        pe.matmul(s.bank[n % 4][:], w1[j][:, P * f:P * (f + 1)], s.xnT[:, W * w:W * (w + 1)],
                                  start=True, stop=True).then_inc(up, 1)

                def downs(w):
                    pe.wait_ge(scaled, 2 * NJ)
                    pe.wait_ge(act, NU * (w + 1))
                    for q in range(4):
                        t = 4 * w + q
                        if t >= 4:
                            pe.wait_ge(summed, t - 3)
                        out = s.bank[4 + q][:, 0:D]
                        for n in range(NU):
                            j = TOPK * (w // 2) + n // FB
                            pe.matmul(out, hh[w % 2][:, n, P * q:P * (q + 1)], w2[j][:, n % FB, :], start=n == 0, stop=False)
                        for k in range(TOPK):
                            last = pe.matmul(out, ones[:], b2[TOPK * (w // 2) + k][:], start=False, stop=k == TOPK - 1)
                        last.then_inc(down, 1)

                ups(0)
                for w in range(NW):
                    if w + 1 < NW:
                        ups(w + 1)
                    downs(w)


def phase_join(nc, m, io, s):
    ctx = ExitStack()
    with ctx:
        mm = Memory(nc, ctx, m)
        tmp = mm.sb("join_tmp", [P, NT, D])
        stat = mm.sb("join_stat", [P, 2, NT])
        chain = mm.sem("join_chain")
        var_ready = mm.sem("join_var")
        std_ready = mm.sem("join_std")
        ready = mm.sem("join_ready")
        turned = mm.sem("join_turned")
        with nc.Block() as block:
            @block.vector
            def _(v):
                link = Link(v, chain)
                link(v.tensor_tensor(s.s0[:], s.s0[:], s.g0[:], ALU.mult))
                link(v.tensor_tensor(s.x[:], s.x[:], s.s0[:], ALU.add))
                layer_norm(v, link, s.xn[:], s.x[:], tmp[:], stat, var_ready, std_ready, 1)
                v.engine_nop().then_inc(ready, 1)

            @block.scalar
            def _(a):
                root(a, var_ready, 1, stat[:, 1, :], std_ready)
                for n in range(NW):
                    a.wait_ge(turned, n + 1)
                    a.activation(s.xnT[:, W * n:W * (n + 1)], s.bank[n][:], ACT.Copy)

            @block.tensor
            def _(pe):
                pe.wait_ge(ready, 1)
                for t in range(NT):
                    last = pe.transpose(s.bank[t // 4][:, P * (t % 4):P * (t % 4 + 1)], s.xn[:, t, :], s.ident[:])
                    if t % 4 == 3:
                        last.then_inc(turned, 1)


def phase_ternary(nc, m, io, s):
    ctx = ExitStack()
    with ctx:
        mm = Memory(nc, ctx, m)
        raw = mm.sb("raw", [P, IB, N])
        raw_v = raw[:].rearrange("p j n -> p (j n)").rearrange("p (t c) -> p t c", c=INNER)
        wk = mm.sb("wk", [P, INNER])
        wks = mm.sb("wk_swapped", [P, INNER])
        wv = mm.sb("wv", [P, INNER])
        wb = mm.sb("wb", [P, NH])
        bb = mm.sb("bb", [P, NH])
        turn = [mm.sb(f"rope_part{n}", [P, W]) for n in range(4)]
        junk = mm.sb("abs_out", [P, W])
        acc = mm.sb("abs_sum", [P, 2, 2 * NT])
        tot = mm.sb("abs_total", [P, 2])
        low = mm.sb("not_above", [P, 2 * N], BF16)
        thr = mm.sb("thr", [P, 4])
        ones = mm.sb("ones_sq", [P, P])
        w_in = mm.sem("qk_w_in")
        chain = mm.sem("tern_chain")
        achain = mm.sem("tern_act_chain")
        k_ready = mm.sem("k_ready")
        parts = mm.sem("rope_parts")
        k_done = mm.sem("k_done")
        k_abs = mm.sem("k_abs")
        total_in = mm.sem("total_in")
        total = mm.sem("total")
        thr_done = mm.sem("thr_done")
        k_tern = mm.sem("k_tern")
        v_ready = mm.sem("v_ready")
        v_done = mm.sem("v_done")
        b_ready = mm.sem("b_ready")
        z_ready = mm.sem("bz_ready")
        floored = mm.sem("floored")
        e_ready = mm.sem("be_ready")
        NU = NW * IB
        with nc.Block() as block:
            @block.sync
            def _(sp):
                sp.dma_start(wk[:], io["L1_attn_WkT"]).then_inc(w_in, 16)
                sp.dma_start(wks[:], io["L1_attn_WkT_swapped"]).then_inc(w_in, 16)
                sp.dma_start(s.cos[:], io["c_cos"]).then_inc(w_in, 16)
                sp.dma_start(s.sin[:], io["c_sin"]).then_inc(w_in, 16)
                sp.dma_start(wv[:], io["L1_attn_WvT"]).then_inc(w_in, 16)
                sp.dma_start(wb[:], io["L1_attn_WbT"]).then_inc(w_in, 16)
                sp.dma_start(bb[:], io["L1_attn_bb"].partition_broadcast(P)).then_inc(w_in, 16)
                sp.dma_start(s.la[:], io["L1_attn_alpha_log"].rearrange("h a -> (h a)").partition_broadcast(P)).then_inc(w_in, 16)
                for k in range(2):
                    sp.dma_start(s.lac[HD * k:HD * (k + 1), :],
                                 io["alpha_log_by_parity"][k].partition_broadcast(HD)).then_inc(w_in, 16)

            @block.tensor
            def _(pe):
                pe.wait_ge(w_in, 160)
                for w in range(NW):
                    for j in range(IB):
                        n = IB * w + j
                        if n >= 4:
                            pe.wait_ge(parts, 2 * (n - 3))
                        for k, weight in enumerate((wk, wks)):
                            pe.matmul(s.bank[2 * (n % 4) + k][:], weight[:, P * j:P * (j + 1)], s.xnT[:, W * w:W * (w + 1)],
                                      start=True, stop=True).then_inc(k_ready, 1)
                pe.wait_ge(parts, 2 * NU)
                for t in range(NT):
                    last = pe.matmul(s.bank[7][:, NH * t:NH * (t + 1)], s.xnT[:, P * t:P * (t + 1)], wb[:], start=True, stop=True)
                last.then_inc(b_ready, 1)
                pe.wait_ge(total_in, 1)
                pe.matmul(s.bank[6][:, 0:1], ones[:], tot[:, 0:1], start=True, stop=True).then_inc(total, 1)
                for t in range(NT):
                    for k in range(2):
                        n = 2 * t + k
                        if n >= 6:
                            pe.wait_ge(v_done, n - 5)
                        pe.matmul(s.bank[n % 6][:], s.xnT[:, P * t:P * (t + 1)], wv[:, W * k:W * (k + 1)],
                                  start=True, stop=True).then_inc(v_ready, 1)
                pe.wait_ge(total_in, 2)
                pe.matmul(s.bank[6][:, 1:2], ones[:], tot[:, 1:2], start=True, stop=True).then_inc(total, 1)

            @block.gpsimd
            def _(g):
                for n in range(NU):
                    w, j = n // IB, n % IB
                    g.wait_ge(parts, 2 * n + 2)
                    g.tensor_tensor(raw[:, j, W * w:W * (w + 1)], turn[2 * (n % 2)][:], turn[2 * (n % 2) + 1][:],
                                    ALU.add).then_inc(k_done, 1)

            @block.vector
            def _(v):
                link = Link(v, chain)
                link(v.memset(ones[:], 1.0))
                v.wait_ge(w_in, 160)
                for n in range(NU):
                    w = n // IB
                    if n >= 2:
                        v.wait_ge(k_done, n - 1)
                    cols = slice(W * (w % 2), W * (w % 2 + 1))
                    for k, table in enumerate((s.cos, s.sin)):
                        v.wait_ge(k_ready, 2 * n + k + 1)
                        v.tensor_tensor(turn[2 * (n % 2) + k][:], s.bank[2 * (n % 4) + k][:], table[:, cols], ALU.mult).then_inc(parts, 1)

                def threshold(k):
                    link(v.tensor_reduce(tot[:, k:k + 1], acc[:, k, :], AX_X, ALU.add))
                    v.engine_nop().then_inc(total_in, 1)
                    v.wait_ge(total, k + 1)
                    up, dn = thr[:, 2 * k:2 * k + 1], thr[:, 2 * k + 1:2 * k + 2]
                    link(v.tensor_scalar(up, s.bank[6][:, k:k + 1], 1.0 / (N * INNER), None, ALU.mult))
                    link(v.tensor_scalar(up, up, 0.01, 10.0, ALU.max, ALU.min))
                    link(v.tensor_scalar(dn, up, -1.0, None, ALU.mult))
                    return up, dn

                def ternary(k, out, src):
                    up, dn = threshold(k)
                    for n in range(IB // 2):
                        part = src[:, 2 * N * n:2 * N * (n + 1)]
                        link(v.tensor_scalar(low[:], part, up, -1.0, ALU.is_gt, ALU.add))
                        ins = v.scalar_tensor_tensor(out[:, 2 * N * n:2 * N * (n + 1)], part, dn, low[:], ALU.is_ge, ALU.add)
                        link(ins)
                    v.engine_nop().then_inc(k_tern, 1)

                flat = raw[:].rearrange("p j n -> p (j n)")
                v.wait_ge(k_abs, NU)
                ternary(0, s.kt[:].rearrange("p j n -> p (j n)"), flat)
                v.wait_ge(b_ready, 1)
                v.tensor_tensor(s.bk[:], s.bank[7][:, 0:NT * NH].rearrange("p (t h) -> p t h", h=NH), bc(bb[:], 1, NT),
                                ALU.add).then_inc(z_ready, 1)
                v.wait_ge(z_ready, 1)
                for x in (s.bk, s.la, s.lac):
                    v.tensor_scalar(x[:], x[:], -87.0, None, ALU.max).then_inc(floored, 1)
                v.wait_ge(e_ready, 3)
                for x in (s.bk, s.la, s.lac):
                    link(v.tensor_scalar(x[:], x[:], 1.0, None, ALU.add))
                    link(v.reciprocal(x[:], x[:]))
                link(v.tensor_scalar(s.la[:], s.la[:], 1e-6, None, ALU.max))
                link(v.tensor_scalar(s.lac[:], s.lac[:], 1e-6, None, ALU.max))
                v.engine_nop().then_inc(z_ready, 1)
                v.wait_ge(k_abs, NU + 2 * NT)
                ternary(1, s.vt[:].rearrange("p t c -> p (t c)"), flat)

            @block.scalar
            def _(a):
                link = Link(a, achain)
                for n in range(NU):
                    w, j = n // IB, n % IB
                    a.wait_ge(k_done, n + 1)
                    link(a.activation(junk[:], raw[:, j, W * w:W * (w + 1)], ACT.Abs, accum_out=acc[:, 0, n:n + 1]))
                    a.sem_inc(k_abs, 1)
                a.wait_ge(z_ready, 1)
                a.wait_ge(floored, 3)
                for x in (s.bk, s.la, s.lac):
                    a.activation(x[:], x[:], ACT.Exp, scale=-1.0).then_inc(e_ready, 1)
                a.wait_ge(k_tern, 1)
                for n in range(2 * NT):
                    t, k = n // 2, n % 2
                    a.wait_ge(v_ready, n + 1)
                    a.activation(raw_v[:, t, W * k:W * (k + 1)], s.bank[n % 6][:], ACT.Copy).then_inc(v_done, 1)
                    a.wait_ge(v_done, n + 1)
                    link(a.activation(junk[:], raw_v[:, t, W * k:W * (k + 1)], ACT.Abs, accum_out=acc[:, 1, n:n + 1]))
                    a.sem_inc(k_abs, 1)
                a.wait_ge(z_ready, 2)
                a.activation(s.la[:], s.la[:], ACT.Ln)
                a.activation(s.lac[:], s.lac[:], ACT.Ln)


def phase_attend(nc, m, io, s):
    ctx = ExitStack()
    with ctx:
        mm = Memory(nc, ctx, m)
        wq = mm.sb("wq", [P, INNER])
        wqs = mm.sb("wq_swapped", [P, INNER])
        wo = mm.sb("wo1", [P, IB, D])
        gap = mm.sb("gap", [P, P])
        le = mm.sb("le_full", [P, P])
        pos = mm.sb("pos1", [P, P])
        rev = mm.sb("rev", [P, 1])
        dd = mm.sb("dd", [P, NH, P])
        dt_ = mm.sb("decay_t", [P, IB, P])
        de = mm.sb("decay_e", [P, NH])
        part = [mm.sb(f"q_part{n}", [P, IB, P]) for n in range(2)]
        qr = mm.sb("qr", [P, IB, P])
        qd = mm.sb("qd", [P, IB, P])
        kf = mm.sb("kf", [P, IB, P])
        kend = mm.sb("k_end", [P, INNER])
        vb = mm.sb("vb", [P, INNER])
        wT = mm.sb("wT", [P, NH, P])
        ot = mm.sb("o_tok", [P, INNER])
        oT = mm.sb("o_feat", [P, IB, P])
        st = [mm.sb(f"att_state{b}", [P, IB, HD]) for b in range(B)]
        sd = mm.sb("state_decayed", [P, IB, HD])
        c_in = mm.sem("att_in")
        init = mm.sem("att_init")
        tables = mm.sem("att_tables")
        q_ready = mm.sem("q_ready")
        q_parts = mm.sem("q_parts")
        q_done = mm.sem("q_done")
        kf_done = mm.sem("kf_done")
        vb_done = mm.sem("vb_done")
        k_turned = mm.sem("k_turned")
        kend_done = mm.sem("kend_done")
        scored = mm.sem("scored")
        w_done = mm.sem("w_done")
        o_ready = mm.sem("att_o_ready")
        ot_done = mm.sem("ot_done")
        o_turned = mm.sem("o_turned")
        oT_done = mm.sem("oT_done")
        s_ready = mm.sem("att_s_ready")
        s_done = mm.sem("att_s_done")
        f_ready = mm.sem("f_ready")
        f_done = mm.sem("f_done")
        with nc.Block() as block:
            @block.sync
            def _(sp):
                sp.dma_start(gap[:], io["c_gap"]).then_inc(c_in, 16)
                sp.dma_start(le[:], io["c_le_full"]).then_inc(c_in, 16)
                sp.dma_start(pos[:], io["c_pos1"]).then_inc(c_in, 16)
                sp.dma_start(rev[:], io["c_rev"]).then_inc(c_in, 16)
                sp.dma_start(wq[:], io["L1_attn_WqT"]).then_inc(c_in, 16)
                sp.dma_start(wqs[:], io["L1_attn_WqT_swapped"]).then_inc(c_in, 16)
                sp.dma_start(wo[:], io["L1_attn_WoT"].rearrange("(j p) d -> p j d", p=P)).then_inc(c_in, 16)

            @block.scalar
            def _(a):
                a.wait_ge(c_in, 112)
                for h in range(NH):
                    a.activation(dd[:, h, :], gap[:], ACT.Exp, scale=s.la[:, h:h + 1]).then_inc(tables, 1)
                for j in range(IB):
                    a.activation(dt_[:, j, :], pos[:], ACT.Exp, scale=s.lac[:, j:j + 1]).then_inc(tables, 1)
                a.activation(de[:], s.la[:], ACT.Exp, scale=rev[:]).then_inc(tables, 1)
                with a.Fori(0, TB) as i:
                    for b in range(B):
                        n = i * B + b
                        a.wait_ge(scored, n * 2)
                        a.activation(kf[:], s.kt[:, :, bass.ds(i * P + b * T, P)], ACT.Copy).then_inc(kf_done, 1)
                        a.wait_ge(o_ready, n * 2 + 2)
                        for k in range(2):
                            a.activation(ot[:].rearrange("p (j k c) -> p j k c", k=2, c=HD)[:, :, k, :],
                                         s.bank[4 + k][:].rearrange("p (j c) -> p j c", c=HD), ACT.Copy).then_inc(ot_done, 1)
                        a.wait_ge(o_turned, n + 1)
                        for k in range(2):
                            a.activation(oT[:, 4 * k:4 * k + 4, :].rearrange("p j t -> p (j t)"), s.bank[4 + k][:], ACT.Copy).then_inc(oT_done, 1)
                        a.wait_ge(f_ready, n + 1)
                        a.activation(s.s1[:, bass.ds(i + b * TB, 1), :].rearrange("p a d -> p (a d)"), s.bank[7][:, 0:D],
                                     ACT.Copy).then_inc(f_done, 1)

            @block.gpsimd
            def _(g):
                g.wait_ge(tables, NH + IB + 1)
                with g.Fori(0, TB) as i:
                    for b in range(B):
                        n = i * B + b
                        g.wait_ge(s_ready, n)
                        bi = s.bk[:, bass.ds(i + b * TB, 1), :].rearrange("p a h -> p (a h)")
                        g.tensor_tensor(vb[:].rearrange("p (h c) -> p h c", h=NH),
                                        s.vt[:, bass.ds(i + b * TB, 1), :].rearrange("p a (h c) -> p (a h) c", c=HD),
                                        bc(bi, 2, HD), ALU.mult).then_inc(vb_done, 1)
                        g.wait_ge(q_parts, n * 4 + 4)
                        g.tensor_tensor(qr[:], part[0][:], part[1][:], ALU.add).then_inc(q_done, 1)
                        g.wait_ge(q_done, n * 2 + 1)
                        g.tensor_tensor(qd[:], qr[:], dt_[:], ALU.mult).then_inc(q_done, 1)

            @block.vector
            def _(v):
                for b in range(B):
                    v.memset(st[b][:], 0.0).then_inc(init, 1)
                v.wait_ge(tables, NH + IB + 1)
                v.tensor_tensor(dd[:], dd[:], bc(le[:], 1, NH), ALU.mult).then_inc(init, 1)
                v.wait_ge(init, B + 1)
                with v.Fori(0, TB) as i:
                    for b in range(B):
                        n = i * B + b
                        v.wait_ge(q_ready, n + 1)
                        v.wait_ge(q_done, n * 2)
                        for k, table in enumerate((s.cos, s.sin)):
                            for c in range(2):
                                v.tensor_tensor(part[k][:, 4 * c:4 * c + 4, :], s.bank[2 * k + c][:].rearrange("p (j t) -> p j t", t=P),
                                                bc(table[:, bass.ds(i * P, P)], 1, 4), ALU.mult).then_inc(q_parts, 1)
                        v.wait_ge(k_turned, n + 1)
                        v.wait_ge(s_ready, n)
                        for c in range(2):
                            v.tensor_tensor(kend[:, W * c:W * (c + 1)].rearrange("p (h c) -> p h c", c=HD),
                                            s.bank[4 + c][:].rearrange("p (h c) -> p h c", c=HD),
                                            bc(de[:, NH // 2 * c:NH // 2 * (c + 1)], 2, HD), ALU.mult).then_inc(kend_done, 1)
                        v.wait_ge(o_ready, n * 2)
                        v.wait_ge(s_done, n * 2)
                        v.tensor_tensor(sd[:], st[b][:], bc(dt_[:, :, P - 1], 2, HD), ALU.mult).then_inc(s_done, 1)
                        for k in range(2):
                            v.wait_ge(scored, n * 2 + k + 1)
                            for c in range(2):
                                hv = wT[:].rearrange("p (j k) t -> p j k t", k=2)[:, 4 * c:4 * c + 4, k, :]
                                dv = dd[:].rearrange("p (j k) t -> p j k t", k=2)[:, 4 * c:4 * c + 4, k, :]
                                v.tensor_tensor(hv, s.bank[2 * k + c][:].rearrange("p (j t) -> p j t", t=P), dv, ALU.mult).then_inc(w_done, 1)
                        v.wait_ge(s_ready, n + 1)
                        v.wait_ge(s_done, n * 2 + 1)
                        v.tensor_tensor(st[b][:], sd[:], s.bank[6][:].rearrange("p (j c) -> p j c", c=HD), ALU.add).then_inc(s_done, 1)

            @block.tensor
            def _(pe):
                pe.wait_ge(c_in, 112)
                pe.wait_ge(init, B + 1)
                with pe.Fori(0, TB) as i:
                    for b in range(B):
                        n = i * B + b
                        pe.wait_ge(w_done, n * 4)
                        for k, weight in enumerate((wq, wqs)):
                            for j in range(IB):
                                last = pe.matmul(s.bank[2 * k + j // 4][:, P * (j % 4):P * (j % 4 + 1)], weight[:, P * j:P * (j + 1)],
                                                 s.xnT[:, bass.ds(i * P + b * T, P)], start=True, stop=True)
                        last.then_inc(q_ready, 1)
                        pe.wait_ge(kf_done, n + 1)
                        pe.wait_ge(oT_done, n * 2)
                        for j in range(IB):
                            last = pe.transpose(s.bank[4 + j // 4][:, P * (j % 4):P * (j % 4 + 1)], kf[:, j, :], s.ident[:])
                        last.then_inc(k_turned, 1)
                        pe.wait_ge(q_parts, n * 4 + 4)
                        pe.wait_ge(q_done, n * 2 + 2)
                        for k in range(2):
                            rows = slice(HD * k, HD * (k + 1))
                            for j in range(IB):
                                last = pe.matmul(s.bank[2 * k + j // 4][:, P * (j % 4):P * (j % 4 + 1)], kf[rows, j, :], qr[rows, j, :],
                                                 start=True, stop=True)
                            last.then_inc(scored, 1)
                        pe.wait_ge(vb_done, n + 1)
                        pe.wait_ge(kend_done, n * 2 + 2)
                        pe.wait_ge(s_done, n * 2)
                        for k in range(2):
                            rows = slice(HD * k, HD * (k + 1))
                            pe.wait_ge(w_done, n * 4 + 2 * k + 2)
                            for j in range(IB):
                                h = 2 * j + k
                                o = s.bank[4 + k][:, HD * j:HD * (j + 1)]
                                pe.matmul(o, wT[:, h, :], vb[:, HD * h:HD * (h + 1)], start=True, stop=False)
                                last = pe.matmul(o, qd[rows, j, :], st[b][rows, j, :], start=False, stop=True)
                            last.then_inc(o_ready, 1)
                        for k in range(2):
                            for j in range(IB):
                                h = 2 * j + k
                                last = pe.matmul(s.bank[6][HD * k:HD * (k + 1), HD * j:HD * (j + 1)], kend[:, HD * h:HD * (h + 1)],
                                                 vb[:, HD * h:HD * (h + 1)], start=True, stop=True)
                        last.then_inc(s_ready, 1)
                        pe.wait_ge(ot_done, n * 2 + 2)
                        for j in range(IB):
                            last = pe.transpose(s.bank[4 + j // 4][:, P * (j % 4):P * (j % 4 + 1)], ot[:, P * j:P * (j + 1)], s.ident[:])
                        last.then_inc(o_turned, 1)
                        pe.wait_ge(oT_done, n * 2 + 2)
                        pe.wait_ge(f_done, n)
                        for j in range(IB):
                            last = pe.matmul(s.bank[7][:, 0:D], oT[:, j, :], wo[:, j, :], start=j == 0, stop=j == IB - 1)
                        last.then_inc(f_ready, 1)


def phase_keys(nc, m, io, s):
    Q = 2 * PH
    EB = NE // P
    ctx = ExitStack()
    with ctx:
        mm = Memory(nc, ctx, m)
        w = mm.sb("wq_bn", [P, Q, P])
        wt = mm.sb("wq_bn_t", [P, Q, P])
        keys = mm.sb("keys", [P, Q, NK])
        bn = mm.sb("bn", [P, 2, Q])
        down = mm.sb("down_t", [P, NE])
        ones = mm.sb("ones_k", [P, P])
        mrow = mm.sb("mean_row", [P, D])
        mcol = mm.sb("mean_col", [P, 1])
        xc = mm.sb("x_centred", [P, NT, D])
        cov = mm.sb("cov", [P, D])
        wc = mm.sb("w_cov_w", [P, Q, P])
        mv = mm.sb("mean_var", [P, 2, Q])
        k_in = mm.sem("keys_in")
        chain = mm.sem("keys_chain")
        ones_done = mm.sem("ones_done")
        row_ready = mm.sem("row_ready")
        centred = mm.sem("centred")
        cov_ready = mm.sem("cov_ready")
        cov_done = mm.sem("cov_done")
        wc_ready = mm.sem("wc_ready")
        wc_done = mm.sem("wc_done")
        mv_ready = mm.sem("mv_ready")
        var_ready = mm.sem("bn_var")
        std_ready = mm.sem("bn_std")
        scaled = mm.sem("keys_scaled")
        m_ready = mm.sem("m_ready")
        h_ready = mm.sem("down_ready")
        h_done = mm.sem("down_done")
        with nc.Block() as block:
            @block.sync
            def _(sp):
                sp.dma_start(w[:].rearrange("p q d -> p (q d)"), io["L1_ffn_w_q"]).then_inc(k_in, 16)
                sp.dma_start(wt[:], io["w_q_by_key_feature"].rearrange("(q d) m -> d q m", d=P)).then_inc(k_in, 16)
                sp.dma_start(keys[:], io["keys_by_feature"]).then_inc(k_in, 16)
                sp.dma_start(bn[:], io["bn_by_feature"]).then_inc(k_in, 16)
                sp.dma_start(down[:], io["down_by_feature"]).then_inc(k_in, 16)
                sp.dma_start(s.up[:], io["L1_ffn_up_embed"].rearrange("(j p) d -> p j d", p=P)).then_inc(k_in, 16)

            @block.tensor
            def _(pe):
                pe.wait_ge(ones_done, 1)
                for t in range(NT):
                    last = pe.matmul(s.bank[0][:, 0:D], ones[:], s.xn[:, t, :], start=t == 0, stop=t == NT - 1)
                last.then_inc(row_ready, 1)
                pe.wait_ge(centred, 1)
                for t in range(NT):
                    last = pe.matmul(s.bank[1][:, 0:D], xc[:, t, :], xc[:, t, :], start=t == 0, stop=t == NT - 1)
                last.then_inc(cov_ready, 1)
                pe.wait_ge(cov_done, 1)
                pe.wait_ge(k_in, 96)
                for q in range(4):
                    pe.matmul(s.bank[4 + q][:], cov[:], w[:, 4 * q:4 * q + 4, :].rearrange("p q d -> p (q d)"), start=True,
                              stop=True).then_inc(wc_ready, 1)
                for q in range(Q):
                    pe.matmul(s.bank[2][:, q:q + 1], w[:, q, :], mcol[:], start=True, stop=True)
                pe.wait_ge(wc_done, 4)
                for q in range(Q):
                    last = pe.matmul(s.bank[2][:, Q + q:Q + q + 1], wc[:, q, :], ones[:, 0:1], start=True, stop=True)
                last.then_inc(mv_ready, 1)
                for j in range(EB):
                    for c in range(NW):
                        n = NW * j + c
                        if n >= 4:
                            pe.wait_ge(h_done, n - 3)
                        pe.matmul(s.bank[4 + n % 4][:], down[:, P * j:P * (j + 1)], s.xnT[:, W * c:W * (c + 1)], start=True,
                                  stop=True).then_inc(h_ready, 1)
                pe.wait_ge(scaled, 2)
                for q in range(Q):
                    pe.matmul(s.bank[0][:, NK * q:NK * (q + 1)], wt[:, q, :], wc[:, q, 0:NK], start=True, stop=True)
                for q in range(Q):
                    last = pe.matmul(s.bank[1][0:1, NK * q:NK * (q + 1)], mv[:, 0, q:q + 1], keys[:, q, :], start=True, stop=True)
                last.then_inc(m_ready, 1)

            @block.vector
            def _(v):
                link = Link(v, chain)
                link(v.memset(s.ones[:], 1.0))
                v.memset(ones[:], 1.0).then_inc(ones_done, 1)
                link(v.tensor_reduce(mcol[:], s.xnT[:], AX_X, ALU.add))
                link(v.tensor_scalar(mcol[:], mcol[:], 1.0 / N, None, ALU.mult))
                v.wait_ge(row_ready, 1)
                link(v.tensor_scalar(mrow[:], s.bank[0][:, 0:D], 1.0 / N, None, ALU.mult))
                v.tensor_tensor(xc[:], s.xn[:], bc(mrow[:], 1, NT), ALU.subtract).then_inc(centred, 1)
                v.wait_ge(cov_ready, 1)
                v.tensor_scalar(cov[:], s.bank[1][:, 0:D], 1.0 / N, None, ALU.mult).then_inc(cov_done, 1)
                v.wait_ge(k_in, 96)
                for q in range(4):
                    v.wait_ge(wc_ready, q + 1)
                    v.tensor_tensor(wc[:, 4 * q:4 * q + 4, :], w[:, 4 * q:4 * q + 4, :],
                                    s.bank[4 + q][:].rearrange("p (q d) -> p q d", d=P), ALU.mult).then_inc(wc_done, 1)
                v.wait_ge(mv_ready, 1)
                link(v.tensor_copy(mv[:], s.bank[2][:, 0:2 * Q].rearrange("p (k q) -> p k q", k=2)))
                mean, var = mv[:, 0, :], mv[:, 1, :]
                v.tensor_scalar(var, var, LN_EPS, None, ALU.add).then_inc(var_ready, 1)
                v.wait_ge(std_ready, 1)
                link(v.reciprocal(var, var))
                link(v.tensor_tensor(var, var, bn[:, 0, :], ALU.mult))
                v.tensor_tensor(wc[:, :, 0:NK], keys[:], bc(var, 2, NK), ALU.mult).then_inc(scaled, 1)
                link(v.tensor_tensor(mean, mean, var, ALU.mult))
                v.tensor_tensor(mean, bn[:, 1, :], mean, ALU.subtract).then_inc(scaled, 1)
                v.wait_ge(m_ready, 1)
                v.tensor_copy(s.keymat[:], s.bank[0][:])
                v.tensor_copy(s.keyrow[:], s.bank[1][0:1, :])

            @block.scalar
            def _(a):
                root(a, var_ready, 1, mv[:, 1, :], std_ready)
                for n in range(EB * NW):
                    a.wait_ge(h_ready, n + 1)
                    a.activation(s.act[:, n // NW, W * (n % NW):W * (n % NW + 1)], s.bank[4 + n % 4][:],
                                 ACT.Gelu_apprx_tanh).then_inc(h_done, 1)


def phase_product_keys(nc, m, io, s, out):
    Q = 2 * PH
    EB = NE // P
    POOL_HEADS = 5
    ctx = ExitStack()
    with ctx:
        mm = Memory(nc, ctx, m)
        xt = [mm.sb(f"x_tile{u}", [P, P]) for u in range(2)]
        sim = [mm.sb(f"sim{u}", [P, Q, NK]) for u in range(2)]
        top = [mm.sb(f"top8_{u}", [P, Q, PK]) for u in range(2)]
        comb = [mm.sb(f"comb{u}", [P, PH, PK * PK]) for u in range(2)]
        best = [mm.sb(f"best{u}", [P, PH, PK]) for u in range(2)]
        rel = [mm.sb(f"rel{u}", [P, PH, PK]) for u in range(2)]
        lz = [mm.sb(f"ln_z{u}", [P, PH]) for u in range(2)]
        nb = [mm.sb(f"neg_bias{u}", [P, PH]) for u in range(2)]
        sums = [mm.sb(f"sums{r}", [P, NK, NK]) for r in range(2)]
        soft = [mm.sb(f"soft{r}", [P, NE]) for r in range(2)]
        sel = [mm.sb(f"selected{r}", [P, NE]) for r in range(2)]
        wgt = [mm.sb(f"weighted{u}", [P, EB, P]) for u in range(2)]
        res = [mm.sb(f"result{u}", [P, D]) for u in range(2)]
        idle = mm.sb("idle", [P, 1])
        xt_done = mm.sem("xt_done")
        sim_ready = mm.sem("sim_ready")
        sim_done = mm.sem("sim_done")
        top_done = mm.sem("top_done")
        comb_done = mm.sem("comb_done")
        best_done = mm.sem("best_done")
        rel_done = mm.sem("rel_done")
        rexp_done = mm.sem("rexp_done")
        z_done = mm.sem("z_done")
        lz_done = mm.sem("lz_done")
        nb_done = mm.sem("nb_done")
        sums_p = mm.sem("sums_by_pool")
        sums_v = mm.sem("sums_by_vector")
        soft_done = mm.sem("soft_done")
        sel_done = mm.sem("sel_done")
        head_in = mm.sem("head_in")
        wgt_done = mm.sem("wgt_done")
        out_ready = mm.sem("pk_out_ready")
        silu_done = mm.sem("pk_silu_done")
        res_done = mm.sem("res_done")
        stored = [mm.sem(f"stored{u}") for u in range(2)]
        out_v = out.rearrange("b (c p) d -> (b c) p d", p=P)
        VH = PH - POOL_HEADS

        def over_tiles(eng, body):
            body(eng, None, 0, 0)
            with eng.Fori(0, NT // 2 - 1) as i:
                for u in range(2):
                    body(eng, i * 2 + u, i * 2 + u + 1, u)
            body(eng, NT - 2, NT - 1, 0)
            body(eng, NT - 1, None, 1)

        def which(eng, n, nxt, u, scores, weigh):
            if nxt is not None:
                scores(nxt, 0 if n is None else 1 - u)
            if n is not None:
                weigh(n, u)

        def at(n, size):
            return bass.ds(n * size, size)

        with nc.Block() as block:
            @block.sync
            def _(sp):
                with sp.Fori(0, NT // 2) as i:
                    for u in range(2):
                        n = i * 2 + u
                        sp.wait_ge(res_done, 2 * n + 2)
                        sp.dma_start(out_v[bass.ds(n, 1)].rearrange("a p d -> p (a d)"), res[u][:]).then_inc(stored[u], 16)
                for u in range(2):
                    sp.wait_ge(stored[u], 16 * NT // 2)

            @block.gpsimd
            def _(g):
                def weigh(n, u):
                    for h in range(POOL_HEADS):
                        r = h % 2
                        g.wait_ge(sel_done, n * PH + (h - 1 if h >= 2 else 0))
                        g.tensor_tensor(sums[r][:], bc(sim[u][:, h, :], 2, NK), bc(sim[u][:, PH + h, :], 1, NK), ALU.add).then_inc(sums_p, 1)
                    g.wait_ge(silu_done, n + 1)
                    g.tensor_tensor(res[u][:], res[u][:], s.s1[:, at(n, 1), :].rearrange("p a d -> p (a d)"), ALU.mult).then_inc(res_done, 1)
                    g.wait_ge(res_done, 2 * n + 1)
                    g.tensor_tensor(res[u][:], res[u][:], s.x[:, at(n, 1), :].rearrange("p a d -> p (a d)"), ALU.add).then_inc(res_done, 1)

                def scores(n, u):
                    g.wait_ge(sim_done, n + 1)

                over_tiles(g, lambda eng, n, nxt, u: which(eng, n, nxt, u, scores, weigh))

            @block.tensor
            def _(pe):
                def scores(n, u):
                    pe.wait_ge(xt_done, n + 1)
                    pe.matmul(s.bank[u][:], xt[u][:], s.keymat[:], start=True, stop=False)
                    pe.matmul(s.bank[u][:], s.ones[:], s.keyrow[:], start=False, stop=True).then_inc(sim_ready, 1)

                def weigh(n, u):
                    ct = s.bank[2 + 2 * u:4 + 2 * u]
                    for h in range(PH):
                        pe.wait_ge(sel_done, n * PH + h + 1)
                        for j in range(EB):
                            last = pe.matmul(ct[j // 4][:, P * (j % 4):P * (j % 4 + 1)], sel[h % 2][:, P * j:P * (j + 1)], s.ident[:],
                                             start=h == 0 and j % 4 == 0, stop=h == PH - 1, skip_group_check=True)
                        last.then_inc(head_in, 1)
                    pe.wait_ge(wgt_done, n * 2 + 2)
                    for j in range(EB):
                        last = pe.matmul(s.bank[6 + u][:, 0:D], wgt[u][:, j, :], s.up[:, j, :], start=j == 0, stop=j == EB - 1)
                    last.then_inc(out_ready, 1)

                over_tiles(pe, lambda eng, n, nxt, u: which(eng, n, nxt, u, scores, weigh))

            @block.scalar
            def _(a):
                def scores(n, u):
                    a.activation(xt[u][:], s.xnT[:, at(n, P)], ACT.Copy).then_inc(xt_done, 1)
                    a.wait_ge(sim_ready, n + 1)
                    a.activation(sim[u][:].rearrange("p q k -> p (q k)"), s.bank[u][:], ACT.Copy).then_inc(sim_done, 1)
                    a.wait_ge(rel_done, n + 1)
                    a.activation(rel[u][:], rel[u][:], ACT.Exp).then_inc(rexp_done, 1)
                    a.wait_ge(z_done, n + 1)
                    a.activation(lz[u][:], lz[u][:], ACT.Ln).then_inc(lz_done, 1)

                def weigh(n, u):
                    a.wait_ge(nb_done, n + 1)
                    for h in range(PH):
                        r = h % 2
                        if h < POOL_HEADS:
                            a.wait_ge(sums_p, n * POOL_HEADS + h + 1)
                        else:
                            a.wait_ge(sums_v, n * VH + h - POOL_HEADS + 1)
                        a.wait_ge(sel_done, n * PH + (h - 1 if h >= 2 else 0))
                        a.activation(soft[r][:], sums[r][:].rearrange("p i j -> p (i j)"), ACT.Exp, bias=nb[u][:, h:h + 1]).then_inc(soft_done, 1)
                    a.wait_ge(out_ready, n + 1)
                    a.wait_ge(stored[u], 8 * (n - u))
                    a.activation(res[u][:], s.bank[6 + u][:, 0:D], ACT.Silu).then_inc(silu_done, 1)

                over_tiles(a, lambda eng, n, nxt, u: which(eng, n, nxt, u, scores, weigh))

            @block.vector
            def _(v):
                def scores(n, u):
                    v.wait_ge(sim_done, n + 1)
                    v.memset(idle[:], 0.0)
                    for q in range(Q):
                        ins = v.max(top[u][:, q, :], sim[u][:, q, :])
                    ins.then_inc(top_done, 1)
                    v.wait_ge(top_done, n + 1)
                    row, col = top[u][:, 0:PH, :], top[u][:, PH:Q, :]
                    v.tensor_tensor(comb[u][:].rearrange("p h (a b) -> p h a b", a=PK), bc(row, 3, PK), bc(col, 2, PK), ALU.add).then_inc(comb_done, 1)
                    v.wait_ge(comb_done, n + 1)
                    v.memset(idle[:], 0.0)
                    for h in range(PH):
                        ins = v.max(best[u][:, h, :], comb[u][:, h, :])
                    ins.then_inc(best_done, 1)
                    v.wait_ge(best_done, n + 1)
                    v.tensor_tensor(rel[u][:], best[u][:], bc(best[u][:, :, 0], 2, PK), ALU.subtract).then_inc(rel_done, 1)
                    v.wait_ge(rexp_done, n + 1)
                    v.tensor_reduce(lz[u][:], rel[u][:], AX_X, ALU.add).then_inc(z_done, 1)
                    v.wait_ge(lz_done, n + 1)
                    v.scalar_tensor_tensor(nb[u][:], best[u][:, :, 0], -1.0, lz[u][:], ALU.mult, ALU.subtract).then_inc(nb_done, 1)

                def weigh(n, u):
                    for h in range(PH):
                        r = h % 2
                        if h >= POOL_HEADS:
                            v.wait_ge(sel_done, n * PH + h - 1)
                            v.tensor_tensor(sums[r][:], bc(sim[u][:, h, :], 2, NK), bc(sim[u][:, PH + h, :], 1, NK), ALU.add).then_inc(sums_v, 1)
                        v.wait_ge(soft_done, n * PH + h + 1)
                        if h >= 2:
                            v.wait_ge(head_in, n * PH + h - 1)
                        else:
                            v.wait_ge(head_in, n * PH)
                        v.scalar_tensor_tensor(sel[r][:], sums[r][:].rearrange("p i j -> p (i j)"), best[u][:, h, PK - 1:PK], soft[r][:],
                                               ALU.is_ge, ALU.mult).then_inc(sel_done, 1)
                    v.wait_ge(head_in, n * PH + PH)
                    for k in range(2):
                        v.tensor_tensor(wgt[u][:, 4 * k:4 * k + 4, :], s.bank[2 + 2 * u + k][:].rearrange("p (j t) -> p j t", t=P),
                                        s.act[:, 4 * k:4 * k + 4, at(n, P)], ALU.mult).then_inc(wgt_done, 1)

                over_tiles(v, lambda eng, n, nxt, u: which(eng, n, nxt, u, scores, weigh))


class Shared:
    pass


def clear(nc, semaphores):
    with nc.Block() as block:
        @block.sync
        def _(sp):
            for semaphore in semaphores:
                sp.sem_clear(semaphore)


def build(nc, io, out):
    ctx = ExitStack()
    with ctx:
        m = Memory(nc, ctx)
        s = Shared()
        s.x = m.sb("x", [P, NT, D])
        s.xn = m.sb("xn", [P, NT, D])
        s.xnT = m.sb("xnT", [P, N])
        s.ident = m.sb("ident", [P, P])
        s.bank = [m.ps(f"bank{i}", [P, W]) for i in range(8)]
        with ExitStack() as block0:
            m0 = Memory(nc, block0)
            sems = Memory(nc, block0)
            s.s0 = m0.sb("s0", [P, NT, D])
            s.g0 = m0.sb("g0", [P, NT, D])
            with ExitStack() as attn:
                m1 = Memory(nc, attn)
                s.gate = m1.sb("gate", [P, NT, H * VD])
                s.o = m1.sb("o", [P, NT, H * VD])
                with ExitStack() as scan:
                    m2 = Memory(nc, scan)
                    s.hT = m2.sb("hT", [P, N])
                    s.kqv = [m2.sb(f"kqv{j}", [P, N]) for j in range(4)]
                    s.rs = [m2.sb(f"rs{j}", [P, N]) for j in range(2)]
                    s.g = m2.sb("g", [P, NT, H])
                    s.beta = m2.sb("beta", [P, NT, H])
                    phase_norm(nc, sems, io, s)
                    phase_project(nc, sems, io, s)
                    phase_delta(nc, sems, io, s)
                phase_encode(nc, sems, io, s)
            phase_experts(nc, sems, io, s)
            phase_join(nc, sems, io, s)
            clear(nc, sems.used)
        with ExitStack() as block1:
            m1 = Memory(nc, block1)
            s.s1 = m1.sb("s1", [P, NT, D])
            with ExitStack() as attn:
                m2 = Memory(nc, attn)
                s.cos = m2.sb("cos", [P, T])
                s.sin = m2.sb("sin", [P, T])
                s.kt = m2.sb("k_tern_bf", [P, IB, N], BF16)
                s.vt = m2.sb("v_tern_bf", [P, NT, INNER], BF16)
                s.bk = m2.sb("beta_k", [P, NT, NH])
                s.la = m2.sb("log_alpha", [P, NH])
                s.lac = m2.sb("log_alpha_c", [P, IB])
                phase_ternary(nc, m, io, s)
                phase_attend(nc, m, io, s)
            m3 = Memory(nc, block1)
            s.act = m3.sb("act_t", [P, NE // P, N])
            s.up = m3.sb("up", [P, NE // P, D])
            s.keymat = m3.sb("keymat", [P, 2 * PH * NK])
            s.keyrow = m3.sb("keyrow", [1, 2 * PH * NK])
            s.ones = m3.sb("ones_r", [1, P])
            phase_keys(nc, m, io, s)
            phase_product_keys(nc, m, io, s, out)


def constants():
    f = np.float32
    i = np.arange(P)
    row, col = i[:, None], i[None, :]
    same = row // C == col // C
    levels = [(row // (2 << n) == col // (2 << n)) & ((row >> n) % 2 == 0) & ((col >> n) % 2 == 1) for n in range(LEVELS)]
    inv = (f(1) / f(10000.0) ** (np.arange(0, HD, 2, dtype=f) / f(HD))).astype(f)
    angle = (np.arange(T, dtype=f)[:, None] * inv[None, :]).astype(f)
    cos, sin = np.cos(angle).T.astype(f), np.sin(angle).T.astype(f)
    return {
        "c_ident": np.eye(P, dtype=f),
        "c_head_ones": (row // KD == col // KD).astype(f),
        "c_own": (row // KD == np.arange(H)[None, :]).astype(f),
        "c_le": ((row <= col) & same).astype(f),
        "c_gt": ((row > col) & same).astype(f),
        "c_levels": np.stack(levels, 1).astype(f),
        "c_cos": np.tile(cos, (4, 1)),
        "c_sin": np.concatenate([-sin, sin, -sin, sin]),
        "c_gap": np.maximum(col - row, 0).astype(f),
        "c_le_full": (row <= col).astype(f),
        "c_pos1": np.tile((i + 1).astype(f), (P, 1)),
        "c_rev": (P - 1 - i).astype(f)[:, None],
    }


_AS_THEY_ARE = ["L0_attn_x", "L0_attn_ln1_g", "L0_attn_ln1_b", "L0_attn_ln2_g", "L0_attn_ln2_b", "L0_attn_rms_in_w", "L0_attn_Wq",
                "L0_attn_Wk", "L0_attn_Wv", "L0_attn_conv_q_w", "L0_attn_conv_k_w", "L0_attn_conv_v_w", "L0_attn_Wa",
                "L0_attn_dt_bias", "L0_attn_A_log", "L0_attn_Wb", "L0_attn_Wg", "L0_attn_o_norm_w", "L0_attn_Wo", "L0_attn_W2",
                "L0_attn_b2", "L0_ffn_W1", "L0_ffn_W2", "L0_ffn_b2", "L0_ffn_Wr", "L0_ffn_br", "L0_ffn_gamma", "L0_ffn_beta",
                "L1_attn_bb", "L1_attn_alpha_log", "L1_ffn_w_q", "L1_ffn_up_embed"]


def laid_out(x):
    def halves_swapped(w):
        return w.T.reshape(D, NH, 2, HD // 2)[:, :, ::-1].reshape(D, INNER)

    return {
        "b1_by_feature": x["L0_ffn_b1"].reshape(E, FB, P).transpose(0, 2, 1),
        "L1_attn_WqT": x["L1_attn_Wq"].T,
        "L1_attn_WkT": x["L1_attn_Wk"].T,
        "L1_attn_WvT": x["L1_attn_Wv"].T,
        "L1_attn_WbT": x["L1_attn_Wb"].T,
        "L1_attn_WoT": x["L1_attn_Wo"].T,
        "L1_attn_WqT_swapped": halves_swapped(x["L1_attn_Wq"]),
        "L1_attn_WkT_swapped": halves_swapped(x["L1_attn_Wk"]),
        "alpha_log_by_parity": x["L1_attn_alpha_log"].reshape(IB, 2).T,
        "w_q_by_key_feature": x["L1_ffn_w_q"].T,
        "keys_by_feature": x["L1_ffn_keys"].transpose(3, 2, 0, 1).reshape(P, 2 * PH, NK),
        "bn_by_feature": np.stack([x["L1_ffn_bn_gamma"].reshape(2 * PH, P).T, x["L1_ffn_bn_beta"].reshape(2 * PH, P).T], 1),
        "down_by_feature": x["L1_ffn_down_embed"].T,
    }


def kernel(**inputs):
    import concourse.bacc as _bacc
    from concourse.bass_utils import run_bass_kernel_spmd as _run

    nc = _bacc.Bacc("TRN2", target_bir_lowering=False, num_devices=1)
    given = {k: np.asarray(v) for k, v in inputs.items()}
    arrays = {k: given[k] for k in _AS_THEY_ARE} | laid_out(given) | constants()
    io = {}
    for name in arrays:
        arrays[name] = np.ascontiguousarray(arrays[name])
        io[name] = nc.dram_tensor(name, arrays[name].shape, mybir.dt.from_np(arrays[name].dtype), kind="ExternalInput").ap()
    out = nc.dram_tensor("out", (B, T, D), F32, kind="ExternalOutput").ap()
    build(nc, io, out)
    r = _run(nc, [arrays], core_ids=[0])
    return r.results[0]["out"]
```

```python
from contextlib import ExitStack

import numpy as np
import concourse.bass as bass
from concourse import mybir

ALU = mybir.AluOpType
ACT = mybir.ActivationFunctionType
F32 = mybir.dt.float32
BF16 = mybir.dt.bfloat16
U32 = mybir.dt.uint32
AX_X = mybir.AxisListType.X

P = 128
B, T, D = 2, 1024, 128
N = B * T
NT = N // P
TB = T // P
W = 512
NW = N // W
LN_EPS = 1e-5
EPS = 1e-6
H, KD, VD, CONV = 4, 32, 64, 4
C = 64
LEVELS = 6
E, F, TOPK = 8, 512, 2
FB = F // P
NH, HD = 16, 64
INNER = NH * HD
IB = INNER // P
PH, NK = 8, 32
NE = NK * NK
PK = 8


class Link:

    def __init__(self, eng, sem, base=0):
        self.eng, self.sem, self.base, self.n = eng, sem, base, 0

    def __call__(self, ins):
        self.n += 1
        ins.then_inc(self.sem, 1)
        self.eng.wait_ge(self.sem, self.base + self.n)


class Memory:

    def __init__(self, nc, ctx, program=None):
        self.nc, self.ctx = nc, ctx
        self.program, self.used = (program.ctx, program.used) if program else (ctx, [])

    def sb(self, name, shape, dt=F32):
        return self.ctx.enter_context(self.nc.sbuf_tensor(name, shape, dt))

    def ps(self, name, shape, dt=F32):
        return self.ctx.enter_context(self.nc.psum_tensor(name, shape, dt))

    def sem(self, name):
        self.used.append(self.program.enter_context(self.nc.semaphore(name)))
        return self.used[-1]


def bc(ap, axis, n):
    v = ap.unsqueeze(axis)
    return v.broadcast_to([*v.shape[:axis], n, *v.shape[axis + 1:]])


def root(a, var_ready, n, var, std_ready):
    a.wait_ge(var_ready, n)
    a.activation(var, var, ACT.Sqrt).then_inc(std_ready, 1)


def layer_norm(v, link, out, x, tmp, stat, var_ready, std_ready, n, gb=None):
    mean, var = stat[:, 0, :], stat[:, 1, :]
    link(v.tensor_reduce(mean, x, AX_X, ALU.add))
    link(v.tensor_scalar(mean, mean, 1.0 / D, None, ALU.mult))
    link(v.tensor_tensor(out, x, bc(mean, 2, D), ALU.subtract))
    link(v.tensor_tensor(tmp, out, out, ALU.mult))
    link(v.tensor_reduce(var, tmp, AX_X, ALU.add))
    v.tensor_scalar(var, var, 1.0 / D, LN_EPS, ALU.mult, ALU.add).then_inc(var_ready, 1)
    v.wait_ge(std_ready, n)
    link(v.reciprocal(var, var))
    link(v.tensor_tensor(out, out, bc(var, 2, D), ALU.mult))
    if gb is not None:
        g, b = gb
        link(v.tensor_tensor(out, out, bc(g, 1, NT), ALU.mult))
        link(v.tensor_tensor(out, out, bc(b, 1, NT), ALU.add))


def phase_norm(nc, m, io, s):
    ctx = ExitStack()
    with ctx:
        mm = Memory(nc, ctx, m)
        g1 = mm.sb("ln1_g", [P, D])
        b1 = mm.sb("ln1_b", [P, D])
        rw = mm.sb("rms_w", [P, 1])
        hid = mm.sb("hid", [P, NT, D])
        tmp = mm.sb("sq_tmp", [P, NT, D])
        stat = mm.sb("stat", [P, 2, NT])
        x_in = mm.sem("x_in")
        ln_in = mm.sem("ln_in")
        chain = mm.sem("norm_chain")
        var_ready = mm.sem("var_ready")
        std_ready = mm.sem("std_ready")
        xn_ready = mm.sem("xn_ready")
        h_ready = mm.sem("h_ready")
        turned = mm.sem("turned")
        copied = mm.sem("copied")
        with nc.Block() as block:
            @block.sync
            def _(sp):
                sp.dma_start(s.x[:], io["L0_attn_x"].rearrange("b (c p) d -> p (b c) d", p=P)).then_inc(x_in, 16)
                sp.dma_start(s.ident[:], io["c_ident"]).then_inc(ln_in, 16)
                sp.dma_start(g1[:], io["L0_attn_ln1_g"].partition_broadcast(P)).then_inc(ln_in, 16)
                sp.dma_start(b1[:], io["L0_attn_ln1_b"].partition_broadcast(P)).then_inc(ln_in, 16)
                sp.dma_start(rw[:], io["L0_attn_rms_in_w"].rearrange("(d a) -> d a", a=1)).then_inc(ln_in, 16)

            @block.vector
            def _(v):
                link = Link(v, chain)
                v.wait_ge(x_in, 16)
                layer_norm(v, link, s.xn[:], s.x[:], tmp[:], stat, var_ready, std_ready, 1)
                v.engine_nop().then_inc(xn_ready, 1)
                v.wait_ge(ln_in, 64)
                layer_norm(v, link, hid[:], s.xn[:], tmp[:], stat, var_ready, std_ready, 2, (g1[:], b1[:]))
                link(v.tensor_tensor(tmp[:], hid[:], hid[:], ALU.mult))
                link(v.tensor_reduce(stat[:, 0, :], tmp[:], AX_X, ALU.add))
                v.tensor_scalar(stat[:, 1, :], stat[:, 0, :], 1.0 / D, EPS, ALU.mult, ALU.add).then_inc(var_ready, 1)
                v.wait_ge(std_ready, 3)
                link(v.reciprocal(stat[:, 1, :], stat[:, 1, :]))
                v.tensor_tensor(hid[:], hid[:], bc(stat[:, 1, :], 2, D), ALU.mult).then_inc(h_ready, 1)

            @block.tensor
            def _(pe):
                pe.wait_ge(ln_in, 64)
                for k, (src, ready) in enumerate(((s.xn, xn_ready), (hid, h_ready))):
                    pe.wait_ge(ready, 1)
                    for t in range(NT):
                        last = pe.transpose(s.bank[4 * k + t // 4][:, P * (t % 4):P * (t % 4 + 1)], src[:, t, :], s.ident[:])
                        if t % 4 == 3:
                            last.then_inc(turned, 1)

            @block.scalar
            def _(a):
                for n in range(3):
                    root(a, var_ready, n + 1, stat[:, 1, :], std_ready)
                for w in range(NW):
                    a.wait_ge(turned, w + 1)
                    a.activation(s.xnT[:, W * w:W * (w + 1)], s.bank[w][:], ACT.Copy).then_inc(copied, 1)
                for w in range(NW):
                    a.wait_ge(turned, NW + w + 1)
                    a.activation(s.hT[:, W * w:W * (w + 1)], s.bank[4 + w][:], ACT.Copy, scale=rw[:]).then_inc(copied, 1)


def phase_project(nc, m, io, s):
    ctx = ExitStack()
    with ctx:
        mm = Memory(nc, ctx, m)
        w = mm.sb("kqv_w", [P, 4 * P])
        gw = mm.sb("gate_w", [P, H * VD + 2 * H])
        cw = mm.sb("conv_w", [P, 4, CONV])
        group = mm.sb("head_ones", [P, P])
        padded = [mm.sb(f"padded{j}", [P, B, CONV - 1 + T]) for j in range(4)]
        dtb = mm.sb("dt_bias", [P, H])
        alog = mm.sb("a_log", [P, H])
        ab = mm.sb("ab", [P, NT, 2 * H])
        az = mm.sb("az", [P, NT, 2 * H])
        ez = mm.sb("ez", [P, NT, 2 * H])
        lp = mm.sb("log1p", [P, NT, 2 * H])
        eps = mm.sb("eps", [P, 2])
        w_in = mm.sem("w_in")
        small_in = mm.sem("small_in")
        pads = mm.sem("pads")
        chain = mm.sem("conv_chain")
        achain = mm.sem("act_chain")
        projected = mm.sem("projected")
        evacuated = mm.sem("evacuated")
        conved = mm.sem("conved")
        silued = mm.sem("silued")
        gated = mm.sem("gated")
        gate_out = mm.sem("gate_out")
        ab_out = mm.sem("ab_out")
        squared = mm.sem("squared")
        summed = mm.sem("summed")
        z_ready = mm.sem("z_ready")
        e_ready = mm.sem("e_ready")
        with nc.Block() as block:
            @block.sync
            def _(sp):
                sp.dma_start(w[:, 0:P], io["L0_attn_Wk"]).then_inc(w_in, 16)
                sp.dma_start(w[:, P:2 * P], io["L0_attn_Wq"]).then_inc(w_in, 16)
                sp.dma_start(w[:, 2 * P:4 * P], io["L0_attn_Wv"]).then_inc(w_in, 16)
                sp.dma_start(cw[:, 0, :], io["L0_attn_conv_k_w"]).then_inc(w_in, 16)
                sp.dma_start(cw[:, 1, :], io["L0_attn_conv_q_w"]).then_inc(w_in, 16)
                sp.dma_start(cw[:, 2:4, :], io["L0_attn_conv_v_w"].rearrange("(j p) i -> p j i", p=P)).then_inc(w_in, 16)
                sp.dma_start(gw[:, 0:H * VD], io["L0_attn_Wg"]).then_inc(small_in, 16)
                sp.dma_start(gw[:, H * VD:H * VD + H], io["L0_attn_Wa"]).then_inc(small_in, 16)
                sp.dma_start(gw[:, H * VD + H:], io["L0_attn_Wb"]).then_inc(small_in, 16)
                sp.dma_start(dtb[:], io["L0_attn_dt_bias"].partition_broadcast(P)).then_inc(small_in, 16)
                sp.dma_start(alog[:], io["L0_attn_A_log"].partition_broadcast(P)).then_inc(small_in, 16)
                sp.dma_start(group[:], io["c_head_ones"]).then_inc(small_in, 16)

            @block.tensor
            def _(pe):
                pe.wait_ge(w_in, 96)
                for j in range(4):
                    for c in range(NW):
                        if j >= 2:
                            pe.wait_ge(evacuated, NW * (j - 2) + c + 1)
                        pe.matmul(s.bank[4 * (j % 2) + c][:], w[:, P * j:P * (j + 1)], s.hT[:, W * c:W * (c + 1)],
                                  start=True, stop=True).then_inc(projected, 1)
                pe.wait_ge(small_in, 96)
                for t in range(NT):
                    pe.wait_ge(evacuated, NW * 2 + t + 1 if t < 8 else NW * 4)
                    if t >= 8:
                        pe.wait_ge(gate_out, t - 7)
                        pe.wait_ge(ab_out, t - 7)
                    pe.matmul(s.bank[t % 8][:, 0:H * VD + 2 * H], s.hT[:, P * t:P * (t + 1)], gw[:],
                              start=True, stop=True).then_inc(gated, 1)
                for j in range(2):
                    pe.wait_ge(squared, j + 1)
                    for c in range(NW):
                        pe.wait_ge(gate_out, 8 + 4 * j + c + 1)
                        pe.wait_ge(ab_out, 8 + 4 * j + c + 1)
                        pe.matmul(s.bank[4 * j + c][:], group[:], s.rs[j][:, W * c:W * (c + 1)],
                                  start=True, stop=True).then_inc(summed, 1)

            @block.vector
            def _(v):
                link = Link(v, chain)
                for j in range(4):
                    v.memset(padded[j][:, :, 0:CONV - 1], 0.0).then_inc(pads, 1)
                v.memset(eps[:, 0:1], EPS).then_inc(pads, 1)
                v.memset(eps[:, 1:2], KD * EPS).then_inc(pads, 1)
                v.wait_ge(pads, 6)
                v.wait_ge(w_in, 96)
                for j in range(4):
                    v.wait_ge(evacuated, NW * (j + 1))
                    y = s.kqv[j][:].rearrange("p (b t) -> p b t", b=B)
                    link(v.tensor_scalar(y, padded[j][:, :, 0:T], cw[:, j, 0:1], None, ALU.mult))
                    for i in range(1, CONV):
                        link(v.scalar_tensor_tensor(y, padded[j][:, :, i:i + T], cw[:, j, i:i + 1], y, ALU.mult, ALU.add))
                    v.engine_nop().then_inc(conved, 1)
                v.wait_ge(ab_out, NT)
                za, zb = ab[:, :, 0:H], ab[:, :, H:2 * H]
                link(v.tensor_tensor(za, za, bc(dtb[:], 1, NT), ALU.add))
                link(v.tensor_scalar(az[:, :, 0:H], za, -1.0, None, ALU.mult))
                link(v.tensor_tensor(az[:, :, 0:H], az[:, :, 0:H], za, ALU.max))
                v.tensor_scalar(az[:, :, H:2 * H], zb, -87.0, None, ALU.max).then_inc(z_ready, 1)
                e, u, d, is0 = ez[:, :, 0:H], az[:, :, 0:H], az[:, :, H:2 * H], lp[:, :, 0:H]
                v.wait_ge(e_ready, 1)
                v.tensor_scalar(u, e, 1.0, None, ALU.add).then_inc(z_ready, 1)
                v.wait_ge(z_ready, 2)
                link(v.tensor_scalar(d, u, -1.0, None, ALU.add))
                link(v.tensor_scalar(is0, d, 0.0, None, ALU.is_equal))
                link(v.tensor_tensor(d, d, is0, ALU.add))
                link(v.reciprocal(d, d))
                link(v.tensor_tensor(d, d, e, ALU.mult))
                v.wait_ge(e_ready, 2)
                link(v.tensor_tensor(is0, lp[:, :, H:2 * H], is0, ALU.add))
                link(v.tensor_tensor(d, d, is0, ALU.mult))
                link(v.tensor_scalar(za, za, 0.0, None, ALU.max))
                link(v.tensor_tensor(za, za, d, ALU.add))
                link(v.tensor_tensor(za, za, bc(alog[:], 1, NT), ALU.mult))
                v.tensor_scalar(s.g[:], za, -1.0, -104.0, ALU.mult, ALU.max).then_inc(z_ready, 1)
                link(v.tensor_scalar(ez[:, :, H:2 * H], ez[:, :, H:2 * H], 1.0, None, ALU.add))
                link(v.reciprocal(s.beta[:], ez[:, :, H:2 * H]))

            @block.scalar
            def _(a):
                link = Link(a, achain)
                def evacuate(j):
                    for c in range(NW):
                        a.wait_ge(projected, NW * j + c + 1)
                        a.activation(padded[j][:, c // 2, CONV - 1 + W * (c % 2):CONV - 1 + W * (c % 2 + 1)],
                                     s.bank[4 * (j % 2) + c][:], ACT.Copy).then_inc(evacuated, 1)

                def silu(j):
                    a.wait_ge(conved, j + 1)
                    a.activation(s.kqv[j][:], s.kqv[j][:], ACT.Silu).then_inc(silued, 1)

                for j in range(4):
                    evacuate(j)
                for t in range(NT):
                    a.wait_ge(gated, t + 1)
                    a.activation(s.gate[:, t, :], s.bank[t % 8][:, 0:H * VD], ACT.Silu).then_inc(gate_out, 1)
                    a.activation(ab[:, t, :], s.bank[t % 8][:, H * VD:H * VD + 2 * H], ACT.Copy).then_inc(ab_out, 1)
                for j in range(4):
                    silu(j)
                for j in range(2):
                    a.wait_ge(silued, j + 1)
                    a.activation(s.rs[j][:], s.kqv[j][:], ACT.Square).then_inc(squared, 1)
                a.wait_ge(small_in, 96)
                link(a.activation(alog[:], alog[:], ACT.Exp))
                a.wait_ge(z_ready, 1)
                a.activation(ez[:], az[:], ACT.Exp, scale=-1.0).then_inc(e_ready, 1)
                a.wait_ge(z_ready, 2)
                a.activation(lp[:, :, H:2 * H], az[:, :, 0:H], ACT.Ln).then_inc(e_ready, 1)
                for j in range(2):
                    for c in range(NW):
                        a.wait_ge(summed, NW * j + c + 1)
                        link(a.activation(s.rs[j][:, W * c:W * (c + 1)], s.bank[4 * j + c][:], ACT.Ln,
                                          bias=eps[:, j:j + 1], scale=float(KD if j else 1)))
                for j in range(2):
                    a.activation(s.rs[j][:], s.rs[j][:], ACT.Exp, scale=-0.5)


def phase_delta(nc, m, io, s):
    LINKS_V = 2 * (3 + 1 + P // C)
    ctx = ExitStack()
    with ctx:
        mm = Memory(nc, ctx, m)
        le = mm.sb("le", [P, P])
        gt = mm.sb("gt", [P, P])
        lvl = mm.sb("lvl", [P, LEVELS, P])
        own = mm.sb("own", [P, H])

        def pair(name, shape):
            return [mm.sb(f"{name}{b}", shape) for b in range(B)]

        kt = pair("kt", [P, P])
        qt = pair("qt", [P, P])
        kbd = pair("kbd", [P, H, P])
        qbd = pair("qbd", [P, H, P])
        vt = pair("vt", [P, 2, P])
        gm = pair("gm", [P, H, P])
        gch = pair("gch", [P, H, KD])
        dmb = pair("dmb", [P, H, P])
        expd = pair("expd", [P, P + 2 * H])
        eb = pair("eb", [P, H])
        at = pair("at", [P, H, P])
        pt = pair("pt", [P, H, P])
        qg = pair("qg", [P, P])
        tok = pair("tok", [P, 3 * P])
        kend = pair("kend", [P, P])
        kg = pair("kg", [P, P])
        off = [pair(f"off{l}_", [P, H, P]) for l in range(2)]
        idle = mm.sb("delta_idle", [P, B])
        xx = pair("xx", [P, H, P])
        tt = pair("tt", [P, H, P])
        rr = pair("rr", [P, H, P])
        wt = pair("wt", [P, P])
        uu = pair("uu", [P, H * VD])
        yy = pair("yy", [P, H * VD])
        st = pair("st", [P, H, VD])
        sown = pair("sown", [P, H, VD])

        def sems(name):
            return [mm.sem(f"{name}{b}") for b in range(B)]

        const_in = mm.sem("const_in")
        chain = mm.sem("delta_chain")
        staged = sems("staged")
        v_staged = sems("v_staged")
        spread = sems("spread")
        masks_g = sems("masks_g")
        decays = sems("decays")
        products = sems("products")
        expd_done = sems("expd_done")
        at_done = sems("at_done")
        turned = sems("turned")
        tok_done = sems("tok_done")
        kscaled = sems("kscaled")
        x_done = sems("x_done")
        t_turned = sems("t_turned")
        t_done = sems("t_done")
        off_done = sems("off_done")
        r_ready = sems("r_ready")
        r_done = sems("r_done")
        dx_ready = sems("dx_ready")
        x_turned = sems("x_turned")
        x_copied = sems("x_copied")
        wu_ready = sems("wu_ready")
        wu_done = sems("wu_done")
        z_ready = sems("z_ready")
        y_done = sems("y_done")
        s_ready = sems("s_ready")
        o_ready = sems("o_ready")
        s_done = sems("s_done")
        o_done = sems("o_done")
        L1 = LEVELS - 1
        NC = P // C

        def over_turns(eng, turn):
            with eng.Fori(0, TB - 1) as i:
                turn(i, True)
            turn(TB - 1, False)

        def tokens(i, b):
            return bass.ds(i * P + b * T, P)

        with nc.Block() as block:
            @block.sync
            def _(sp):
                sp.dma_start(le[:], io["c_le"]).then_inc(const_in, 16)
                sp.dma_start(gt[:], io["c_gt"]).then_inc(const_in, 16)
                sp.dma_start(lvl[:], io["c_levels"]).then_inc(const_in, 16)
                sp.dma_start(own[:], io["c_own"]).then_inc(const_in, 16)

            @block.gpsimd
            def _(g):
                g.wait_ge(const_in, 64)

                def spread_heads(i):
                    for b in range(B):
                        for k, (flat, wide) in enumerate(((kt, kbd), (qt, qbd))):
                            g.wait_ge(staged[b], 2 * i + (k + 1))
                            g.tensor_tensor(wide[b][:], bc(flat[b][:], 1, H), bc(own[:], 2, P), ALU.mult).then_inc(spread[b], 1)

                def turn(i, more):
                    for l in range(1, LEVELS):
                        for b in range(B):
                            if l == 1:
                                g.wait_ge(at_done[b], 2 * i + 1)
                            if l > 2:
                                g.wait_ge(r_ready[b], i * L1 + (l - 2))
                            g.tensor_tensor(off[l % 2][b][:], at[b][:], bc(lvl[:, l, :], 1, H), ALU.mult).then_inc(off_done[b], 1)
                    if more:
                        spread_heads(i + 1)

                spread_heads(0)
                over_turns(g, turn)

            @block.vector
            def _(v):
                for b in range(B):
                    v.memset(st[b][:], 0.0).then_inc(s_done[b], 1)
                    v.memset(idle[:, b:b + 1], 0.0).then_inc(o_done[b], 1)
                for b in range(B):
                    v.wait_ge(s_done[b], 1)
                v.wait_ge(const_in, 64)

                def stage(i, b):
                    cols = tokens(i, b)
                    v.tensor_tensor(kt[b][:], s.kqv[0][:, cols], s.rs[0][:, cols], ALU.mult).then_inc(staged[b], 1)
                    v.tensor_tensor(qt[b][:], s.kqv[1][:, cols], s.rs[1][:, cols], ALU.mult).then_inc(staged[b], 1)
                    gi = s.g[:, bass.ds(i + b * TB, 1), :].rearrange("p a h -> p (a h)")
                    v.tensor_tensor(gm[b][:], bc(gt[:], 1, H), bc(gi, 2, P), ALU.mult).then_inc(masks_g[b], 1)
                    v.tensor_copy(gch[b][:], bc(gi, 2, KD)).then_inc(masks_g[b], 1)

                def turn(i, more):
                    link = Link(v, chain, i * LINKS_V)
                    for b in range(B):
                        bi = s.beta[:, bass.ds(i + b * TB, 1), :].rearrange("p a h -> p (a h)")
                        v.wait_ge(expd_done[b], 2 * i + 2)
                        link(v.tensor_tensor(dmb[b][:], dmb[b][:], bc(le[:], 1, H), ALU.mult))
                        link(v.tensor_tensor(dmb[b][:], dmb[b][:], bc(bi, 2, P), ALU.mult))
                        link(v.tensor_tensor(eb[b][:], expd[b][:, P + H:], bi, ALU.mult))
                        v.wait_ge(products[b], i + 1)
                        v.tensor_tensor(at[b][:], s.bank[4 * b + 2][:].rearrange("p (h t) -> p h t", h=H), dmb[b][:],
                                        ALU.mult).then_inc(at_done[b], 1)
                        v.tensor_tensor(pt[b][:], s.bank[4 * b + 3][:].rearrange("p (h t) -> p h t", h=H), dmb[b][:],
                                        ALU.mult).then_inc(at_done[b], 1)
                    for b in range(B):
                        v.wait_ge(at_done[b], 2 * i + 2)
                        link(v.tensor_tensor(tt[b][:], at[b][:], bc(lvl[:, 0, :], 1, H), ALU.mult))
                        v.tensor_tensor(xx[b][:], bc(s.ident[:], 1, H), tt[b][:], ALU.subtract).then_inc(x_done[b], 1)
                    for b in range(B):
                        v.wait_ge(tok_done[b], i + 1)
                        kk = tok[b][:, 0:P].rearrange("p (h c) -> p h c", h=H)
                        v.tensor_tensor(kend[b][:].rearrange("p (h c) -> p h c", h=H), kk, bc(eb[b][:], 2, KD),
                                        ALU.mult).then_inc(kscaled[b], 1)
                        v.tensor_tensor(kg[b][:].rearrange("p (h c) -> p h c", h=H), kk, bc(expd[b][:, P:P + H], 2, KD),
                                        ALU.mult).then_inc(kscaled[b], 1)
                        v.tensor_tensor(qg[b][:], qt[b][:], expd[b][:, 0:P], ALU.mult).then_inc(kscaled[b], 1)
                    for l in range(1, LEVELS):
                        for b in range(B):
                            v.wait_ge(dx_ready[b], i * L1 + l)
                            x = (tt if l < L1 else xx)[b][:].rearrange("p h t -> p (h t)")
                            v.tensor_tensor(x, x, s.bank[4 * b + (0 if l < L1 else 3)][:], ALU.subtract).then_inc(x_done[b], 1)
                        if more and l <= B:
                            v.wait_ge(kscaled[l - 1], 3 * i + 3)
                            stage(i + 1, l - 1)
                    for c in range(NC):
                        rows = slice(C * c, C * (c + 1))
                        for b in range(B):
                            v.wait_ge(wu_done[b], 2 * i + 2)
                            v.wait_ge(z_ready[b], i * NC + c + 1)
                            v.tensor_tensor(yy[b][rows, :], uu[b][rows, :], s.bank[4 * b + 3][rows, 0:H * VD],
                                            ALU.subtract).then_inc(y_done[b], 1)
                        for b in range(B):
                            last = C * (c + 1) - 1
                            v.wait_ge(s_ready[b], i * NC + c + 1)
                            link(v.tensor_tensor(sown[b][:], s.bank[4 * b + 1][:, 0:H * VD].rearrange("p (h v) -> p h v", h=H),
                                                 bc(own[:], 2, VD), ALU.mult))
                            v.scalar_tensor_tensor(st[b][:], st[b][:], expd[b][:, last:last + 1], sown[b][:],
                                                   ALU.mult, ALU.add).then_inc(s_done[b], 1)
                    assert link.n == LINKS_V, link.n

                for b in range(B):
                    stage(0, b)
                over_turns(v, turn)

            @block.scalar
            def _(a):
                def stage(i):
                    for b in range(B):
                        for j in range(2):
                            a.activation(vt[b][:, j, :], s.kqv[2 + j][:, tokens(i, b)], ACT.Copy).then_inc(v_staged[b], 1)

                def turn(i, more):
                    for b in range(B):
                        a.wait_ge(decays[b], i + 1)
                        a.activation(dmb[b][:].rearrange("p h t -> p (h t)"), s.bank[4 * b][:], ACT.Exp).then_inc(expd_done[b], 1)
                        a.activation(expd[b][:], s.bank[4 * b + 1][:, 0:P + 2 * H], ACT.Exp).then_inc(expd_done[b], 1)
                    for b in range(B):
                        a.wait_ge(turned[b], i + 1)
                        a.activation(tok[b][:], s.bank[4 * b + 1][:, 0:3 * P], ACT.Copy).then_inc(tok_done[b], 1)
                    for b in range(B):
                        a.wait_ge(t_turned[b], i + 1)
                        a.activation(tt[b][:].rearrange("p h t -> p (h t)"), s.bank[4 * b][:], ACT.Copy).then_inc(t_done[b], 1)
                    for l in range(1, LEVELS):
                        for b in range(B):
                            a.wait_ge(r_ready[b], i * L1 + l)
                            a.activation(rr[b][:].rearrange("p h t -> p (h t)"), s.bank[4 * b + 2][:], ACT.Copy).then_inc(r_done[b], 1)
                            if l > 1:
                                a.wait_ge(x_turned[b], i * (L1 - 1) + (l - 1))
                                a.activation(xx[b][:].rearrange("p h t -> p (h t)"), s.bank[4 * b + 3][:], ACT.Copy).then_inc(x_copied[b], 1)
                        if more and l == 2:
                            stage(i + 1)
                    for b in range(B):
                        a.wait_ge(wu_ready[b], i + 1)
                        a.activation(wt[b][:], s.bank[4 * b + 1][:, 0:P], ACT.Copy).then_inc(wu_done[b], 1)
                        a.activation(uu[b][:], s.bank[4 * b + 2][:, 0:H * VD], ACT.Copy).then_inc(wu_done[b], 1)
                    for b in range(B):
                        a.wait_ge(o_ready[b], (i + 1) * NC)
                        a.activation(s.o[:, bass.ds(i + b * TB, 1), :].rearrange("p a c -> p (a c)"), s.bank[4 * b][:, 0:H * VD],
                                     ACT.Copy).then_inc(o_done[b], 1)

                stage(0)
                over_turns(a, turn)

            @block.tensor
            def _(pe):
                pe.wait_ge(const_in, 64)

                def turn(i, more):
                    for b in range(B):
                        p0, p1, p2, p3 = s.bank[4 * b:4 * b + 4]
                        pe.wait_ge(o_done[b], i + 1)
                        pe.wait_ge(s_done[b], i * NC + 1)
                        pe.wait_ge(masks_g[b], 2 * i + 2)
                        gi = s.g[:, bass.ds(i + b * TB, 1), :].rearrange("p a h -> p (a h)")
                        for h in range(H):
                            pe.matmul(p0[:, P * h:P * (h + 1)], gm[b][:, h, :], le[:], start=True, stop=True)
                        pe.matmul(p1[:, 0:P], gch[b][:].rearrange("p h c -> p (h c)"), le[:], start=True, stop=True)
                        pe.matmul(p1[:, P:P + H], le[:], gi, start=True, stop=True)
                        pe.matmul(p1[:, P + H:P + 2 * H], gt[:], gi, start=True, stop=True).then_inc(decays[b], 1)
                        pe.wait_ge(staged[b], 2 * i + 1)
                        pe.wait_ge(spread[b], 2 * i + 1)
                        pe.matmul(p2[:], kt[b][:], kbd[b][:].rearrange("p h t -> p (h t)"), start=True, stop=True)
                        pe.wait_ge(spread[b], 2 * i + 2)
                        pe.matmul(p3[:], kt[b][:], qbd[b][:].rearrange("p h t -> p (h t)"), start=True,
                                  stop=True).then_inc(products[b], 1)
                    for b in range(B):
                        p1 = s.bank[4 * b + 1]
                        pe.wait_ge(expd_done[b], 2 * i + 2)
                        pe.wait_ge(v_staged[b], 2 * i + 2)
                        pe.transpose(p1[:, 0:P], kt[b][:], s.ident[:])
                        pe.transpose(p1[:, P:2 * P], vt[b][:, 0, :], s.ident[:])
                        pe.transpose(p1[:, 2 * P:3 * P], vt[b][:, 1, :], s.ident[:]).then_inc(turned[b], 1)
                    for b in range(B):
                        pe.wait_ge(x_done[b], i * LEVELS + 1)
                        for h in range(H):
                            last = pe.transpose(s.bank[4 * b][:, P * h:P * (h + 1)], xx[b][:, h, :], s.ident[:])
                        last.then_inc(t_turned[b], 1)
                    for l in range(1, LEVELS):
                        for b in range(B):
                            if l == 1:
                                pe.wait_ge(t_done[b], i + 1)
                                pe.wait_ge(at_done[b], 2 * i + 2)
                            pe.wait_ge(x_done[b], i * LEVELS + l)
                            pe.wait_ge(off_done[b], i * L1 + l)
                            for h in range(H):
                                last = pe.matmul(s.bank[4 * b + 2][:, P * h:P * (h + 1)], off[l % 2][b][:, h, :], tt[b][:, h, :],
                                                 start=True, stop=True)
                            last.then_inc(r_ready[b], 1)
                            if l > 1:
                                for h in range(H):
                                    last = pe.transpose(s.bank[4 * b + 3][:, P * h:P * (h + 1)], tt[b][:, h, :], s.ident[:])
                                last.then_inc(x_turned[b], 1)
                        for b in range(B):
                            pe.wait_ge(r_done[b], i * L1 + l)
                            if l > 1:
                                pe.wait_ge(x_copied[b], i * (L1 - 1) + (l - 1))
                            for h in range(H):
                                if l < L1:
                                    last = pe.matmul(s.bank[4 * b][:, P * h:P * (h + 1)], xx[b][:, h, :], rr[b][:, h, :], start=True, stop=True)
                                else:
                                    last = pe.matmul(s.bank[4 * b + 3][:, P * h:P * (h + 1)], rr[b][:, h, :], xx[b][:, h, :], start=True, stop=True)
                            last.then_inc(dx_ready[b], 1)
                    for b in range(B):
                        pe.wait_ge(x_done[b], (i + 1) * LEVELS)
                        pe.wait_ge(kscaled[b], 3 * i + 3)
                        pe.wait_ge(tok_done[b], i + 1)
                        for h in range(H):
                            pe.matmul(s.bank[4 * b + 1][KD * h:KD * (h + 1), 0:P], kg[b][:, KD * h:KD * (h + 1)], xx[b][:, h, :],
                                      start=True, stop=True)
                        for h in range(H):
                            last = pe.matmul(s.bank[4 * b + 2][:, VD * h:VD * (h + 1)], xx[b][:, h, :],
                                             tok[b][:, P + VD * h:P + VD * (h + 1)], start=True, stop=True)
                        last.then_inc(wu_ready[b], 1)
                    for c in range(NC):
                        cols = slice(C * c, C * (c + 1))
                        for b in range(B):
                            p0, p1, p2, p3 = s.bank[4 * b:4 * b + 4]
                            pe.wait_ge(wu_done[b], 2 * i + 2)
                            pe.wait_ge(s_done[b], i * NC + (c + 1))
                            state = st[b][:].rearrange("p h v -> p (h v)")
                            pe.matmul(p3[cols, 0:H * VD], wt[b][:, cols], state, start=True, stop=True).then_inc(z_ready[b], 1)
                            pe.matmul(p0[cols, 0:H * VD], qg[b][:, cols], state, start=True, stop=False, skip_group_check=True)
                        for b in range(B):
                            p0, p1, p2, p3 = s.bank[4 * b:4 * b + 4]
                            pe.wait_ge(y_done[b], i * NC + c + 1)
                            pe.matmul(p1[:, 0:H * VD], kend[b][cols, :], yy[b][cols, :], start=True, stop=True).then_inc(s_ready[b], 1)
                            for h in range(H):
                                last = pe.matmul(p0[cols, VD * h:VD * (h + 1)], pt[b][cols, h, cols], yy[b][cols, VD * h:VD * (h + 1)],
                                                 start=False, stop=h == H - 1, skip_group_check=True)
                            last.then_inc(o_ready[b], 1)

                over_turns(pe, turn)


def phase_encode(nc, m, io, s):
    ctx = ExitStack()
    with ctx:
        mm = Memory(nc, ctx, m)
        nw = mm.sb("o_norm_w", [P, VD])
        wo = mm.sb("wo", [P, 2, D])
        w2 = mm.sb("w2", [P, D])
        b2 = mm.sb("b2", [1, D])
        ones = mm.sb("ones", [1, P])
        g2 = mm.sb("ln2_g", [P, D])
        bb2 = mm.sb("ln2_b", [P, D])
        osq = mm.sb("osq", [P, NT * H, VD])
        ost = mm.sb("ost", [P, NT * H])
        oT = mm.sb("oT", [P, 2, N])
        xe = mm.sb("xe", [P, NT, D])
        h2 = mm.sb("h2", [P, NT, D])
        h2T = mm.sb("h2T", [P, N])
        stat = mm.sb("enc_stat", [P, 2, NT])
        w_in = mm.sem("enc_w_in")
        chain = mm.sem("enc_chain")
        squared = mm.sem("o_squared")
        gate_done = mm.sem("gate_done")
        var_ready = mm.sem("enc_var")
        std_ready = mm.sem("enc_std")
        o_ready = mm.sem("o_ready")
        turned = mm.sem("enc_turned")
        copied = mm.sem("enc_copied")
        encoded = mm.sem("encoded")
        xe_done = mm.sem("xe_done")
        h2_ready = mm.sem("h2_ready")
        h2_out = mm.sem("h2_out")
        gelued = mm.sem("gelued")
        ov = s.o[:].rearrange("p t (h v) -> p (t h) v", v=VD)
        with nc.Block() as block:
            @block.sync
            def _(sp):
                sp.dma_start(nw[:], io["L0_attn_o_norm_w"].partition_broadcast(P)).then_inc(w_in, 16)
                sp.dma_start(wo[:], io["L0_attn_Wo"].rearrange("(j p) d -> p j d", p=P)).then_inc(w_in, 16)
                sp.dma_start(w2[:], io["L0_attn_W2"]).then_inc(w_in, 16)
                sp.dma_start(b2[:], io["L0_attn_b2"].rearrange("(a d) -> a d", a=1)).then_inc(w_in, 16)
                sp.dma_start(g2[:], io["L0_attn_ln2_g"].partition_broadcast(P)).then_inc(w_in, 16)
                sp.dma_start(bb2[:], io["L0_attn_ln2_b"].partition_broadcast(P)).then_inc(w_in, 16)

            @block.gpsimd
            def _(g):
                g.memset(ones[:], 1.0).then_inc(gate_done, 1)
                g.wait_ge(w_in, 96)
                gv = s.gate[:].rearrange("p t (h v) -> p (t h) v", v=VD)
                g.tensor_tensor(gv, gv, bc(nw[:], 1, NT * H), ALU.mult).then_inc(gate_done, 1)

            @block.vector
            def _(v):
                link = Link(v, chain)
                v.wait_ge(squared, 1)
                link(v.tensor_reduce(ost[:], osq[:], AX_X, ALU.add))
                v.tensor_scalar(ost[:], ost[:], 1.0 / VD, EPS, ALU.mult, ALU.add).then_inc(var_ready, 1)
                v.wait_ge(std_ready, 1)
                link(v.reciprocal(ost[:], ost[:]))
                link(v.tensor_tensor(ov, ov, bc(ost[:], 2, VD), ALU.mult))
                v.wait_ge(gate_done, 2)
                v.tensor_tensor(s.o[:], s.o[:], s.gate[:], ALU.mult).then_inc(o_ready, 1)
                for w in range(NW):
                    v.wait_ge(encoded, w + 1)
                    v.tensor_tensor(xe[:, 4 * w:4 * w + 4, :], s.xn[:, 4 * w:4 * w + 4, :],
                                    s.bank[w][:].rearrange("p (t d) -> p t d", d=D), ALU.add).then_inc(xe_done, 1)
                v.wait_ge(xe_done, NW)
                v.wait_ge(w_in, 96)
                layer_norm(v, link, h2[:], xe[:], s.s0[:], stat, var_ready, std_ready, 2, (g2[:], bb2[:]))
                v.engine_nop().then_inc(h2_ready, 1)
                for w in range(NW):
                    v.wait_ge(gelued, w + 1)
                    v.tensor_tensor(s.s0[:, 4 * w:4 * w + 4, :], s.s0[:, 4 * w:4 * w + 4, :], xe[:, 4 * w:4 * w + 4, :], ALU.add)

            @block.tensor
            def _(pe):
                pe.wait_ge(w_in, 96)
                pe.wait_ge(gate_done, 1)
                pe.wait_ge(o_ready, 1)
                for j in range(2):
                    for t in range(NT):
                        last = pe.transpose(s.bank[4 * j + t // 4][:, P * (t % 4):P * (t % 4 + 1)],
                                            s.o[:, t, P * j:P * (j + 1)], s.ident[:])
                        if t % 4 == 3:
                            last.then_inc(turned, 1)
                pe.wait_ge(copied, 2 * NW)
                for t in range(NT):
                    for j in range(2):
                        last = pe.matmul(s.bank[t // 4][:, P * (t % 4):P * (t % 4 + 1)], oT[:, j, P * t:P * (t + 1)], wo[:, j, :],
                                         start=j == 0, stop=j == 1)
                    if t % 4 == 3:
                        last.then_inc(encoded, 1)
                pe.wait_ge(h2_ready, 1)
                for t in range(NT):
                    last = pe.transpose(s.bank[4 + t // 4][:, P * (t % 4):P * (t % 4 + 1)], h2[:, t, :], s.ident[:])
                    if t % 4 == 3:
                        last.then_inc(turned, 1)
                for t in range(NT):
                    pe.wait_ge(copied, 2 * NW + t // 4 + 1)
                    out = s.bank[t // 4][:, P * (t % 4):P * (t % 4 + 1)]
                    pe.matmul(out, h2T[:, P * t:P * (t + 1)], w2[:], start=True, stop=False)
                    last = pe.matmul(out, ones[:], b2[:], start=False, stop=True)
                    if t % 4 == 3:
                        last.then_inc(h2_out, 1)

            @block.scalar
            def _(a):
                a.activation(osq[:], ov, ACT.Square).then_inc(squared, 1)
                root(a, var_ready, 1, ost[:], std_ready)
                for n in range(2 * NW):
                    a.wait_ge(turned, n + 1)
                    a.activation(oT[:, n // NW, W * (n % NW):W * (n % NW + 1)], s.bank[n][:], ACT.Copy).then_inc(copied, 1)
                root(a, var_ready, 2, stat[:, 1, :], std_ready)
                for n in range(NW):
                    a.wait_ge(turned, 2 * NW + n + 1)
                    a.activation(h2T[:, W * n:W * (n + 1)], s.bank[4 + n][:], ACT.Copy).then_inc(copied, 1)
                for n in range(NW):
                    a.wait_ge(h2_out, n + 1)
                    a.activation(s.s0[:, 4 * n:4 * n + 4, :].rearrange("p t d -> p (t d)"), s.bank[n][:],
                                 ACT.Gelu).then_inc(gelued, 1)


def phase_experts(nc, m, io, s):
    NJ = B * TOPK
    ctx = ExitStack()
    with ctx:
        mm = Memory(nc, ctx, m)
        wr = mm.sb("wr", [P, E])
        br = mm.sb("br", [1, E])
        ones = mm.sb("ones_row", [1, P])
        mean = mm.sb("mean_x", [P, B])
        lg = mm.sb("logits", [1, B, E])
        st = mm.sb("router_stat", [1, B, 2])
        top = mm.sb("top", [1, B, 8])
        idx = mm.sb("expert", [1, B, 8], U32)
        cw = mm.sb("mix", [1, B, TOPK])
        cwb = mm.sb("mix_b", [P, NJ])
        w1 = [mm.sb(f"w1_{j}", [P, F]) for j in range(NJ)]
        w2 = [mm.sb(f"w2_{j}", [P, FB, D]) for j in range(NJ)]
        b1 = [mm.sb(f"b1_{j}", [P, FB]) for j in range(NJ)]
        b2 = [mm.sb(f"b2_{j}", [1, D]) for j in range(NJ)]
        hh = [mm.sb(f"hidden{n}", [P, TOPK * FB, W]) for n in range(2)]
        y = mm.sb("y_moe", [P, NT, D])
        tmp = mm.sb("moe_tmp", [P, NT, D])
        stat = mm.sb("moe_stat", [P, 2, NT])
        gam = mm.sb("gamma", [P, D])
        bet = mm.sb("beta_ln", [P, D])
        in_ = mm.sem("router_in")
        chain = mm.sem("moe_chain")
        mean_done = mm.sem("mean_done")
        logit_ready = mm.sem("logit_ready")
        sub_done = mm.sem("sub_done")
        exp_done = mm.sem("exp_done")
        picked = mm.sem("picked")
        mixed = mm.sem("mixed")
        mix_out = mm.sem("mix_out")
        mix_done = mm.sem("mix_done")
        w_in = [mm.sem(f"expert_in{j}") for j in range(NJ)]
        scaled = mm.sem("scaled")
        up = mm.sem("up")
        act = mm.sem("act")
        down = mm.sem("down")
        summed = mm.sem("y_summed")
        var_ready = mm.sem("moe_var")
        std_ready = mm.sem("moe_std")
        normed = mm.sem("y_normed")
        NU = TOPK * FB
        with nc.Block() as block:
            @block.sync
            def _(sp):
                sp.dma_start(wr[:], io["L0_ffn_Wr"]).then_inc(in_, 16)
                sp.dma_start(br[:], io["L0_ffn_br"].rearrange("(a e) -> a e", a=1)).then_inc(in_, 16)
                sp.dma_start(gam[:], io["L0_ffn_gamma"].partition_broadcast(P)).then_inc(in_, 16)
                sp.dma_start(bet[:], io["L0_ffn_beta"].partition_broadcast(P)).then_inc(in_, 16)
                sp.wait_ge(picked, B)
                for j in range(NJ):
                    e = sp.value_load(idx[0:1, j // TOPK, j % TOPK:j % TOPK + 1], min_val=0, max_val=E - 1)
                    pick = bass.ds(e, 1)
                    sp.dma_start(w1[j][:], io["L0_ffn_W1"][pick].rearrange("a p f -> p (a f)")).then_inc(w_in[j], 16)
                    sp.dma_start(b1[j][:], io["b1_by_feature"][pick].rearrange("a p f -> p (a f)")).then_inc(w_in[j], 16)
                    sp.dma_start(w2[j][:], io["L0_ffn_W2"][pick].rearrange("a (f p) d -> p (a f) d", p=P)).then_inc(w_in[j], 16)
                    sp.dma_start(b2[j][:], io["L0_ffn_b2"][pick]).then_inc(w_in[j], 16)

            @block.vector
            def _(v):
                link = Link(v, chain)
                link(v.memset(ones[:], 1.0))
                link(v.tensor_reduce(mean[:], s.xnT[:].rearrange("p (b t) -> p b t", b=B), AX_X, ALU.add))
                v.tensor_scalar(mean[:], mean[:], 1.0 / T, None, ALU.mult).then_inc(mean_done, 1)
                v.wait_ge(in_, 64)
                v.wait_ge(logit_ready, 1)
                link(v.tensor_tensor(lg[:], s.bank[0][0:1, 0:B * E].rearrange("p (b e) -> p b e", b=B), bc(br[:], 1, B), ALU.add))
                link(v.tensor_reduce(st[:, :, 0], lg[:], AX_X, ALU.max))
                v.tensor_tensor(lg[:], lg[:], bc(st[:, :, 0], 2, E), ALU.subtract).then_inc(sub_done, 1)
                v.wait_ge(exp_done, 1)
                link(v.tensor_reduce(st[:, :, 1], lg[:], AX_X, ALU.add))
                link(v.reciprocal(st[:, :, 1], st[:, :, 1]))
                link(v.tensor_tensor(lg[:], lg[:], bc(st[:, :, 1], 2, E), ALU.mult))
                for b in range(B):
                    link(v.max(top[:, b, :], lg[:, b, :]))
                    v.max_index(idx[:, b, :], top[:, b, :], lg[:, b, :]).then_inc(picked, 1)
                v.tensor_tensor(cw[:], top[:, :, 0:TOPK], bc(top[:, :, 0], 2, TOPK), ALU.subtract).then_inc(sub_done, 1)
                v.wait_ge(exp_done, 2)
                link(v.tensor_reduce(st[:, :, 1], cw[:], AX_X, ALU.add))
                link(v.reciprocal(st[:, :, 1], st[:, :, 1]))
                v.tensor_tensor(cw[:], cw[:], bc(st[:, :, 1], 2, TOPK), ALU.mult).then_inc(mixed, 1)
                v.wait_ge(mixed, 1)
                v.wait_ge(mix_done, 1)
                for j in range(NJ):
                    v.wait_ge(w_in[j], 64)
                    v.tensor_scalar(w2[j][:], w2[j][:], cwb[:, j:j + 1], None, ALU.mult).then_inc(scaled, 1)
                    v.tensor_scalar(b2[j][:], b2[j][:], cw[0:1, j // TOPK, j % TOPK:j % TOPK + 1], None, ALU.mult).then_inc(scaled, 1)
                for t in range(NT):
                    v.wait_ge(down, t + 1)
                    v.tensor_tensor(y[:, t, :], s.bank[4 + t % 4][:, 0:D], s.xn[:, t, :], ALU.add).then_inc(summed, 1)
                v.wait_ge(summed, NT)
                layer_norm(v, link, tmp[:], y[:], s.g0[:], stat, var_ready, std_ready, 1, (gam[:], bet[:]))
                v.engine_nop().then_inc(normed, 1)

            @block.scalar
            def _(a):
                a.wait_ge(sub_done, 1)
                a.activation(lg[:], lg[:], ACT.Exp).then_inc(exp_done, 1)
                a.wait_ge(sub_done, 2)
                a.activation(cw[:], cw[:], ACT.Exp).then_inc(exp_done, 1)
                a.wait_ge(mix_out, 1)
                a.activation(cwb[:], s.bank[1][:, 0:NJ], ACT.Copy).then_inc(mix_done, 1)
                for w in range(NW):
                    if w >= 2:
                        a.wait_ge(down, 4 * (w - 1))
                    for n in range(NU):
                        j = TOPK * (w // 2) + n // FB
                        a.wait_ge(up, NU * w + n + 1)
                        if w % 2 == 0:
                            a.wait_ge(w_in[j], 64)
                        a.activation(hh[w % 2][:, n, :], s.bank[n % 4][:], ACT.Gelu, bias=b1[j][:, n % FB:n % FB + 1]).then_inc(act, 1)
                root(a, var_ready, 1, stat[:, 1, :], std_ready)
                a.wait_ge(normed, 1)
                a.activation(s.g0[:], tmp[:], ACT.Silu)

            @block.tensor
            def _(pe):
                pe.wait_ge(mean_done, 1)
                pe.wait_ge(in_, 64)
                for b in range(B):
                    last = pe.matmul(s.bank[0][0:1, E * b:E * (b + 1)], mean[:, b:b + 1], wr[:], start=True, stop=True)
                last.then_inc(logit_ready, 1)
                pe.wait_ge(mixed, 1)
                pe.matmul(s.bank[1][:, 0:NJ], ones[:], cw[:].rearrange("p b k -> p (b k)"), start=True, stop=True).then_inc(mix_out, 1)
                pe.wait_ge(mix_done, 1)

                def ups(w):
                    for n in range(NU):
                        j = TOPK * (w // 2) + n // FB
                        if w % 2 == 0:
                            pe.wait_ge(w_in[j], 64)
                        if NU * w + n >= 4:
                            pe.wait_ge(act, NU * w + n - 3)
                        f = n % FB
                        pe.matmul(s.bank[n % 4][:], w1[j][:, P * f:P * (f + 1)], s.xnT[:, W * w:W * (w + 1)],
                                  start=True, stop=True).then_inc(up, 1)

                def downs(w):
                    pe.wait_ge(scaled, 2 * NJ)
                    pe.wait_ge(act, NU * (w + 1))
                    for q in range(4):
                        t = 4 * w + q
                        if t >= 4:
                            pe.wait_ge(summed, t - 3)
                        out = s.bank[4 + q][:, 0:D]
                        for n in range(NU):
                            j = TOPK * (w // 2) + n // FB
                            pe.matmul(out, hh[w % 2][:, n, P * q:P * (q + 1)], w2[j][:, n % FB, :], start=n == 0, stop=False)
                        for k in range(TOPK):
                            last = pe.matmul(out, ones[:], b2[TOPK * (w // 2) + k][:], start=False, stop=k == TOPK - 1)
                        last.then_inc(down, 1)

                ups(0)
                for w in range(NW):
                    if w + 1 < NW:
                        ups(w + 1)
                    downs(w)


def phase_join(nc, m, io, s):
    ctx = ExitStack()
    with ctx:
        mm = Memory(nc, ctx, m)
        tmp = mm.sb("join_tmp", [P, NT, D])
        stat = mm.sb("join_stat", [P, 2, NT])
        chain = mm.sem("join_chain")
        var_ready = mm.sem("join_var")
        std_ready = mm.sem("join_std")
        ready = mm.sem("join_ready")
        turned = mm.sem("join_turned")
        with nc.Block() as block:
            @block.vector
            def _(v):
                link = Link(v, chain)
                link(v.tensor_tensor(s.s0[:], s.s0[:], s.g0[:], ALU.mult))
                link(v.tensor_tensor(s.x[:], s.x[:], s.s0[:], ALU.add))
                layer_norm(v, link, s.xn[:], s.x[:], tmp[:], stat, var_ready, std_ready, 1)
                v.engine_nop().then_inc(ready, 1)

            @block.scalar
            def _(a):
                root(a, var_ready, 1, stat[:, 1, :], std_ready)
                for n in range(NW):
                    a.wait_ge(turned, n + 1)
                    a.activation(s.xnT[:, W * n:W * (n + 1)], s.bank[n][:], ACT.Copy)

            @block.tensor
            def _(pe):
                pe.wait_ge(ready, 1)
                for t in range(NT):
                    last = pe.transpose(s.bank[t // 4][:, P * (t % 4):P * (t % 4 + 1)], s.xn[:, t, :], s.ident[:])
                    if t % 4 == 3:
                        last.then_inc(turned, 1)


def phase_ternary(nc, m, io, s):
    ctx = ExitStack()
    with ctx:
        mm = Memory(nc, ctx, m)
        raw = mm.sb("raw", [P, IB, N])
        raw_v = raw[:].rearrange("p j n -> p (j n)").rearrange("p (t c) -> p t c", c=INNER)
        wk = mm.sb("wk", [P, INNER])
        wks = mm.sb("wk_swapped", [P, INNER])
        wv = mm.sb("wv", [P, INNER])
        wb = mm.sb("wb", [P, NH])
        bb = mm.sb("bb", [P, NH])
        turn = [mm.sb(f"rope_part{n}", [P, W]) for n in range(4)]
        junk = mm.sb("abs_out", [P, W])
        acc = mm.sb("abs_sum", [P, 2, 2 * NT])
        tot = mm.sb("abs_total", [P, 2])
        low = mm.sb("not_above", [P, 2 * N], BF16)
        thr = mm.sb("thr", [P, 4])
        ones = mm.sb("ones_sq", [P, P])
        w_in = mm.sem("qk_w_in")
        chain = mm.sem("tern_chain")
        achain = mm.sem("tern_act_chain")
        k_ready = mm.sem("k_ready")
        parts = mm.sem("rope_parts")
        k_done = mm.sem("k_done")
        k_abs = mm.sem("k_abs")
        total_in = mm.sem("total_in")
        total = mm.sem("total")
        thr_done = mm.sem("thr_done")
        k_tern = mm.sem("k_tern")
        v_ready = mm.sem("v_ready")
        v_done = mm.sem("v_done")
        b_ready = mm.sem("b_ready")
        z_ready = mm.sem("bz_ready")
        floored = mm.sem("floored")
        e_ready = mm.sem("be_ready")
        NU = NW * IB
        with nc.Block() as block:
            @block.sync
            def _(sp):
                sp.dma_start(wk[:], io["L1_attn_WkT"]).then_inc(w_in, 16)
                sp.dma_start(wks[:], io["L1_attn_WkT_swapped"]).then_inc(w_in, 16)
                sp.dma_start(s.cos[:], io["c_cos"]).then_inc(w_in, 16)
                sp.dma_start(s.sin[:], io["c_sin"]).then_inc(w_in, 16)
                sp.dma_start(wv[:], io["L1_attn_WvT"]).then_inc(w_in, 16)
                sp.dma_start(wb[:], io["L1_attn_WbT"]).then_inc(w_in, 16)
                sp.dma_start(bb[:], io["L1_attn_bb"].partition_broadcast(P)).then_inc(w_in, 16)
                sp.dma_start(s.la[:], io["L1_attn_alpha_log"].rearrange("h a -> (h a)").partition_broadcast(P)).then_inc(w_in, 16)
                for k in range(2):
                    sp.dma_start(s.lac[HD * k:HD * (k + 1), :],
                                 io["alpha_log_by_parity"][k].partition_broadcast(HD)).then_inc(w_in, 16)

            @block.tensor
            def _(pe):
                pe.wait_ge(w_in, 160)
                for w in range(NW):
                    for j in range(IB):
                        n = IB * w + j
                        if n >= 4:
                            pe.wait_ge(parts, 2 * (n - 3))
                        for k, weight in enumerate((wk, wks)):
                            pe.matmul(s.bank[2 * (n % 4) + k][:], weight[:, P * j:P * (j + 1)], s.xnT[:, W * w:W * (w + 1)],
                                      start=True, stop=True).then_inc(k_ready, 1)
                pe.wait_ge(parts, 2 * NU)
                for t in range(NT):
                    last = pe.matmul(s.bank[7][:, NH * t:NH * (t + 1)], s.xnT[:, P * t:P * (t + 1)], wb[:], start=True, stop=True)
                last.then_inc(b_ready, 1)
                pe.wait_ge(total_in, 1)
                pe.matmul(s.bank[6][:, 0:1], ones[:], tot[:, 0:1], start=True, stop=True).then_inc(total, 1)
                for t in range(NT):
                    for k in range(2):
                        n = 2 * t + k
                        if n >= 6:
                            pe.wait_ge(v_done, n - 5)
                        pe.matmul(s.bank[n % 6][:], s.xnT[:, P * t:P * (t + 1)], wv[:, W * k:W * (k + 1)],
                                  start=True, stop=True).then_inc(v_ready, 1)
                pe.wait_ge(total_in, 2)
                pe.matmul(s.bank[6][:, 1:2], ones[:], tot[:, 1:2], start=True, stop=True).then_inc(total, 1)

            @block.gpsimd
            def _(g):
                for n in range(NU):
                    w, j = n // IB, n % IB
                    g.wait_ge(parts, 2 * n + 2)
                    g.tensor_tensor(raw[:, j, W * w:W * (w + 1)], turn[2 * (n % 2)][:], turn[2 * (n % 2) + 1][:],
                                    ALU.add).then_inc(k_done, 1)

            @block.vector
            def _(v):
                link = Link(v, chain)
                link(v.memset(ones[:], 1.0))
                v.wait_ge(w_in, 160)
                for n in range(NU):
                    w = n // IB
                    if n >= 2:
                        v.wait_ge(k_done, n - 1)
                    cols = slice(W * (w % 2), W * (w % 2 + 1))
                    for k, table in enumerate((s.cos, s.sin)):
                        v.wait_ge(k_ready, 2 * n + k + 1)
                        v.tensor_tensor(turn[2 * (n % 2) + k][:], s.bank[2 * (n % 4) + k][:], table[:, cols], ALU.mult).then_inc(parts, 1)

                def threshold(k):
                    link(v.tensor_reduce(tot[:, k:k + 1], acc[:, k, :], AX_X, ALU.add))
                    v.engine_nop().then_inc(total_in, 1)
                    v.wait_ge(total, k + 1)
                    up, dn = thr[:, 2 * k:2 * k + 1], thr[:, 2 * k + 1:2 * k + 2]
                    link(v.tensor_scalar(up, s.bank[6][:, k:k + 1], 1.0 / (N * INNER), None, ALU.mult))
                    link(v.tensor_scalar(up, up, 0.01, 10.0, ALU.max, ALU.min))
                    link(v.tensor_scalar(dn, up, -1.0, None, ALU.mult))
                    return up, dn

                def ternary(k, out, src):
                    up, dn = threshold(k)
                    for n in range(IB // 2):
                        part = src[:, 2 * N * n:2 * N * (n + 1)]
                        link(v.tensor_scalar(low[:], part, up, -1.0, ALU.is_gt, ALU.add))
                        ins = v.scalar_tensor_tensor(out[:, 2 * N * n:2 * N * (n + 1)], part, dn, low[:], ALU.is_ge, ALU.add)
                        link(ins)
                    v.engine_nop().then_inc(k_tern, 1)

                flat = raw[:].rearrange("p j n -> p (j n)")
                v.wait_ge(k_abs, NU)
                ternary(0, s.kt[:].rearrange("p j n -> p (j n)"), flat)
                v.wait_ge(b_ready, 1)
                v.tensor_tensor(s.bk[:], s.bank[7][:, 0:NT * NH].rearrange("p (t h) -> p t h", h=NH), bc(bb[:], 1, NT),
                                ALU.add).then_inc(z_ready, 1)
                v.wait_ge(z_ready, 1)
                for x in (s.bk, s.la, s.lac):
                    v.tensor_scalar(x[:], x[:], -87.0, None, ALU.max).then_inc(floored, 1)
                v.wait_ge(e_ready, 3)
                for x in (s.bk, s.la, s.lac):
                    link(v.tensor_scalar(x[:], x[:], 1.0, None, ALU.add))
                    link(v.reciprocal(x[:], x[:]))
                link(v.tensor_scalar(s.la[:], s.la[:], 1e-6, None, ALU.max))
                link(v.tensor_scalar(s.lac[:], s.lac[:], 1e-6, None, ALU.max))
                v.engine_nop().then_inc(z_ready, 1)
                v.wait_ge(k_abs, NU + 2 * NT)
                ternary(1, s.vt[:].rearrange("p t c -> p (t c)"), flat)

            @block.scalar
            def _(a):
                link = Link(a, achain)
                for n in range(NU):
                    w, j = n // IB, n % IB
                    a.wait_ge(k_done, n + 1)
                    link(a.activation(junk[:], raw[:, j, W * w:W * (w + 1)], ACT.Abs, accum_out=acc[:, 0, n:n + 1]))
                    a.sem_inc(k_abs, 1)
                a.wait_ge(z_ready, 1)
                a.wait_ge(floored, 3)
                for x in (s.bk, s.la, s.lac):
                    a.activation(x[:], x[:], ACT.Exp, scale=-1.0).then_inc(e_ready, 1)
                a.wait_ge(k_tern, 1)
                for n in range(2 * NT):
                    t, k = n // 2, n % 2
                    a.wait_ge(v_ready, n + 1)
                    a.activation(raw_v[:, t, W * k:W * (k + 1)], s.bank[n % 6][:], ACT.Copy).then_inc(v_done, 1)
                    a.wait_ge(v_done, n + 1)
                    link(a.activation(junk[:], raw_v[:, t, W * k:W * (k + 1)], ACT.Abs, accum_out=acc[:, 1, n:n + 1]))
                    a.sem_inc(k_abs, 1)
                a.wait_ge(z_ready, 2)
                a.activation(s.la[:], s.la[:], ACT.Ln)
                a.activation(s.lac[:], s.lac[:], ACT.Ln)


def phase_attend(nc, m, io, s):
    ctx = ExitStack()
    HB = IB // 2
    UH = 2 * HB
    UNITS = 4
    with ctx:
        mm = Memory(nc, ctx, m)
        wq = mm.sb("wq", [P, INNER])
        wqs = mm.sb("wq_swapped", [P, INNER])
        wo = mm.sb("wo1", [P, IB, D])
        gap = mm.sb("gap", [P, P])
        le = mm.sb("le_full", [P, P])
        pos = mm.sb("pos1", [P, P])
        rev = mm.sb("rev", [P, 1])
        dd = mm.sb("dd", [P, NH, P])
        dt_ = mm.sb("decay_t", [P, IB, P])
        de = mm.sb("decay_e", [P, NH])
        part = [[mm.sb(f"q_part{c}{n}", [P, HB, P]) for n in range(2)] for c in range(2)]
        qr = [mm.sb(f"qr{c}", [P, HB, P]) for c in range(2)]
        qbd = [mm.sb(f"q_by_head{c}", [P, HB, 2, P]) for c in range(2)]
        qd = [mm.sb(f"qd{c}", [P, HB, P]) for c in range(2)]
        kf = [mm.sb(f"kf{c}", [P, HB, P]) for c in range(2)]
        kend = [mm.sb(f"k_end{c}", [P, UH, HD]) for c in range(2)]
        vb = [mm.sb(f"vb{c}", [P, UH, HD]) for c in range(2)]
        wT = [mm.sb(f"wT{c}", [P, UH, P]) for c in range(2)]
        oT = [mm.sb(f"o_feat{c}", [P, HB, P]) for c in range(2)]
        st = [mm.sb(f"att_state{b}", [P, IB, P]) for b in range(B)]
        c_in = mm.sem("att_in")
        init = mm.sem("att_init")
        tables = mm.sem("att_tables")
        q_ready = mm.sem("q_ready")
        q_parts = mm.sem("q_parts")
        qr_done = mm.sem("qr_done")
        qd_done = mm.sem("qd_done")
        qbd_done = mm.sem("q_by_head_done")
        kf_done = mm.sem("kf_done")
        vb_done = mm.sem("vb_done")
        k_turned = mm.sem("k_turned")
        kend_done = mm.sem("kend_done")
        scored = mm.sem("scored")
        w_done = mm.sem("w_done")
        o_ready = mm.sem("att_o_ready")
        oT_done = mm.sem("oT_done")
        s_ready = mm.sem("att_s_ready")
        s_done = mm.sem("att_s_done")
        f_ready = mm.sem("f_ready")
        f_done = mm.sem("f_done")

        def number(unit):
            i, b, c = unit
            return i * UNITS + (2 * b + c)

        def tile(unit):
            i, b, c = unit
            return i * B + b

        def after(unit):
            i, b, c = unit
            if c == 0:
                return i, b, 1
            return (i, 1, 0) if b == 0 else (i + 1, 0, 0)

        def over_units(eng, step):
            def tile_units(i, prev, last):
                for b in range(B):
                    for c in range(2):
                        unit = (i, b, c)
                        step(prev, unit, None if last and b + c == 2 else after(unit))
                        prev = unit

            step(None, None, (0, 0, 0))
            tile_units(0, None, False)
            with eng.Fori(0, TB - 2) as k:
                tile_units(k + 1, (k, 1, 1), False)
            tile_units(TB - 1, (TB - 2, 1, 1), True)
            step((TB - 1, 1, 1), None, None)

        def later(eng, sem, value):
            if not (isinstance(value, int) and value <= 0):
                eng.wait_ge(sem, value)

        def tokens(unit):
            i, b, c = unit
            return bass.ds(i * P + b * T, P)

        with nc.Block() as block:
            @block.sync
            def _(sp):
                sp.dma_start(gap[:], io["c_gap"]).then_inc(c_in, 16)
                sp.dma_start(le[:], io["c_le_full"]).then_inc(c_in, 16)
                sp.dma_start(pos[:], io["c_pos1"]).then_inc(c_in, 16)
                sp.dma_start(rev[:], io["c_rev"]).then_inc(c_in, 16)
                sp.dma_start(wq[:], io["L1_attn_WqT"]).then_inc(c_in, 16)
                sp.dma_start(wqs[:], io["L1_attn_WqT_swapped"]).then_inc(c_in, 16)
                sp.dma_start(wo[:], io["L1_attn_WoT"].rearrange("(j p) d -> p j d", p=P)).then_inc(c_in, 16)

            @block.scalar
            def _(a):
                a.wait_ge(c_in, 112)
                for h in range(NH):
                    a.activation(dd[:, h, :], gap[:], ACT.Exp, scale=s.la[:, h:h + 1]).then_inc(tables, 1)
                for j in range(IB):
                    a.activation(dt_[:, j, :], pos[:], ACT.Exp, scale=s.lac[:, j:j + 1]).then_inc(tables, 1)
                a.activation(de[:], s.la[:], ACT.Exp, scale=rev[:]).then_inc(tables, 1)
                a.wait_ge(init, 2 * B + 1)

                def step(prev, unit, nxt):
                    if nxt is not None:
                        n, c = number(nxt), nxt[2]
                        later(a, scored, n - 1)
                        a.activation(kf[c][:], s.kt[:, HB * c:HB * (c + 1), tokens(nxt)], ACT.Copy).then_inc(kf_done, 1)
                    if prev is not None:
                        n, c = number(prev), prev[2]
                        a.wait_ge(o_ready, n + 1)
                        a.activation(oT[c][:].rearrange("p j t -> p (j t)"), s.bank[5][:], ACT.Copy).then_inc(oT_done, 1)
                    if nxt is not None:
                        n, c = number(nxt), nxt[2]
                        a.wait_ge(qr_done, n + 1)
                        for k in range(2):
                            rows = slice(HD * k, HD * (k + 1))
                            a.activation(qbd[c][rows, :, k, :], qr[c][rows], ACT.Copy).then_inc(qbd_done, 1)
                    if prev is not None and prev[2] == 1:
                        i, b, c = prev
                        a.wait_ge(f_ready, tile(prev) + 1)
                        a.activation(s.s1[:, bass.ds(i + b * TB, 1), :].rearrange("p a d -> p (a d)"), s.bank[7][:, 0:D],
                                     ACT.Copy).then_inc(f_done, 1)

                over_units(a, step)

            @block.gpsimd
            def _(g):
                g.wait_ge(tables, NH + IB + 1)

                def step(prev, unit, nxt):
                    if nxt is None:
                        return
                    i, b, c = nxt
                    n = number(nxt)
                    later(g, s_ready, n - 1)
                    beta = s.bk[:, bass.ds(i + b * TB, 1), UH * c:UH * (c + 1)].rearrange("p a h -> p (a h)")
                    g.tensor_tensor(vb[c][:], s.vt[:, bass.ds(i + b * TB, 1), W * c:W * (c + 1)].rearrange("p a (h c) -> p (a h) c", c=HD),
                                    bc(beta, 2, HD), ALU.mult).then_inc(vb_done, 1)
                    g.wait_ge(q_parts, n * 2 + 2)
                    later(g, qbd_done, n * 2 - 2)
                    g.tensor_tensor(qr[c][:], part[c][0][:], part[c][1][:], ALU.add).then_inc(qr_done, 1)
                    g.wait_ge(qr_done, n + 1)
                    g.tensor_tensor(qd[c][:], qr[c][:], dt_[:, HB * c:HB * (c + 1), :], ALU.mult).then_inc(qd_done, 1)

                over_units(g, step)

            @block.vector
            def _(v):
                for b in range(B):
                    v.memset(st[b][:], 0.0).then_inc(init, 1)
                for c in range(2):
                    v.memset(qbd[c][:], 0.0).then_inc(init, 1)
                v.wait_ge(tables, NH + IB + 1)
                v.tensor_tensor(dd[:], dd[:], bc(le[:], 1, NH), ALU.mult).then_inc(init, 1)
                v.wait_ge(init, 2 * B + 1)

                def step(prev, unit, nxt):
                    if unit is not None:
                        n, c = number(unit), unit[2]
                        v.wait_ge(scored, n + 1)
                        for k in range(2):
                            v.tensor_tensor(wT[c][:, 4 * k:4 * (k + 1), :], s.bank[3 + k][:].rearrange("p (h t) -> p h t", t=P),
                                            dd[:, UH * c + 4 * k:UH * c + 4 * (k + 1), :], ALU.mult).then_inc(w_done, 1)
                    if nxt is not None:
                        n, c = number(nxt), nxt[2]
                        v.wait_ge(q_ready, n + 1)
                        later(v, qr_done, n - 1)
                        for k, table in enumerate((s.cos, s.sin)):
                            v.tensor_tensor(part[c][k][:], s.bank[k][:].rearrange("p (j t) -> p j t", t=P),
                                            bc(table[:, bass.ds(nxt[0] * P, P)], 1, HB), ALU.mult).then_inc(q_parts, 1)
                        v.wait_ge(k_turned, n + 1)
                        v.tensor_tensor(kend[c][:], s.bank[2][:].rearrange("p (h c) -> p h c", c=HD),
                                        bc(de[:, UH * c:UH * (c + 1)], 2, HD), ALU.mult).then_inc(kend_done, 1)
                    if unit is not None:
                        i, b, c = unit
                        n = number(unit)
                        v.wait_ge(s_ready, n + 1)
                        later(v, s_done, n * UH)
                        for j in range(HB):
                            for k in range(2):
                                rows, cols = slice(HD * k, HD * (k + 1)), slice(HD * k, HD * (k + 1))
                                block_ = st[b][rows, HB * c + j, cols]
                                v.scalar_tensor_tensor(block_, block_, dt_[rows, HB * c + j, P - 1:P],
                                                       s.bank[6][rows, P * j + HD * k:P * j + HD * (k + 1)], ALU.mult, ALU.add).then_inc(s_done, 1)

                over_units(v, step)

            @block.tensor
            def _(pe):
                pe.wait_ge(c_in, 112)
                pe.wait_ge(init, 2 * B + 1)

                def step(prev, unit, nxt):
                    if unit is not None:
                        n, c = number(unit), unit[2]
                        pe.wait_ge(qbd_done, n * 2 + 2)
                        later(pe, w_done, n * 2)
                        for j in range(HB):
                            last = pe.matmul(s.bank[3 + j // 2][:, 2 * P * (j % 2):2 * P * (j % 2 + 1)], kf[c][:, j, :],
                                             qbd[c][:, j].rearrange("p k t -> p (k t)"), start=True, stop=True)
                        last.then_inc(scored, 1)
                    if nxt is not None:
                        n, c = number(nxt), nxt[2]
                        later(pe, q_parts, n * 2)
                        for k, weight in enumerate((wq, wqs)):
                            for j in range(HB):
                                block_ = P * (HB * c + j)
                                last = pe.matmul(s.bank[k][:, P * j:P * (j + 1)], weight[:, block_:block_ + P], s.xnT[:, tokens(nxt)],
                                                 start=True, stop=True)
                        last.then_inc(q_ready, 1)
                        pe.wait_ge(kf_done, n + 1)
                        later(pe, kend_done, n)
                        for j in range(HB):
                            last = pe.transpose(s.bank[2][:, P * j:P * (j + 1)], kf[c][:, j, :], s.ident[:])
                        last.then_inc(k_turned, 1)
                    if unit is not None:
                        i, b, c = unit
                        n = number(unit)
                        pe.wait_ge(qd_done, n + 1)
                        later(pe, oT_done, n)
                        later(pe, s_done, n * UH)
                        pe.wait_ge(vb_done, n + 1)
                        pe.wait_ge(w_done, n * 2 + 2)
                        for j in range(HB):
                            pe.matmul(s.bank[5][:, P * j:P * (j + 1)], st[b][:, HB * c + j, :], qd[c][:, j, :], start=True, stop=False)
                            for k in range(2):
                                last = pe.matmul(s.bank[5][HD * k:HD * (k + 1), P * j:P * (j + 1)], vb[c][:, 2 * j + k, :],
                                                 wT[c][:, 2 * j + k, :], start=False, stop=True)
                        last.then_inc(o_ready, 1)
                        pe.wait_ge(kend_done, n + 1)
                        for j in range(HB):
                            pair = slice(2 * j, 2 * j + 2)
                            last = pe.matmul(s.bank[6][:, P * j:P * (j + 1)], kend[c][:, pair, :].rearrange("p h c -> p (h c)"),
                                             vb[c][:, pair, :].rearrange("p h c -> p (h c)"), start=True, stop=True)
                        last.then_inc(s_ready, 1)
                    if prev is not None:
                        n, c = number(prev), prev[2]
                        pe.wait_ge(oT_done, n + 1)
                        if c == 0:
                            later(pe, f_done, tile(prev))
                        for j in range(HB):
                            last = pe.matmul(s.bank[7][:, 0:D], oT[c][:, j, :], wo[:, HB * c + j, :],
                                             start=c == 0 and j == 0, stop=c == 1 and j == HB - 1)
                        if c == 1:
                            last.then_inc(f_ready, 1)

                over_units(pe, step)


def phase_keys(nc, m, io, s):
    Q = 2 * PH
    EB = NE // P
    ctx = ExitStack()
    with ctx:
        mm = Memory(nc, ctx, m)
        w = mm.sb("wq_bn", [P, Q, P])
        wt = mm.sb("wq_bn_t", [P, Q, P])
        keys = mm.sb("keys", [P, Q, NK])
        bn = mm.sb("bn", [P, 2, Q])
        down = mm.sb("down_t", [P, NE])
        ones = mm.sb("ones_k", [P, P])
        mrow = mm.sb("mean_row", [P, D])
        mcol = mm.sb("mean_col", [P, 1])
        xc = mm.sb("x_centred", [P, NT, D])
        cov = mm.sb("cov", [P, D])
        wc = mm.sb("w_cov_w", [P, Q, P])
        mv = mm.sb("mean_var", [P, 2, Q])
        k_in = mm.sem("keys_in")
        chain = mm.sem("keys_chain")
        ones_done = mm.sem("ones_done")
        row_ready = mm.sem("row_ready")
        centred = mm.sem("centred")
        cov_ready = mm.sem("cov_ready")
        cov_done = mm.sem("cov_done")
        wc_ready = mm.sem("wc_ready")
        wc_done = mm.sem("wc_done")
        mv_ready = mm.sem("mv_ready")
        var_ready = mm.sem("bn_var")
        std_ready = mm.sem("bn_std")
        scaled = mm.sem("keys_scaled")
        m_ready = mm.sem("m_ready")
        h_ready = mm.sem("down_ready")
        h_done = mm.sem("down_done")
        with nc.Block() as block:
            @block.sync
            def _(sp):
                sp.dma_start(w[:].rearrange("p q d -> p (q d)"), io["L1_ffn_w_q"]).then_inc(k_in, 16)
                sp.dma_start(wt[:], io["w_q_by_key_feature"].rearrange("(q d) m -> d q m", d=P)).then_inc(k_in, 16)
                sp.dma_start(keys[:], io["keys_by_feature"]).then_inc(k_in, 16)
                sp.dma_start(bn[:], io["bn_by_feature"]).then_inc(k_in, 16)
                sp.dma_start(down[:], io["down_by_feature"]).then_inc(k_in, 16)
                sp.dma_start(s.up[:], io["L1_ffn_up_embed"].rearrange("(j p) d -> p j d", p=P)).then_inc(k_in, 16)

            @block.tensor
            def _(pe):
                pe.wait_ge(ones_done, 1)
                for t in range(NT):
                    last = pe.matmul(s.bank[0][:, 0:D], ones[:], s.xn[:, t, :], start=t == 0, stop=t == NT - 1)
                last.then_inc(row_ready, 1)
                pe.wait_ge(centred, 1)
                for t in range(NT):
                    last = pe.matmul(s.bank[1][:, 0:D], xc[:, t, :], xc[:, t, :], start=t == 0, stop=t == NT - 1)
                last.then_inc(cov_ready, 1)
                pe.wait_ge(cov_done, 1)
                pe.wait_ge(k_in, 96)
                for q in range(4):
                    pe.matmul(s.bank[4 + q][:], cov[:], w[:, 4 * q:4 * q + 4, :].rearrange("p q d -> p (q d)"), start=True,
                              stop=True).then_inc(wc_ready, 1)
                for q in range(Q):
                    pe.matmul(s.bank[2][:, q:q + 1], w[:, q, :], mcol[:], start=True, stop=True)
                pe.wait_ge(wc_done, 4)
                for q in range(Q):
                    last = pe.matmul(s.bank[2][:, Q + q:Q + q + 1], wc[:, q, :], ones[:, 0:1], start=True, stop=True)
                last.then_inc(mv_ready, 1)
                for j in range(EB):
                    for c in range(NW):
                        n = NW * j + c
                        if n >= 4:
                            pe.wait_ge(h_done, n - 3)
                        pe.matmul(s.bank[4 + n % 4][:], down[:, P * j:P * (j + 1)], s.xnT[:, W * c:W * (c + 1)], start=True,
                                  stop=True).then_inc(h_ready, 1)
                pe.wait_ge(scaled, 2)
                for q in range(Q):
                    pe.matmul(s.bank[0][:, NK * q:NK * (q + 1)], wt[:, q, :], wc[:, q, 0:NK], start=True, stop=True)
                for q in range(Q):
                    last = pe.matmul(s.bank[1][0:1, NK * q:NK * (q + 1)], mv[:, 0, q:q + 1], keys[:, q, :], start=True, stop=True)
                last.then_inc(m_ready, 1)

            @block.vector
            def _(v):
                link = Link(v, chain)
                link(v.memset(s.ones[:], 1.0))
                v.memset(ones[:], 1.0).then_inc(ones_done, 1)
                link(v.tensor_reduce(mcol[:], s.xnT[:], AX_X, ALU.add))
                link(v.tensor_scalar(mcol[:], mcol[:], 1.0 / N, None, ALU.mult))
                v.wait_ge(row_ready, 1)
                link(v.tensor_scalar(mrow[:], s.bank[0][:, 0:D], 1.0 / N, None, ALU.mult))
                v.tensor_tensor(xc[:], s.xn[:], bc(mrow[:], 1, NT), ALU.subtract).then_inc(centred, 1)
                v.wait_ge(cov_ready, 1)
                v.tensor_scalar(cov[:], s.bank[1][:, 0:D], 1.0 / N, None, ALU.mult).then_inc(cov_done, 1)
                v.wait_ge(k_in, 96)
                for q in range(4):
                    v.wait_ge(wc_ready, q + 1)
                    v.tensor_tensor(wc[:, 4 * q:4 * q + 4, :], w[:, 4 * q:4 * q + 4, :],
                                    s.bank[4 + q][:].rearrange("p (q d) -> p q d", d=P), ALU.mult).then_inc(wc_done, 1)
                v.wait_ge(mv_ready, 1)
                link(v.tensor_copy(mv[:], s.bank[2][:, 0:2 * Q].rearrange("p (k q) -> p k q", k=2)))
                mean, var = mv[:, 0, :], mv[:, 1, :]
                v.tensor_scalar(var, var, LN_EPS, None, ALU.add).then_inc(var_ready, 1)
                v.wait_ge(std_ready, 1)
                link(v.reciprocal(var, var))
                link(v.tensor_tensor(var, var, bn[:, 0, :], ALU.mult))
                v.tensor_tensor(wc[:, :, 0:NK], keys[:], bc(var, 2, NK), ALU.mult).then_inc(scaled, 1)
                link(v.tensor_tensor(mean, mean, var, ALU.mult))
                v.tensor_tensor(mean, bn[:, 1, :], mean, ALU.subtract).then_inc(scaled, 1)
                v.wait_ge(m_ready, 1)
                v.tensor_copy(s.keymat[:], s.bank[0][:])
                v.tensor_copy(s.keyrow[:], s.bank[1][0:1, :])

            @block.scalar
            def _(a):
                root(a, var_ready, 1, mv[:, 1, :], std_ready)
                for n in range(EB * NW):
                    a.wait_ge(h_ready, n + 1)
                    a.activation(s.act[:, n // NW, W * (n % NW):W * (n % NW + 1)], s.bank[4 + n % 4][:],
                                 ACT.Gelu_apprx_tanh).then_inc(h_done, 1)


def phase_product_keys(nc, m, io, s, out):
    Q = 2 * PH
    EB = NE // P
    RING = 4
    POOL_HEADS = 7
    VH = PH - POOL_HEADS
    GROUP = 4
    ctx = ExitStack()
    with ctx:
        mm = Memory(nc, ctx, m)
        xt = mm.sb("x_tile", [P, P])
        sim = [mm.sb(f"sim{u}", [P, Q, NK]) for u in range(2)]
        top = mm.sb("top8", [P, Q, PK])
        comb = mm.sb("comb", [P, PH, PK * PK])
        best = [mm.sb(f"best{u}", [P, PH, PK]) for u in range(2)]
        neg_max = [mm.sb(f"neg_max{u}", [P, PH]) for u in range(2)]
        rel = mm.sb("rel", [P, PH, PK])
        rz = mm.sb("recip_z", [P, PH])
        diag = [mm.sb(f"diag_recip_z{u}", [P, PH, P]) for u in range(2)]
        sums = [mm.sb(f"sums{r}", [P, NK, NK]) for r in range(RING)]
        soft = [mm.sb(f"soft{r}", [P, NE]) for r in range(RING)]
        sel = [mm.sb(f"selected{r}", [P, NE]) for r in range(RING)]
        wgt = mm.sb("weighted", [P, EB, P])
        pk = mm.sb("pk_out", [P, NT, D])
        idle = mm.sb("idle", [P, 1])
        xt_done = mm.sem("xt_done")
        sim_ready = mm.sem("sim_ready")
        sim_done = mm.sem("sim_done")
        top_done = mm.sem("top_done")
        comb_done = mm.sem("comb_done")
        best_done = mm.sem("best_done")
        rel_done = mm.sem("rel_done")
        rexp_done = mm.sem("rexp_done")
        z_done = mm.sem("z_done")
        rz_done = mm.sem("rz_done")
        diag_done = mm.sem("diag_done")
        sums_p = mm.sem("sums_by_pool")
        sums_v = mm.sem("sums_by_vector")
        soft_done = mm.sem("soft_done")
        sel_done = mm.sem("sel_done")
        head_in = mm.sem("head_in")
        wgt_done = mm.sem("wgt_done")
        out_ready = mm.sem("pk_out_ready")
        out_kept = mm.sem("pk_out_kept")
        silu_done = mm.sem("pk_silu_done")
        gated = mm.sem("pk_gated")
        res_done = mm.sem("res_done")
        stored = mm.sem("stored")
        out_v = out.rearrange("b (c p) d -> p (b c) d", p=P)

        def over_tiles(eng, steps):
            steps(None, 1, None, 0)
            steps(0, 0, None, 1)
            with eng.Fori(0, NT // 2 - 1) as i:
                for k in range(2):
                    n = i * 2 + 1 + k
                    steps(n, 1 - k, n - 1, n + 1)
            steps(NT - 1, 1, NT - 2, None)
            steps(None, 0, NT - 1, None)

        def heads(n):
            return range(PH)

        def at(n, size):
            return bass.ds(n * size, size)

        def ring_free(eng, sem, n, h):
            if not (isinstance(n, int) and n * PH + h < RING):
                eng.wait_ge(sem, n * PH + (h - RING + 1))

        with nc.Block() as block:
            @block.sync
            def _(sp):
                for k in range(NT // GROUP):
                    sp.wait_ge(res_done, k + 1)
                    rows = slice(GROUP * k, GROUP * (k + 1))
                    sp.dma_start(out_v[:, rows, :], pk[:, rows, :]).then_inc(stored, 16)
                sp.wait_ge(stored, 16 * NT // GROUP)

            @block.gpsimd
            def _(g):
                def steps(n, u, prev, nxt):
                    if n is None:
                        return
                    g.wait_ge(sim_done, n + 1)
                    for h in range(POOL_HEADS):
                        ring_free(g, sel_done, n, h)
                        g.tensor_tensor(sums[h % RING][:], bc(sim[u][:, h, :], 2, NK), bc(sim[u][:, PH + h, :], 1, NK), ALU.add).then_inc(sums_p, 1)

                over_tiles(g, steps)
                for k in range(NT // GROUP):
                    g.wait_ge(gated, k + 1)
                    rows = slice(GROUP * k, GROUP * (k + 1))
                    g.tensor_tensor(pk[:, rows, :], pk[:, rows, :], s.x[:, rows, :], ALU.add).then_inc(res_done, 1)

            @block.tensor
            def _(pe):
                def steps(n, u, prev, nxt):
                    ct = s.bank[2 + 2 * u:4 + 2 * u]
                    for h in range(PH):
                        if h == 0 and nxt is not None:
                            pe.wait_ge(xt_done, nxt + 1)
                            pe.matmul(s.bank[0][:], xt[:], s.keymat[:], start=True, stop=False)
                            pe.matmul(s.bank[0][:], s.ones[:], s.keyrow[:], start=False, stop=True).then_inc(sim_ready, 1)
                        if n is not None:
                            if h == 0:
                                pe.wait_ge(diag_done, n + 1)
                            pe.wait_ge(sel_done, n * PH + (h + 1))
                            for j in range(EB):
                                last = pe.matmul(ct[j // 4][:, P * (j % 4):P * (j % 4 + 1)], sel[h % RING][:, P * j:P * (j + 1)], diag[u][:, h, :],
                                                 start=h == 0 and j % 4 == 0, stop=h == PH - 1, skip_group_check=True)
                            last.then_inc(head_in, 1)
                        if h == 3 and prev is not None:
                            pe.wait_ge(wgt_done, prev * 2 + 2)
                            if not (isinstance(prev, int) and prev == 0):
                                pe.wait_ge(out_kept, prev)
                            for j in range(EB):
                                last = pe.matmul(s.bank[6][:, 0:D], wgt[:, j, :], s.up[:, j, :], start=j == 0, stop=j == EB - 1)
                            last.then_inc(out_ready, 1)

                over_tiles(pe, steps)

            @block.scalar
            def _(a):
                def steps(n, u, prev, nxt):
                    for h in range(PH):
                        r = h % RING
                        if n is not None:
                            if h < POOL_HEADS:
                                a.wait_ge(sums_p, n * POOL_HEADS + (h + 1))
                            else:
                                a.wait_ge(sums_v, n * VH + (h - POOL_HEADS + 1))
                            ring_free(a, sel_done, n, h)
                            a.activation(soft[r][:], sums[r][:].rearrange("p i j -> p (i j)"), ACT.Exp, bias=neg_max[u][:, h:h + 1]).then_inc(soft_done, 1)
                        if nxt is not None:
                            if h == 0:
                                a.activation(xt[:], s.xnT[:, at(nxt, P)], ACT.Copy).then_inc(xt_done, 1)
                            if h == 2:
                                a.wait_ge(sim_ready, nxt + 1)
                                a.activation(sim[1 - u][:].rearrange("p q k -> p (q k)"), s.bank[0][:], ACT.Copy).then_inc(sim_done, 1)
                            if h == 7:
                                a.wait_ge(rel_done, nxt + 1)
                                a.activation(rel[:], rel[:], ACT.Exp).then_inc(rexp_done, 1)
                        if h == 1 and n is not None:
                            a.wait_ge(rz_done, n + 1)
                            for k in range(PH):
                                last = a.activation(diag[u][:, k, :], s.ident[:], ACT.Copy, scale=rz[:, k:k + 1])
                            last.then_inc(diag_done, 1)
                        if h == 6 and prev is not None:
                            a.wait_ge(out_ready, prev + 1)
                            a.activation(pk[:, at(prev, 1), :].rearrange("p a d -> p (a d)"), s.bank[6][:, 0:D], ACT.Copy).then_inc(out_kept, 1)

                over_tiles(a, steps)
                a.wait_ge(out_kept, NT)
                for k in range(NT // GROUP):
                    rows = slice(GROUP * k, GROUP * (k + 1))
                    a.activation(pk[:, rows, :], pk[:, rows, :], ACT.Silu).then_inc(silu_done, 1)

            @block.vector
            def _(v):
                def steps(n, u, prev, nxt):
                    w = 1 - u
                    for h in range(PH):
                        r = h % RING
                        if n is not None:
                            v.wait_ge(soft_done, n * PH + (h + 1))
                            ring_free(v, head_in, n, h)
                            v.scalar_tensor_tensor(sel[r][:], sums[r][:].rearrange("p i j -> p (i j)"), best[u][:, h, PK - 1:PK], soft[r][:],
                                                   ALU.is_ge, ALU.mult).then_inc(sel_done, 1)
                            k = h + RING
                            if POOL_HEADS <= k < PH:
                                ring_free(v, sel_done, n, k)
                                v.tensor_tensor(sums[k % RING][:], bc(sim[u][:, k, :], 2, NK), bc(sim[u][:, PH + k, :], 1, NK), ALU.add).then_inc(sums_v, 1)
                        if h == 1 and prev is not None:
                            v.wait_ge(head_in, prev * PH + PH)
                            if not (isinstance(prev, int) and prev == 0):
                                v.wait_ge(out_ready, prev)
                            for k in range(2):
                                v.tensor_tensor(wgt[:, 4 * k:4 * k + 4, :], s.bank[2 + 2 * w + k][:].rearrange("p (j t) -> p j t", t=P),
                                                s.act[:, 4 * k:4 * k + 4, at(prev, P)], ALU.mult).then_inc(wgt_done, 1)
                        if nxt is not None:
                            if h == 4:
                                v.wait_ge(sim_done, nxt + 1)
                                v.memset(idle[:], 0.0)
                                for q in range(Q):
                                    ins = v.max(top[:, q, :], sim[w][:, q, :])
                                ins.then_inc(top_done, 1)
                            if h == 5:
                                v.wait_ge(top_done, nxt + 1)
                                row, col = top[:, 0:PH, :], top[:, PH:Q, :]
                                v.tensor_tensor(comb[:].rearrange("p h (a b) -> p h a b", a=PK), bc(row, 3, PK), bc(col, 2, PK), ALU.add).then_inc(comb_done, 1)
                                v.wait_ge(comb_done, nxt + 1)
                                v.memset(idle[:], 0.0)
                                for k in range(PH):
                                    ins = v.max(best[w][:, k, :], comb[:, k, :])
                                ins.then_inc(best_done, 1)
                            if h == 6:
                                v.wait_ge(best_done, nxt + 1)
                                v.tensor_scalar(neg_max[w][:], best[w][:, :, 0], -1.0, None, ALU.mult)
                                v.tensor_tensor(rel[:], best[w][:], bc(best[w][:, :, 0], 2, PK), ALU.subtract).then_inc(rel_done, 1)
                            if h == 7:
                                v.wait_ge(rexp_done, nxt + 1)
                                v.tensor_reduce(rz[:], rel[:], AX_X, ALU.add).then_inc(z_done, 1)
                                v.wait_ge(z_done, nxt + 1)
                                v.reciprocal(rz[:], rz[:]).then_inc(rz_done, 1)

                over_tiles(v, steps)
                for k in range(NT // GROUP):
                    v.wait_ge(silu_done, k + 1)
                    rows = slice(GROUP * k, GROUP * (k + 1))
                    v.tensor_tensor(pk[:, rows, :], pk[:, rows, :], s.s1[:, rows, :], ALU.mult).then_inc(gated, 1)


class Shared:
    pass


def clear(nc, semaphores):
    with nc.Block() as block:
        @block.sync
        def _(sp):
            for semaphore in semaphores:
                sp.sem_clear(semaphore)


def build(nc, io, out):
    ctx = ExitStack()
    with ctx:
        m = Memory(nc, ctx)
        s = Shared()
        s.x = m.sb("x", [P, NT, D])
        s.xn = m.sb("xn", [P, NT, D])
        s.xnT = m.sb("xnT", [P, N])
        s.ident = m.sb("ident", [P, P])
        s.bank = [m.ps(f"bank{i}", [P, W]) for i in range(8)]
        with ExitStack() as block0:
            m0 = Memory(nc, block0)
            sems = Memory(nc, block0)
            s.s0 = m0.sb("s0", [P, NT, D])
            s.g0 = m0.sb("g0", [P, NT, D])
            with ExitStack() as attn:
                m1 = Memory(nc, attn)
                s.gate = m1.sb("gate", [P, NT, H * VD])
                s.o = m1.sb("o", [P, NT, H * VD])
                with ExitStack() as scan:
                    m2 = Memory(nc, scan)
                    s.hT = m2.sb("hT", [P, N])
                    s.kqv = [m2.sb(f"kqv{j}", [P, N]) for j in range(4)]
                    s.rs = [m2.sb(f"rs{j}", [P, N]) for j in range(2)]
                    s.g = m2.sb("g", [P, NT, H])
                    s.beta = m2.sb("beta", [P, NT, H])
                    phase_norm(nc, sems, io, s)
                    phase_project(nc, sems, io, s)
                    phase_delta(nc, sems, io, s)
                phase_encode(nc, sems, io, s)
            phase_experts(nc, sems, io, s)
            phase_join(nc, sems, io, s)
            clear(nc, sems.used)
        with ExitStack() as block1:
            m1 = Memory(nc, block1)
            s.s1 = m1.sb("s1", [P, NT, D])
            with ExitStack() as attn:
                m2 = Memory(nc, attn)
                s.cos = m2.sb("cos", [P, T])
                s.sin = m2.sb("sin", [P, T])
                s.kt = m2.sb("k_tern_bf", [P, IB, N], BF16)
                s.vt = m2.sb("v_tern_bf", [P, NT, INNER], BF16)
                s.bk = m2.sb("beta_k", [P, NT, NH])
                s.la = m2.sb("log_alpha", [P, NH])
                s.lac = m2.sb("log_alpha_c", [P, IB])
                phase_ternary(nc, m, io, s)
                phase_attend(nc, m, io, s)
            m3 = Memory(nc, block1)
            s.act = m3.sb("act_t", [P, NE // P, N])
            s.up = m3.sb("up", [P, NE // P, D])
            s.keymat = m3.sb("keymat", [P, 2 * PH * NK])
            s.keyrow = m3.sb("keyrow", [1, 2 * PH * NK])
            s.ones = m3.sb("ones_r", [1, P])
            phase_keys(nc, m, io, s)
            phase_product_keys(nc, m, io, s, out)


def constants():
    f = np.float32
    i = np.arange(P)
    row, col = i[:, None], i[None, :]
    same = row // C == col // C
    levels = [(row // (2 << n) == col // (2 << n)) & ((row >> n) % 2 == 0) & ((col >> n) % 2 == 1) for n in range(LEVELS)]
    inv = (f(1) / f(10000.0) ** (np.arange(0, HD, 2, dtype=f) / f(HD))).astype(f)
    angle = (np.arange(T, dtype=f)[:, None] * inv[None, :]).astype(f)
    cos, sin = np.cos(angle).T.astype(f), np.sin(angle).T.astype(f)
    return {
        "c_ident": np.eye(P, dtype=f),
        "c_head_ones": (row // KD == col // KD).astype(f),
        "c_own": (row // KD == np.arange(H)[None, :]).astype(f),
        "c_le": ((row <= col) & same).astype(f),
        "c_gt": ((row > col) & same).astype(f),
        "c_levels": np.stack(levels, 1).astype(f),
        "c_cos": np.tile(cos, (4, 1)),
        "c_sin": np.concatenate([-sin, sin, -sin, sin]),
        "c_gap": np.maximum(col - row, 0).astype(f),
        "c_le_full": (row <= col).astype(f),
        "c_pos1": np.tile((i + 1).astype(f), (P, 1)),
        "c_rev": (P - 1 - i).astype(f)[:, None],
    }


_AS_THEY_ARE = ["L0_attn_x", "L0_attn_ln1_g", "L0_attn_ln1_b", "L0_attn_ln2_g", "L0_attn_ln2_b", "L0_attn_rms_in_w", "L0_attn_Wq",
                "L0_attn_Wk", "L0_attn_Wv", "L0_attn_conv_q_w", "L0_attn_conv_k_w", "L0_attn_conv_v_w", "L0_attn_Wa",
                "L0_attn_dt_bias", "L0_attn_A_log", "L0_attn_Wb", "L0_attn_Wg", "L0_attn_o_norm_w", "L0_attn_Wo", "L0_attn_W2",
                "L0_attn_b2", "L0_ffn_W1", "L0_ffn_W2", "L0_ffn_b2", "L0_ffn_Wr", "L0_ffn_br", "L0_ffn_gamma", "L0_ffn_beta",
                "L1_attn_bb", "L1_attn_alpha_log", "L1_ffn_w_q", "L1_ffn_up_embed"]


def laid_out(x):
    def halves_swapped(w):
        return w.T.reshape(D, NH, 2, HD // 2)[:, :, ::-1].reshape(D, INNER)

    return {
        "b1_by_feature": x["L0_ffn_b1"].reshape(E, FB, P).transpose(0, 2, 1),
        "L1_attn_WqT": x["L1_attn_Wq"].T,
        "L1_attn_WkT": x["L1_attn_Wk"].T,
        "L1_attn_WvT": x["L1_attn_Wv"].T,
        "L1_attn_WbT": x["L1_attn_Wb"].T,
        "L1_attn_WoT": x["L1_attn_Wo"].T,
        "L1_attn_WqT_swapped": halves_swapped(x["L1_attn_Wq"]),
        "L1_attn_WkT_swapped": halves_swapped(x["L1_attn_Wk"]),
        "alpha_log_by_parity": x["L1_attn_alpha_log"].reshape(IB, 2).T,
        "w_q_by_key_feature": x["L1_ffn_w_q"].T,
        "keys_by_feature": x["L1_ffn_keys"].transpose(3, 2, 0, 1).reshape(P, 2 * PH, NK),
        "bn_by_feature": np.stack([x["L1_ffn_bn_gamma"].reshape(2 * PH, P).T, x["L1_ffn_bn_beta"].reshape(2 * PH, P).T], 1),
        "down_by_feature": x["L1_ffn_down_embed"].T,
    }


def kernel(**inputs):
    import concourse.bacc as _bacc
    from concourse.bass_utils import run_bass_kernel_spmd as _run

    nc = _bacc.Bacc("TRN2", target_bir_lowering=False, num_devices=1)
    given = {k: np.asarray(v) for k, v in inputs.items()}
    arrays = {k: given[k] for k in _AS_THEY_ARE} | laid_out(given) | constants()
    io = {}
    for name in arrays:
        arrays[name] = np.ascontiguousarray(arrays[name])
        io[name] = nc.dram_tensor(name, arrays[name].shape, mybir.dt.from_np(arrays[name].dtype), kind="ExternalInput").ap()
    out = nc.dram_tensor("out", (B, T, D), F32, kind="ExternalOutput").ap()
    build(nc, io, out)
    r = _run(nc, [arrays], core_ids=[0])
    return r.results[0]["out"]
```

```python
from contextlib import ExitStack

import numpy as np
import concourse.bass as bass
from concourse import mybir

ALU = mybir.AluOpType
ACT = mybir.ActivationFunctionType
F32 = mybir.dt.float32
BF16 = mybir.dt.bfloat16
U32 = mybir.dt.uint32
AX_X = mybir.AxisListType.X

P = 128
B, T, D = 2, 1024, 128
N = B * T
NT = N // P
TB = T // P
W = 512
NW = N // W
LN_EPS = 1e-5
EPS = 1e-6
H, KD, VD, CONV = 4, 32, 64, 4
C = 64
LEVELS = 6
E, F, TOPK = 8, 512, 2
FB = F // P
NH, HD = 16, 64
INNER = NH * HD
IB = INNER // P
PH, NK = 8, 32
NE = NK * NK
PK = 8


class Link:

    def __init__(self, eng, sem, base=0):
        self.eng, self.sem, self.base, self.n = eng, sem, base, 0

    def __call__(self, ins):
        self.n += 1
        ins.then_inc(self.sem, 1)
        self.eng.wait_ge(self.sem, self.base + self.n)


class Memory:

    def __init__(self, nc, ctx, program=None):
        self.nc, self.ctx = nc, ctx
        self.program, self.used = (program.ctx, program.used) if program else (ctx, [])

    def sb(self, name, shape, dt=F32):
        return self.ctx.enter_context(self.nc.sbuf_tensor(name, shape, dt))

    def ps(self, name, shape, dt=F32):
        return self.ctx.enter_context(self.nc.psum_tensor(name, shape, dt))

    def sem(self, name):
        self.used.append(self.program.enter_context(self.nc.semaphore(name)))
        return self.used[-1]


def bc(ap, axis, n):
    v = ap.unsqueeze(axis)
    return v.broadcast_to([*v.shape[:axis], n, *v.shape[axis + 1:]])


def root(a, var_ready, n, var, std_ready):
    a.wait_ge(var_ready, n)
    a.activation(var, var, ACT.Sqrt).then_inc(std_ready, 1)


def centre(v, link, out, x, mean, centred):
    link(v.tensor_reduce(mean, x, AX_X, ALU.add))
    link(v.tensor_scalar(mean, mean, 1.0 / D, None, ALU.mult))
    v.tensor_tensor(out, x, bc(mean, 2, D), ALU.subtract).then_inc(centred, 1)


def square_sums(a, x, junk, sums, tiles, summed):
    for t in range(tiles):
        a.activation(junk[:, t, :], x[:, t, :], ACT.Square, accum_out=sums[:, t:t + 1]).then_inc(summed, 1)


def scale_by_root(v, link, x, var, std_ready, n, done, gb=None):
    v.wait_ge(std_ready, n)
    link(v.reciprocal(var, var))
    ops = [(ALU.mult, bc(var, 2, D))]
    if gb is not None:
        ops += [(ALU.mult, bc(gb[0], 1, x.shape[1])), (ALU.add, bc(gb[1], 1, x.shape[1]))]
    for k, (op, y) in enumerate(ops):
        ins = v.tensor_tensor(x, x, y, op)
        if k < len(ops) - 1:
            link(ins)
    ins.then_inc(done, 1)


def phase_norm(nc, m, io, s):
    ctx = ExitStack()
    with ctx:
        mm = Memory(nc, ctx, m)
        g1 = mm.sb("ln1_g", [P, D])
        b1 = mm.sb("ln1_b", [P, D])
        rw = mm.sb("rms_w", [P, 1])
        hid = mm.sb("hid", [P, NT, D])
        tmp = mm.sb("sq_tmp", [P, NT, D])
        stat = mm.sb("stat", [P, 3, 2, NT])
        x_in = [mm.sem(f"x_in{b}") for b in range(B)]
        ln_in = mm.sem("ln_in")
        next_in = mm.sem("project_w_in")
        chain = mm.sem("norm_chain")
        centred = mm.sem("centred")
        ln_done = mm.sem("ln_done")
        sq_done = mm.sem("sq_done")
        var_ready = mm.sem("var_ready")
        std_ready = mm.sem("std_ready")
        xn_ready = mm.sem("xn_ready")
        h_ready = mm.sem("h_ready")
        turned = mm.sem("turned")
        copied = mm.sem("copied")
        halves = [slice(TB * b, TB * (b + 1)) for b in range(B)]
        with nc.Block() as block:
            @block.sync
            def _(sp):
                for b in range(B):
                    sp.dma_start(s.x[:, halves[b], :], io["L0_attn_x"][b].rearrange("(c p) d -> p c d", p=P)).then_inc(x_in[b], 16)
                sp.dma_start(s.ident[:], io["c_ident"]).then_inc(ln_in, 16)
                sp.dma_start(g1[:], io["L0_attn_ln1_g"].partition_broadcast(P)).then_inc(ln_in, 16)
                sp.dma_start(b1[:], io["L0_attn_ln1_b"].partition_broadcast(P)).then_inc(ln_in, 16)
                sp.dma_start(rw[:], io["L0_attn_rms_in_w"].rearrange("(d a) -> d a", a=1)).then_inc(ln_in, 16)
                sp.dma_start(s.kqv_w[:, 0:P], io["L0_attn_Wk"]).then_inc(next_in, 16)
                sp.dma_start(s.kqv_w[:, P:2 * P], io["L0_attn_Wq"]).then_inc(next_in, 16)
                sp.dma_start(s.kqv_w[:, 2 * P:4 * P], io["L0_attn_Wv"]).then_inc(next_in, 16)
                sp.dma_start(s.conv_w[:, 0, :], io["L0_attn_conv_k_w"]).then_inc(next_in, 16)
                sp.dma_start(s.conv_w[:, 1, :], io["L0_attn_conv_q_w"]).then_inc(next_in, 16)
                sp.dma_start(s.conv_w[:, 2:4, :], io["L0_attn_conv_v_w"].rearrange("(j p) i -> p j i", p=P)).then_inc(next_in, 16)
                sp.wait_ge(next_in, 96)

            @block.vector
            def _(v):
                link = Link(v, chain)

                def variance(k, b, eps):
                    var = stat[:, k, 1, halves[b]]
                    v.wait_ge(sq_done, TB * (B * k + b + 1))
                    v.tensor_scalar(var, var, 1.0 / D, eps, ALU.mult, ALU.add).then_inc(var_ready, 1)
                    return var

                for b in range(B):
                    v.wait_ge(x_in[b], 16)
                    centre(v, link, s.xn[:, halves[b], :], s.x[:, halves[b], :], stat[:, 0, 0, halves[b]], centred)
                for b in range(B):
                    var = variance(0, b, LN_EPS)
                    scale_by_root(v, link, s.xn[:, halves[b], :], var, std_ready, b + 1, xn_ready)
                    v.wait_ge(xn_ready, b + 1)
                    centre(v, link, hid[:, halves[b], :], s.xn[:, halves[b], :], stat[:, 1, 0, halves[b]], centred)
                v.wait_ge(ln_in, 64)
                for b in range(B):
                    var = variance(1, b, LN_EPS)
                    scale_by_root(v, link, hid[:, halves[b], :], var, std_ready, B + b + 1, ln_done, (g1[:], b1[:]))
                for b in range(B):
                    var = variance(2, b, EPS)
                    scale_by_root(v, link, hid[:, halves[b], :], var, std_ready, 2 * B + b + 1, h_ready)

            @block.tensor
            def _(pe):
                pe.wait_ge(ln_in, 64)
                for k, (src, ready) in enumerate(((s.xn, xn_ready), (hid, h_ready))):
                    for t in range(NT):
                        pe.wait_ge(ready, t // TB + 1)
                        last = pe.transpose(s.bank[4 * k + t // 4][:, P * (t % 4):P * (t % 4 + 1)], src[:, t, :], s.ident[:])
                        if t % 4 == 3:
                            last.then_inc(turned, 1)

            @block.scalar
            def _(a):
                for k in range(3):
                    for b in range(B):
                        if k < 2:
                            a.wait_ge(centred, B * k + b + 1)
                        else:
                            a.wait_ge(ln_done, b + 1)
                        square_sums(a, (s.xn if k == 0 else hid)[:, halves[b], :], tmp[:, halves[b], :], stat[:, k, 1, halves[b]], TB, sq_done)
                        root(a, var_ready, B * k + b + 1, stat[:, k, 1, halves[b]], std_ready)
                for w in range(NW):
                    a.wait_ge(turned, w + 1)
                    a.activation(s.xnT[:, W * w:W * (w + 1)], s.bank[w][:], ACT.Copy).then_inc(copied, 1)
                for w in range(NW):
                    a.wait_ge(turned, NW + w + 1)
                    a.activation(s.hT[:, W * w:W * (w + 1)], s.bank[4 + w][:], ACT.Copy, scale=rw[:]).then_inc(copied, 1)


def phase_project(nc, m, io, s):
    ctx = ExitStack()
    with ctx:
        mm = Memory(nc, ctx, m)
        w, cw = s.kqv_w, s.conv_w
        gw = mm.sb("gate_w", [P, H * VD + 2 * H])
        group = mm.sb("head_ones", [P, P])
        padded = [mm.sb(f"padded{j}", [P, B, CONV - 1 + T]) for j in range(4)]
        dtb = mm.sb("dt_bias", [P, H])
        alog = mm.sb("a_log", [P, H])
        ab = mm.sb("ab", [P, NT, 2 * H])
        az = mm.sb("az", [P, NT, 2 * H])
        ez = mm.sb("ez", [P, NT, 2 * H])
        lp = mm.sb("log1p", [P, NT, 2 * H])
        eps = mm.sb("eps", [P, 2])
        next_in = mm.sem("delta_in")
        small_in = mm.sem("small_in")
        pads = mm.sem("pads")
        chain = mm.sem("conv_chain")
        achain = mm.sem("act_chain")
        projected = mm.sem("projected")
        evacuated = mm.sem("evacuated")
        conved = mm.sem("conved")
        silued = mm.sem("silued")
        gated = mm.sem("gated")
        gate_out = mm.sem("gate_out")
        ab_out = mm.sem("ab_out")
        squared = mm.sem("squared")
        summed = mm.sem("summed")
        z_ready = mm.sem("z_ready")
        e_ready = mm.sem("e_ready")
        with nc.Block() as block:
            @block.sync
            def _(sp):
                sp.dma_start(gw[:, 0:H * VD], io["L0_attn_Wg"]).then_inc(small_in, 16)
                sp.dma_start(gw[:, H * VD:H * VD + H], io["L0_attn_Wa"]).then_inc(small_in, 16)
                sp.dma_start(gw[:, H * VD + H:], io["L0_attn_Wb"]).then_inc(small_in, 16)
                sp.dma_start(dtb[:], io["L0_attn_dt_bias"].partition_broadcast(P)).then_inc(small_in, 16)
                sp.dma_start(alog[:], io["L0_attn_A_log"].partition_broadcast(P)).then_inc(small_in, 16)
                sp.dma_start(group[:], io["c_head_ones"]).then_inc(small_in, 16)
                sp.dma_start(s.le[:], io["c_le"]).then_inc(next_in, 16)
                sp.dma_start(s.gt[:], io["c_gt"]).then_inc(next_in, 16)
                sp.dma_start(s.levels[:], io["c_levels"]).then_inc(next_in, 16)
                sp.dma_start(s.own[:], io["c_own"]).then_inc(next_in, 16)
                sp.wait_ge(next_in, 64)

            @block.tensor
            def _(pe):
                for j in range(4):
                    for c in range(NW):
                        if j >= 2:
                            pe.wait_ge(evacuated, NW * (j - 2) + c + 1)
                        pe.matmul(s.bank[4 * (j % 2) + c][:], w[:, P * j:P * (j + 1)], s.hT[:, W * c:W * (c + 1)],
                                  start=True, stop=True).then_inc(projected, 1)
                pe.wait_ge(small_in, 96)
                for t in range(NT):
                    pe.wait_ge(evacuated, NW * 2 + t + 1 if t < 8 else NW * 4)
                    if t >= 8:
                        pe.wait_ge(gate_out, t - 7)
                        pe.wait_ge(ab_out, t - 7)
                    pe.matmul(s.bank[t % 8][:, 0:H * VD + 2 * H], s.hT[:, P * t:P * (t + 1)], gw[:],
                              start=True, stop=True).then_inc(gated, 1)
                for j in range(2):
                    pe.wait_ge(squared, j + 1)
                    for c in range(NW):
                        pe.wait_ge(gate_out, 8 + 4 * j + c + 1)
                        pe.wait_ge(ab_out, 8 + 4 * j + c + 1)
                        pe.matmul(s.bank[4 * j + c][:], group[:], s.rs[j][:, W * c:W * (c + 1)],
                                  start=True, stop=True).then_inc(summed, 1)

            @block.vector
            def _(v):
                link = Link(v, chain)
                for j in range(4):
                    v.memset(padded[j][:, :, 0:CONV - 1], 0.0).then_inc(pads, 1)
                v.memset(eps[:, 0:1], EPS).then_inc(pads, 1)
                v.memset(eps[:, 1:2], KD * EPS).then_inc(pads, 1)
                v.wait_ge(pads, 6)
                for j in range(4):
                    v.wait_ge(evacuated, NW * (j + 1))
                    y = s.kqv[j][:].rearrange("p (b t) -> p b t", b=B)
                    link(v.tensor_scalar(y, padded[j][:, :, 0:T], cw[:, j, 0:1], None, ALU.mult))
                    for i in range(1, CONV):
                        link(v.scalar_tensor_tensor(y, padded[j][:, :, i:i + T], cw[:, j, i:i + 1], y, ALU.mult, ALU.add))
                    v.engine_nop().then_inc(conved, 1)
                v.wait_ge(ab_out, NT)
                za, zb = ab[:, :, 0:H], ab[:, :, H:2 * H]
                link(v.tensor_tensor(za, za, bc(dtb[:], 1, NT), ALU.add))
                link(v.tensor_scalar(az[:, :, 0:H], za, -1.0, None, ALU.mult))
                link(v.tensor_tensor(az[:, :, 0:H], az[:, :, 0:H], za, ALU.max))
                v.tensor_scalar(az[:, :, H:2 * H], zb, -87.0, None, ALU.max).then_inc(z_ready, 1)
                e, u, d, is0 = ez[:, :, 0:H], az[:, :, 0:H], az[:, :, H:2 * H], lp[:, :, 0:H]
                v.wait_ge(e_ready, 1)
                v.tensor_scalar(u, e, 1.0, None, ALU.add).then_inc(z_ready, 1)
                v.wait_ge(z_ready, 2)
                link(v.tensor_scalar(d, u, -1.0, None, ALU.add))
                link(v.tensor_scalar(is0, d, 0.0, None, ALU.is_equal))
                link(v.tensor_tensor(d, d, is0, ALU.add))
                link(v.reciprocal(d, d))
                link(v.tensor_tensor(d, d, e, ALU.mult))
                v.wait_ge(e_ready, 2)
                link(v.tensor_tensor(is0, lp[:, :, H:2 * H], is0, ALU.add))
                link(v.tensor_tensor(d, d, is0, ALU.mult))
                link(v.tensor_scalar(za, za, 0.0, None, ALU.max))
                link(v.tensor_tensor(za, za, d, ALU.add))
                link(v.tensor_tensor(za, za, bc(alog[:], 1, NT), ALU.mult))
                v.tensor_scalar(s.g[:], za, -1.0, -104.0, ALU.mult, ALU.max).then_inc(z_ready, 1)
                link(v.tensor_scalar(ez[:, :, H:2 * H], ez[:, :, H:2 * H], 1.0, None, ALU.add))
                link(v.reciprocal(s.beta[:], ez[:, :, H:2 * H]))

            @block.scalar
            def _(a):
                link = Link(a, achain)
                def evacuate(j):
                    for c in range(NW):
                        a.wait_ge(projected, NW * j + c + 1)
                        a.activation(padded[j][:, c // 2, CONV - 1 + W * (c % 2):CONV - 1 + W * (c % 2 + 1)],
                                     s.bank[4 * (j % 2) + c][:], ACT.Copy).then_inc(evacuated, 1)

                def silu(j):
                    a.wait_ge(conved, j + 1)
                    a.activation(s.kqv[j][:], s.kqv[j][:], ACT.Silu).then_inc(silued, 1)

                for j in range(4):
                    evacuate(j)
                for t in range(NT):
                    a.wait_ge(gated, t + 1)
                    a.activation(s.gate[:, t, :], s.bank[t % 8][:, 0:H * VD], ACT.Silu).then_inc(gate_out, 1)
                    a.activation(ab[:, t, :], s.bank[t % 8][:, H * VD:H * VD + 2 * H], ACT.Copy).then_inc(ab_out, 1)
                for j in range(4):
                    silu(j)
                for j in range(2):
                    a.wait_ge(silued, j + 1)
                    a.activation(s.rs[j][:], s.kqv[j][:], ACT.Square).then_inc(squared, 1)
                a.wait_ge(small_in, 96)
                link(a.activation(alog[:], alog[:], ACT.Exp))
                a.wait_ge(z_ready, 1)
                a.activation(ez[:], az[:], ACT.Exp, scale=-1.0).then_inc(e_ready, 1)
                a.wait_ge(z_ready, 2)
                a.activation(lp[:, :, H:2 * H], az[:, :, 0:H], ACT.Ln).then_inc(e_ready, 1)
                for j in range(2):
                    for c in range(NW):
                        a.wait_ge(summed, NW * j + c + 1)
                        link(a.activation(s.rs[j][:, W * c:W * (c + 1)], s.bank[4 * j + c][:], ACT.Ln,
                                          bias=eps[:, j:j + 1], scale=float(KD if j else 1)))
                for j in range(2):
                    a.activation(s.rs[j][:], s.rs[j][:], ACT.Exp, scale=-0.5)


def phase_delta(nc, m, io, s):
    LINKS_V = 2 * (2 + 1 + P // C)
    ctx = ExitStack()
    with ctx:
        mm = Memory(nc, ctx, m)
        le, gt, lvl, own = s.le, s.gt, s.levels, s.own

        def pair(name, shape):
            return [mm.sb(f"{name}{b}", shape) for b in range(B)]

        kt = pair("kt", [P, P])
        qt = pair("qt", [P, P])
        kbd = pair("kbd", [P, H, P])
        qbd = pair("qbd", [P, H, P])
        vt = pair("vt", [P, 2, P])
        gm = pair("gm", [P, H, P])
        gch = pair("gch", [P, H, KD])
        bmask = pair("bmask", [P, H, P])
        dmb = pair("dmb", [P, H, P])
        expd = pair("expd", [P, P + 2 * H])
        eb = pair("eb", [P, H])
        at = pair("at", [P, H, P])
        pt = pair("pt", [P, H, P])
        qg = pair("qg", [P, P])
        tok = pair("tok", [P, 3 * P])
        kend = pair("kend", [P, P])
        kg = pair("kg", [P, P])
        off = [pair(f"off{l}_", [P, H, P]) for l in range(2)]
        idle = mm.sb("delta_idle", [P, B])
        xx = pair("xx", [P, H, P])
        tt = pair("tt", [P, H, P])
        rr = pair("rr", [P, H, P])
        wt = pair("wt", [P, P])
        uu = pair("uu", [P, H * VD])
        yy = pair("yy", [P, H * VD])
        st = pair("st", [P, H, VD])
        sown = pair("sown", [P, H, VD])

        def sems(name):
            return [mm.sem(f"{name}{b}") for b in range(B)]

        chain = mm.sem("delta_chain")
        staged = sems("staged")
        v_staged = sems("v_staged")
        spread = sems("spread")
        bmask_done = sems("bmask_done")
        masks_g = sems("masks_g")
        decays = sems("decays")
        products = sems("products")
        expd_done = sems("expd_done")
        at_done = sems("at_done")
        turned = sems("turned")
        tok_done = sems("tok_done")
        kscaled = sems("kscaled")
        x_done = sems("x_done")
        t_turned = sems("t_turned")
        t_done = sems("t_done")
        off_done = sems("off_done")
        r_ready = sems("r_ready")
        r_done = sems("r_done")
        dx_ready = sems("dx_ready")
        x_turned = sems("x_turned")
        x_copied = sems("x_copied")
        wu_ready = sems("wu_ready")
        wu_done = sems("wu_done")
        z_ready = sems("z_ready")
        y_done = sems("y_done")
        s_ready = sems("s_ready")
        o_ready = sems("o_ready")
        s_done = sems("s_done")
        o_done = sems("o_done")
        L1 = LEVELS - 1
        NC = P // C

        def over_turns(eng, turn):
            with eng.Fori(0, TB - 1) as i:
                turn(i, True)
            turn(TB - 1, False)

        def tokens(i, b):
            return bass.ds(i * P + b * T, P)

        with nc.Block() as block:
            @block.gpsimd
            def _(g):

                def spread_heads(i):
                    for b in range(B):
                        for k, (flat, wide) in enumerate(((kt, kbd), (qt, qbd))):
                            g.wait_ge(staged[b], 2 * i + (k + 1))
                            g.tensor_tensor(wide[b][:], bc(flat[b][:], 1, H), bc(own[:], 2, P), ALU.mult).then_inc(spread[b], 1)
                    for b in range(B):
                        bi = s.beta[:, bass.ds(i + b * TB, 1), :].rearrange("p a h -> p (a h)")
                        g.tensor_tensor(bmask[b][:], bc(le[:], 1, H), bc(bi, 2, P), ALU.mult).then_inc(bmask_done[b], 1)

                def turn(i, more):
                    for l in range(1, LEVELS):
                        for b in range(B):
                            if l == 1:
                                g.wait_ge(at_done[b], 2 * i + 1)
                            if l > 2:
                                g.wait_ge(r_ready[b], i * L1 + (l - 2))
                            g.tensor_tensor(off[l % 2][b][:], at[b][:], bc(lvl[:, l, :], 1, H), ALU.mult).then_inc(off_done[b], 1)
                    if more:
                        spread_heads(i + 1)

                spread_heads(0)
                over_turns(g, turn)

            @block.vector
            def _(v):
                for b in range(B):
                    v.memset(st[b][:], 0.0).then_inc(s_done[b], 1)
                    v.memset(idle[:, b:b + 1], 0.0).then_inc(o_done[b], 1)
                for b in range(B):
                    v.wait_ge(s_done[b], 1)

                def stage(i, b):
                    cols = tokens(i, b)
                    v.tensor_tensor(kt[b][:], s.kqv[0][:, cols], s.rs[0][:, cols], ALU.mult).then_inc(staged[b], 1)
                    v.tensor_tensor(qt[b][:], s.kqv[1][:, cols], s.rs[1][:, cols], ALU.mult).then_inc(staged[b], 1)
                    gi = s.g[:, bass.ds(i + b * TB, 1), :].rearrange("p a h -> p (a h)")
                    v.tensor_tensor(gm[b][:], bc(gt[:], 1, H), bc(gi, 2, P), ALU.mult).then_inc(masks_g[b], 1)
                    v.tensor_copy(gch[b][:], bc(gi, 2, KD)).then_inc(masks_g[b], 1)

                def turn(i, more):
                    link = Link(v, chain, i * LINKS_V)
                    for b in range(B):
                        bi = s.beta[:, bass.ds(i + b * TB, 1), :].rearrange("p a h -> p (a h)")
                        v.wait_ge(expd_done[b], 2 * i + 2)
                        v.wait_ge(bmask_done[b], i + 1)
                        link(v.tensor_tensor(dmb[b][:], dmb[b][:], bmask[b][:], ALU.mult))
                        link(v.tensor_tensor(eb[b][:], expd[b][:, P + H:], bi, ALU.mult))
                    for b in range(B):
                        v.wait_ge(products[b], 2 * i + 1)
                        v.tensor_tensor(at[b][:], s.bank[4 * b + 2][:].rearrange("p (h t) -> p h t", h=H), dmb[b][:],
                                        ALU.mult).then_inc(at_done[b], 1)
                        v.wait_ge(at_done[b], 2 * i + 1)
                        link(v.tensor_tensor(tt[b][:], at[b][:], bc(lvl[:, 0, :], 1, H), ALU.mult))
                        v.tensor_tensor(xx[b][:], bc(s.ident[:], 1, H), tt[b][:], ALU.subtract).then_inc(x_done[b], 1)
                    for b in range(B):
                        v.wait_ge(products[b], 2 * i + 2)
                        v.tensor_tensor(pt[b][:], s.bank[4 * b + 3][:].rearrange("p (h t) -> p h t", h=H), dmb[b][:],
                                        ALU.mult).then_inc(at_done[b], 1)
                    for b in range(B):
                        v.wait_ge(tok_done[b], i + 1)
                        kk = tok[b][:, 0:P].rearrange("p (h c) -> p h c", h=H)
                        v.tensor_tensor(kend[b][:].rearrange("p (h c) -> p h c", h=H), kk, bc(eb[b][:], 2, KD),
                                        ALU.mult).then_inc(kscaled[b], 1)
                        v.tensor_tensor(kg[b][:].rearrange("p (h c) -> p h c", h=H), kk, bc(expd[b][:, P:P + H], 2, KD),
                                        ALU.mult).then_inc(kscaled[b], 1)
                        v.tensor_tensor(qg[b][:], qt[b][:], expd[b][:, 0:P], ALU.mult).then_inc(kscaled[b], 1)
                    for l in range(1, LEVELS):
                        for b in range(B):
                            v.wait_ge(dx_ready[b], i * L1 + l)
                            x = (tt if l < L1 else xx)[b][:].rearrange("p h t -> p (h t)")
                            v.tensor_tensor(x, x, s.bank[4 * b + (0 if l < L1 else 3)][:], ALU.subtract).then_inc(x_done[b], 1)
                        if more and l <= B:
                            v.wait_ge(kscaled[l - 1], 3 * i + 3)
                            stage(i + 1, l - 1)
                    for c in range(NC):
                        rows = slice(C * c, C * (c + 1))
                        for b in range(B):
                            v.wait_ge(wu_done[b], 2 * i + 2)
                            v.wait_ge(z_ready[b], i * NC + c + 1)
                            v.tensor_tensor(yy[b][rows, :], uu[b][rows, :], s.bank[4 * b + 3][rows, 0:H * VD],
                                            ALU.subtract).then_inc(y_done[b], 1)
                        for b in range(B):
                            last = C * (c + 1) - 1
                            v.wait_ge(s_ready[b], i * NC + c + 1)
                            link(v.tensor_tensor(sown[b][:], s.bank[4 * b + 1][:, 0:H * VD].rearrange("p (h v) -> p h v", h=H),
                                                 bc(own[:], 2, VD), ALU.mult))
                            v.scalar_tensor_tensor(st[b][:], st[b][:], expd[b][:, last:last + 1], sown[b][:],
                                                   ALU.mult, ALU.add).then_inc(s_done[b], 1)
                    assert link.n == LINKS_V, link.n

                for b in range(B):
                    stage(0, b)
                over_turns(v, turn)

            @block.scalar
            def _(a):
                def stage(i):
                    for b in range(B):
                        for j in range(2):
                            a.activation(vt[b][:, j, :], s.kqv[2 + j][:, tokens(i, b)], ACT.Copy).then_inc(v_staged[b], 1)

                def turn(i, more):
                    for b in range(B):
                        a.wait_ge(decays[b], i + 1)
                        a.activation(dmb[b][:].rearrange("p h t -> p (h t)"), s.bank[4 * b][:], ACT.Exp).then_inc(expd_done[b], 1)
                        a.activation(expd[b][:], s.bank[4 * b + 1][:, 0:P + 2 * H], ACT.Exp).then_inc(expd_done[b], 1)
                    for b in range(B):
                        a.wait_ge(turned[b], i + 1)
                        a.activation(tok[b][:], s.bank[4 * b + 1][:, 0:3 * P], ACT.Copy).then_inc(tok_done[b], 1)
                    for b in range(B):
                        a.wait_ge(t_turned[b], i + 1)
                        a.activation(tt[b][:].rearrange("p h t -> p (h t)"), s.bank[4 * b][:], ACT.Copy).then_inc(t_done[b], 1)
                    for l in range(1, LEVELS):
                        for b in range(B):
                            a.wait_ge(r_ready[b], i * L1 + l)
                            a.activation(rr[b][:].rearrange("p h t -> p (h t)"), s.bank[4 * b + 2][:], ACT.Copy).then_inc(r_done[b], 1)
                            if l > 1:
                                a.wait_ge(x_turned[b], i * (L1 - 1) + (l - 1))
                                a.activation(xx[b][:].rearrange("p h t -> p (h t)"), s.bank[4 * b + 3][:], ACT.Copy).then_inc(x_copied[b], 1)
                        if more and l == 2:
                            stage(i + 1)
                    for b in range(B):
                        a.wait_ge(wu_ready[b], i + 1)
                        a.activation(wt[b][:], s.bank[4 * b + 1][:, 0:P], ACT.Copy).then_inc(wu_done[b], 1)
                        a.activation(uu[b][:], s.bank[4 * b + 2][:, 0:H * VD], ACT.Copy).then_inc(wu_done[b], 1)
                    for b in range(B):
                        a.wait_ge(o_ready[b], (i + 1) * NC)
                        a.activation(s.o[:, bass.ds(i + b * TB, 1), :].rearrange("p a c -> p (a c)"), s.bank[4 * b][:, 0:H * VD],
                                     ACT.Copy).then_inc(o_done[b], 1)

                stage(0)
                over_turns(a, turn)

            @block.tensor
            def _(pe):

                def turn(i, more):
                    for b in range(B):
                        p0, p1 = s.bank[4 * b:4 * b + 2]
                        pe.wait_ge(o_done[b], i + 1)
                        pe.wait_ge(s_done[b], i * NC + 1)
                        pe.wait_ge(masks_g[b], 2 * i + 2)
                        gi = s.g[:, bass.ds(i + b * TB, 1), :].rearrange("p a h -> p (a h)")
                        for h in range(H):
                            pe.matmul(p0[:, P * h:P * (h + 1)], gm[b][:, h, :], le[:], start=True, stop=True)
                        pe.matmul(p1[:, 0:P], gch[b][:].rearrange("p h c -> p (h c)"), le[:], start=True, stop=True)
                        pe.matmul(p1[:, P:P + H], le[:], gi, start=True, stop=True)
                        pe.matmul(p1[:, P + H:P + 2 * H], gt[:], gi, start=True, stop=True).then_inc(decays[b], 1)
                    for k, wide in enumerate((kbd, qbd)):
                        for b in range(B):
                            pe.wait_ge(spread[b], 2 * i + (k + 1))
                            pe.matmul(s.bank[4 * b + 2 + k][:], kt[b][:], wide[b][:].rearrange("p h t -> p (h t)"), start=True,
                                      stop=True).then_inc(products[b], 1)
                    for b in range(B):
                        p1 = s.bank[4 * b + 1]
                        pe.wait_ge(expd_done[b], 2 * i + 2)
                        pe.wait_ge(v_staged[b], 2 * i + 2)
                        pe.transpose(p1[:, 0:P], kt[b][:], s.ident[:])
                        pe.transpose(p1[:, P:2 * P], vt[b][:, 0, :], s.ident[:])
                        pe.transpose(p1[:, 2 * P:3 * P], vt[b][:, 1, :], s.ident[:]).then_inc(turned[b], 1)
                    for b in range(B):
                        pe.wait_ge(x_done[b], i * LEVELS + 1)
                        for h in range(H):
                            last = pe.transpose(s.bank[4 * b][:, P * h:P * (h + 1)], xx[b][:, h, :], s.ident[:])
                        last.then_inc(t_turned[b], 1)
                    for l in range(1, LEVELS):
                        for b in range(B):
                            if l == 1:
                                pe.wait_ge(t_done[b], i + 1)
                                pe.wait_ge(at_done[b], 2 * i + 1)
                            if l == 2:
                                pe.wait_ge(at_done[b], 2 * i + 2)
                            pe.wait_ge(x_done[b], i * LEVELS + l)
                            pe.wait_ge(off_done[b], i * L1 + l)
                            for h in range(H):
                                last = pe.matmul(s.bank[4 * b + 2][:, P * h:P * (h + 1)], off[l % 2][b][:, h, :], tt[b][:, h, :],
                                                 start=True, stop=True)
                            last.then_inc(r_ready[b], 1)
                            if l > 1:
                                for h in range(H):
                                    last = pe.transpose(s.bank[4 * b + 3][:, P * h:P * (h + 1)], tt[b][:, h, :], s.ident[:])
                                last.then_inc(x_turned[b], 1)
                        for b in range(B):
                            pe.wait_ge(r_done[b], i * L1 + l)
                            if l > 1:
                                pe.wait_ge(x_copied[b], i * (L1 - 1) + (l - 1))
                            for h in range(H):
                                if l < L1:
                                    last = pe.matmul(s.bank[4 * b][:, P * h:P * (h + 1)], xx[b][:, h, :], rr[b][:, h, :], start=True, stop=True)
                                else:
                                    last = pe.matmul(s.bank[4 * b + 3][:, P * h:P * (h + 1)], rr[b][:, h, :], xx[b][:, h, :], start=True, stop=True)
                            last.then_inc(dx_ready[b], 1)
                    for b in range(B):
                        pe.wait_ge(x_done[b], (i + 1) * LEVELS)
                        pe.wait_ge(kscaled[b], 3 * i + 3)
                        pe.wait_ge(tok_done[b], i + 1)
                        for h in range(H):
                            pe.matmul(s.bank[4 * b + 1][KD * h:KD * (h + 1), 0:P], kg[b][:, KD * h:KD * (h + 1)], xx[b][:, h, :],
                                      start=True, stop=True)
                        for h in range(H):
                            last = pe.matmul(s.bank[4 * b + 2][:, VD * h:VD * (h + 1)], xx[b][:, h, :],
                                             tok[b][:, P + VD * h:P + VD * (h + 1)], start=True, stop=True)
                        last.then_inc(wu_ready[b], 1)
                    for c in range(NC):
                        cols = slice(C * c, C * (c + 1))
                        for b in range(B):
                            p0, p1, p2, p3 = s.bank[4 * b:4 * b + 4]
                            pe.wait_ge(wu_done[b], 2 * i + 2)
                            pe.wait_ge(s_done[b], i * NC + (c + 1))
                            state = st[b][:].rearrange("p h v -> p (h v)")
                            pe.matmul(p3[cols, 0:H * VD], wt[b][:, cols], state, start=True, stop=True).then_inc(z_ready[b], 1)
                            pe.matmul(p0[cols, 0:H * VD], qg[b][:, cols], state, start=True, stop=False, skip_group_check=True)
                        for b in range(B):
                            p0, p1, p2, p3 = s.bank[4 * b:4 * b + 4]
                            pe.wait_ge(y_done[b], i * NC + c + 1)
                            pe.matmul(p1[:, 0:H * VD], kend[b][cols, :], yy[b][cols, :], start=True, stop=True).then_inc(s_ready[b], 1)
                            for h in range(H):
                                last = pe.matmul(p0[cols, VD * h:VD * (h + 1)], pt[b][cols, h, cols], yy[b][cols, VD * h:VD * (h + 1)],
                                                 start=False, stop=h == H - 1, skip_group_check=True)
                            last.then_inc(o_ready[b], 1)

                over_turns(pe, turn)


def phase_encode(nc, m, io, s):
    ctx = ExitStack()
    with ctx:
        mm = Memory(nc, ctx, m)
        nw = mm.sb("o_norm_w", [P, VD])
        wo = mm.sb("wo", [P, 2, D])
        w2 = mm.sb("w2", [P, D])
        b2 = mm.sb("b2", [1, D])
        ones = mm.sb("ones", [1, P])
        g2 = mm.sb("ln2_g", [P, D])
        bb2 = mm.sb("ln2_b", [P, D])
        osq = mm.sb("osq", [P, NT * H, VD])
        ost = mm.sb("ost", [P, NT * H])
        oT = mm.sb("oT", [P, 2, N])
        xe = mm.sb("xe", [P, NT, D])
        h2 = mm.sb("h2", [P, NT, D])
        h2T = mm.sb("h2T", [P, N])
        stat = mm.sb("enc_stat", [P, 2, NT])
        w_in = mm.sem("enc_w_in")
        chain = mm.sem("enc_chain")
        squared = mm.sem("o_squared")
        centred = mm.sem("h2_centred")
        h2_squared = mm.sem("h2_squared")
        gate_done = mm.sem("gate_done")
        var_ready = mm.sem("enc_var")
        std_ready = mm.sem("enc_std")
        o_ready = mm.sem("o_ready")
        turned = mm.sem("enc_turned")
        copied = mm.sem("enc_copied")
        encoded = mm.sem("encoded")
        xe_done = mm.sem("xe_done")
        h2_ready = mm.sem("h2_ready")
        h2_out = mm.sem("h2_out")
        gelued = mm.sem("gelued")
        ov = s.o[:].rearrange("p t (h v) -> p (t h) v", v=VD)
        HW = NW // B
        halves = [slice(TB * b, TB * (b + 1)) for b in range(B)]
        heads = [slice(TB * H * b, TB * H * (b + 1)) for b in range(B)]
        with nc.Block() as block:
            @block.sync
            def _(sp):
                sp.dma_start(nw[:], io["L0_attn_o_norm_w"].partition_broadcast(P)).then_inc(w_in, 16)
                sp.dma_start(wo[:], io["L0_attn_Wo"].rearrange("(j p) d -> p j d", p=P)).then_inc(w_in, 16)
                sp.dma_start(w2[:], io["L0_attn_W2"]).then_inc(w_in, 16)
                sp.dma_start(b2[:], io["L0_attn_b2"].rearrange("(a d) -> a d", a=1)).then_inc(w_in, 16)
                sp.dma_start(g2[:], io["L0_attn_ln2_g"].partition_broadcast(P)).then_inc(w_in, 16)
                sp.dma_start(bb2[:], io["L0_attn_ln2_b"].partition_broadcast(P)).then_inc(w_in, 16)

            @block.gpsimd
            def _(g):
                g.memset(ones[:], 1.0).then_inc(gate_done, 1)
                g.wait_ge(w_in, 96)
                for b in range(B):
                    gv = s.gate[:, halves[b], :].rearrange("p t (h v) -> p (t h) v", v=VD)
                    g.tensor_tensor(gv, gv, bc(nw[:], 1, TB * H), ALU.mult).then_inc(gate_done, 1)

            @block.vector
            def _(v):
                link = Link(v, chain)
                v.wait_ge(w_in, 96)
                for b in range(B):
                    v.wait_ge(squared, b + 1)
                    link(v.tensor_reduce(ost[:, heads[b]], osq[:, heads[b], :], AX_X, ALU.add))
                    v.tensor_scalar(ost[:, heads[b]], ost[:, heads[b]], 1.0 / VD, EPS, ALU.mult, ALU.add).then_inc(var_ready, 1)
                for b in range(B):
                    v.wait_ge(std_ready, b + 1)
                    link(v.reciprocal(ost[:, heads[b]], ost[:, heads[b]]))
                    link(v.tensor_tensor(ov[:, heads[b], :], ov[:, heads[b], :], bc(ost[:, heads[b]], 2, VD), ALU.mult))
                    v.wait_ge(gate_done, b + 2)
                    v.tensor_tensor(s.o[:, halves[b], :], s.o[:, halves[b], :], s.gate[:, halves[b], :], ALU.mult).then_inc(o_ready, 1)
                for b in range(B):
                    for w in range(HW * b, HW * (b + 1)):
                        v.wait_ge(encoded, w + 1)
                        v.tensor_tensor(xe[:, 4 * w:4 * w + 4, :], s.xn[:, 4 * w:4 * w + 4, :],
                                        s.bank[w][:].rearrange("p (t d) -> p t d", d=D), ALU.add).then_inc(xe_done, 1)
                    v.wait_ge(xe_done, HW * (b + 1))
                    centre(v, link, h2[:, halves[b], :], xe[:, halves[b], :], stat[:, 0, halves[b]], centred)
                for b in range(B):
                    var = stat[:, 1, halves[b]]
                    v.wait_ge(h2_squared, TB * (b + 1))
                    v.tensor_scalar(var, var, 1.0 / D, LN_EPS, ALU.mult, ALU.add).then_inc(var_ready, 1)
                    scale_by_root(v, link, h2[:, halves[b], :], var, std_ready, B + b + 1, h2_ready, (g2[:], bb2[:]))
                for w in range(NW):
                    v.wait_ge(gelued, w + 1)
                    v.tensor_tensor(s.s0[:, 4 * w:4 * w + 4, :], s.s0[:, 4 * w:4 * w + 4, :], xe[:, 4 * w:4 * w + 4, :], ALU.add)

            @block.tensor
            def _(pe):
                pe.wait_ge(w_in, 96)
                pe.wait_ge(gate_done, 1)
                for w in range(NW):
                    pe.wait_ge(o_ready, w // HW + 1)
                    for j in range(2):
                        for t in range(4 * w, 4 * w + 4):
                            last = pe.transpose(s.bank[4 * j + w][:, P * (t % 4):P * (t % 4 + 1)], s.o[:, t, P * j:P * (j + 1)], s.ident[:])
                        last.then_inc(turned, 1)
                for w in range(NW):
                    pe.wait_ge(copied, 2 * w + 2)
                    for t in range(4 * w, 4 * w + 4):
                        for j in range(2):
                            last = pe.matmul(s.bank[w][:, P * (t % 4):P * (t % 4 + 1)], oT[:, j, P * t:P * (t + 1)], wo[:, j, :],
                                             start=j == 0, stop=j == 1)
                    last.then_inc(encoded, 1)
                for t in range(NT):
                    pe.wait_ge(h2_ready, t // TB + 1)
                    last = pe.transpose(s.bank[4 + t // 4][:, P * (t % 4):P * (t % 4 + 1)], h2[:, t, :], s.ident[:])
                    if t % 4 == 3:
                        last.then_inc(turned, 1)
                for t in range(NT):
                    pe.wait_ge(copied, 2 * NW + t // 4 + 1)
                    out = s.bank[t // 4][:, P * (t % 4):P * (t % 4 + 1)]
                    pe.matmul(out, h2T[:, P * t:P * (t + 1)], w2[:], start=True, stop=False)
                    last = pe.matmul(out, ones[:], b2[:], start=False, stop=True)
                    if t % 4 == 3:
                        last.then_inc(h2_out, 1)

            @block.scalar
            def _(a):
                for b in range(B):
                    a.activation(osq[:, heads[b], :], ov[:, heads[b], :], ACT.Square).then_inc(squared, 1)
                for b in range(B):
                    root(a, var_ready, b + 1, ost[:, heads[b]], std_ready)
                for n in range(2 * NW):
                    w, j = n // 2, n % 2
                    a.wait_ge(turned, n + 1)
                    a.activation(oT[:, j, W * w:W * (w + 1)], s.bank[4 * j + w][:], ACT.Copy).then_inc(copied, 1)
                for b in range(B):
                    a.wait_ge(centred, b + 1)
                    square_sums(a, h2[:, halves[b], :], s.s0[:, halves[b], :], stat[:, 1, halves[b]], TB, h2_squared)
                    root(a, var_ready, B + b + 1, stat[:, 1, halves[b]], std_ready)
                for n in range(NW):
                    a.wait_ge(turned, 2 * NW + n + 1)
                    a.activation(h2T[:, W * n:W * (n + 1)], s.bank[4 + n][:], ACT.Copy).then_inc(copied, 1)
                for n in range(NW):
                    a.wait_ge(h2_out, n + 1)
                    a.activation(s.s0[:, 4 * n:4 * n + 4, :].rearrange("p t d -> p (t d)"), s.bank[n][:],
                                 ACT.Gelu).then_inc(gelued, 1)


def phase_experts(nc, m, io, s):
    NJ = B * TOPK
    NU = TOPK * FB
    GT = NT // NW
    UP_BANKS = 4
    ctx = ExitStack()
    with ctx:
        mm = Memory(nc, ctx, m)
        wr = mm.sb("wr", [P, E])
        br = mm.sb("br", [1, E])
        ones = mm.sb("ones_row", [1, P])
        mean = mm.sb("mean_x", [P, B])
        lg = mm.sb("logits", [1, B, E])
        st = mm.sb("router_stat", [1, B, 2])
        top = mm.sb("top", [1, B, 8])
        idx = mm.sb("expert", [1, B, 8], U32)
        cw = mm.sb("mix", [1, B, TOPK])
        cwb = mm.sb("mix_b", [P, NJ])
        w1 = [mm.sb(f"w1_{j}", [P, F]) for j in range(NJ)]
        w2 = [mm.sb(f"w2_{j}", [P, FB, D]) for j in range(NJ)]
        b1 = [mm.sb(f"b1_{j}", [P, FB]) for j in range(NJ)]
        b2 = [mm.sb(f"b2_{j}", [1, D]) for j in range(NJ)]
        hh = [mm.sb(f"hidden{n}", [P, TOPK * FB, W]) for n in range(2)]
        y = mm.sb("y_moe", [P, NT, D])
        junk = mm.sb("moe_squares", [P, TB, D])
        stat = mm.sb("moe_stat", [P, 2, 2, NT])
        gam = mm.sb("gamma", [P, D])
        bet = mm.sb("beta_ln", [P, D])
        in_ = mm.sem("router_in")
        chain = mm.sem("moe_chain")
        mean_done = mm.sem("mean_done")
        logit_ready = mm.sem("logit_ready")
        sub_done = mm.sem("sub_done")
        exp_done = mm.sem("exp_done")
        picked = mm.sem("picked")
        mixed = mm.sem("mixed")
        mix_out = mm.sem("mix_out")
        mix_done = mm.sem("mix_done")
        w_in = [mm.sem(f"expert_in{j}") for j in range(NJ)]
        scaled = mm.sem("scaled")
        up = mm.sem("up")
        act = mm.sem("act")
        down = mm.sem("down")
        summed = mm.sem("y_summed")
        centred = mm.sem("moe_centred")
        sq_done = mm.sem("moe_squared")
        var_ready = mm.sem("moe_var")
        std_ready = mm.sem("moe_std")
        normed = mm.sem("y_normed")
        silued = mm.sem("y_silued")
        xn_done = mm.sem("xn_done")
        turned = mm.sem("xn_turned")
        with nc.Block() as block:
            @block.sync
            def _(sp):
                sp.dma_start(wr[:], io["L0_ffn_Wr"]).then_inc(in_, 16)
                sp.dma_start(br[:], io["L0_ffn_br"].rearrange("(a e) -> a e", a=1)).then_inc(in_, 16)
                sp.dma_start(gam[:], io["L0_ffn_gamma"].partition_broadcast(P)).then_inc(in_, 16)
                sp.dma_start(bet[:], io["L0_ffn_beta"].partition_broadcast(P)).then_inc(in_, 16)
                sp.wait_ge(picked, B)
                for j in range(NJ):
                    e = sp.value_load(idx[0:1, j // TOPK, j % TOPK:j % TOPK + 1], min_val=0, max_val=E - 1)
                    pick = bass.ds(e, 1)
                    sp.dma_start(w1[j][:], io["L0_ffn_W1"][pick].rearrange("a p f -> p (a f)")).then_inc(w_in[j], 16)
                    sp.dma_start(b1[j][:], io["b1_by_feature"][pick].rearrange("a p f -> p (a f)")).then_inc(w_in[j], 16)
                    sp.dma_start(w2[j][:], io["L0_ffn_W2"][pick].rearrange("a (f p) d -> p (a f) d", p=P)).then_inc(w_in[j], 16)
                    sp.dma_start(b2[j][:], io["L0_ffn_b2"][pick]).then_inc(w_in[j], 16)

            @block.vector
            def _(v):
                link = Link(v, chain)
                link(v.memset(ones[:], 1.0))
                link(v.tensor_reduce(mean[:], s.xnT[:].rearrange("p (b t) -> p b t", b=B), AX_X, ALU.add))
                v.tensor_scalar(mean[:], mean[:], 1.0 / T, None, ALU.mult).then_inc(mean_done, 1)
                v.wait_ge(in_, 64)
                v.wait_ge(logit_ready, 1)
                link(v.tensor_tensor(lg[:], s.bank[0][0:1, 0:B * E].rearrange("p (b e) -> p b e", b=B), bc(br[:], 1, B), ALU.add))
                link(v.tensor_reduce(st[:, :, 0], lg[:], AX_X, ALU.max))
                v.tensor_tensor(lg[:], lg[:], bc(st[:, :, 0], 2, E), ALU.subtract).then_inc(sub_done, 1)
                v.wait_ge(exp_done, 1)
                link(v.tensor_reduce(st[:, :, 1], lg[:], AX_X, ALU.add))
                link(v.reciprocal(st[:, :, 1], st[:, :, 1]))
                link(v.tensor_tensor(lg[:], lg[:], bc(st[:, :, 1], 2, E), ALU.mult))
                for b in range(B):
                    link(v.max(top[:, b, :], lg[:, b, :]))
                    v.max_index(idx[:, b, :], top[:, b, :], lg[:, b, :]).then_inc(picked, 1)
                v.tensor_tensor(cw[:], top[:, :, 0:TOPK], bc(top[:, :, 0], 2, TOPK), ALU.subtract).then_inc(sub_done, 1)
                v.wait_ge(exp_done, 2)
                link(v.tensor_reduce(st[:, :, 1], cw[:], AX_X, ALU.add))
                link(v.reciprocal(st[:, :, 1], st[:, :, 1]))
                v.tensor_tensor(cw[:], cw[:], bc(st[:, :, 1], 2, TOPK), ALU.mult).then_inc(mixed, 1)
                v.wait_ge(mixed, 1)
                v.wait_ge(mix_done, 1)
                for j in range(NJ):
                    v.wait_ge(w_in[j], 64)
                    v.tensor_scalar(w2[j][:], w2[j][:], cwb[:, j:j + 1], None, ALU.mult).then_inc(scaled, 1)
                    v.tensor_scalar(b2[j][:], b2[j][:], cw[0:1, j // TOPK, j % TOPK:j % TOPK + 1], None, ALU.mult).then_inc(scaled, 1)

                def add(w):
                    for t in range(GT * w, GT * (w + 1)):
                        v.wait_ge(down, t + 1)
                        v.tensor_tensor(y[:, t, :], s.bank[4 + t % 4][:, 0:D], s.xn[:, t, :], ALU.add).then_inc(summed, 1)

                def norm(b, k):
                    rows = slice(TB * b, TB * (b + 1))
                    x, out = ((y, s.g0), (s.x, s.xn))[k]
                    group_mean, var = stat[:, k, 0, rows], stat[:, k, 1, rows]
                    if k == 1:
                        v.wait_ge(silued, b + 1)
                        link(v.tensor_tensor(s.s0[:, rows, :], s.s0[:, rows, :], s.g0[:, rows, :], ALU.mult))
                        link(v.tensor_tensor(s.x[:, rows, :], s.x[:, rows, :], s.s0[:, rows, :], ALU.add))
                    centre(v, link, out[:, rows, :], x[:, rows, :], group_mean, centred)
                    v.wait_ge(sq_done, TB * (2 * b + k + 1))
                    v.tensor_scalar(var, var, 1.0 / D, LN_EPS, ALU.mult, ALU.add).then_inc(var_ready, 1)
                    scale_by_root(v, link, out[:, rows, :], var, std_ready, 2 * b + k + 1, xn_done if k else normed,
                                  None if k else (gam[:], bet[:]))

                add(0)
                add(1)
                v.wait_ge(summed, TB)
                norm(0, 0)
                add(2)
                norm(0, 1)
                add(3)
                v.wait_ge(summed, NT)
                norm(1, 0)
                norm(1, 1)

            @block.scalar
            def _(a):
                a.wait_ge(sub_done, 1)
                a.activation(lg[:], lg[:], ACT.Exp).then_inc(exp_done, 1)
                a.wait_ge(sub_done, 2)
                a.activation(cw[:], cw[:], ACT.Exp).then_inc(exp_done, 1)
                a.wait_ge(mix_out, 1)
                a.activation(cwb[:], s.bank[1][:, 0:NJ], ACT.Copy).then_inc(mix_done, 1)

                def gelus(w):
                    if w >= 2:
                        a.wait_ge(down, GT * (w - 1))
                    for n in range(NU):
                        j = TOPK * (w // 2) + n // FB
                        a.wait_ge(up, NU * w + n + 1)
                        if w % 2 == 0:
                            a.wait_ge(w_in[j], 64)
                        a.activation(hh[w % 2][:, n, :], s.bank[(NU * w + n) % UP_BANKS][:], ACT.Gelu,
                                     bias=b1[j][:, n % FB:n % FB + 1]).then_inc(act, 1)

                def norms(b):
                    rows = slice(TB * b, TB * (b + 1))
                    for k, x in enumerate((s.g0, s.xn)):
                        if k == 1:
                            a.wait_ge(normed, b + 1)
                            a.activation(s.g0[:, rows, :], s.g0[:, rows, :], ACT.Silu).then_inc(silued, 1)
                        a.wait_ge(centred, 2 * b + k + 1)
                        square_sums(a, x[:, rows, :], junk, stat[:, k, 1, rows], TB, sq_done)
                        root(a, var_ready, 2 * b + k + 1, stat[:, k, 1, rows], std_ready)

                for w in range(NW):
                    gelus(w)
                for b in range(B):
                    norms(b)
                for w in range(NW):
                    a.wait_ge(turned, w + 1)
                    a.activation(s.xnT[:, W * w:W * (w + 1)], s.bank[w][:], ACT.Copy)

            @block.tensor
            def _(pe):
                pe.wait_ge(mean_done, 1)
                pe.wait_ge(in_, 64)
                for b in range(B):
                    last = pe.matmul(s.bank[0][0:1, E * b:E * (b + 1)], mean[:, b:b + 1], wr[:], start=True, stop=True)
                last.then_inc(logit_ready, 1)
                pe.wait_ge(mixed, 1)
                pe.matmul(s.bank[1][:, 0:NJ], ones[:], cw[:].rearrange("p b k -> p (b k)"), start=True, stop=True).then_inc(mix_out, 1)
                pe.wait_ge(mix_done, 1)

                def ups(w):
                    for n in range(NU):
                        j = TOPK * (w // 2) + n // FB
                        if w % 2 == 0:
                            pe.wait_ge(w_in[j], 64)
                        if NU * w + n >= UP_BANKS:
                            pe.wait_ge(act, NU * w + n - (UP_BANKS - 1))
                        f = n % FB
                        pe.matmul(s.bank[(NU * w + n) % UP_BANKS][:], w1[j][:, P * f:P * (f + 1)], s.xnT[:, W * w:W * (w + 1)],
                                  start=True, stop=True).then_inc(up, 1)

                def downs(w):
                    pe.wait_ge(scaled, 2 * NJ)
                    pe.wait_ge(act, NU * (w + 1))
                    for q in range(4):
                        t = 4 * w + q
                        if t >= 4:
                            pe.wait_ge(summed, t - 3)
                        out = s.bank[4 + q][:, 0:D]
                        for n in range(NU):
                            j = TOPK * (w // 2) + n // FB
                            pe.matmul(out, hh[w % 2][:, n, P * q:P * (q + 1)], w2[j][:, n % FB, :], start=n == 0, stop=False)
                        for k in range(TOPK):
                            last = pe.matmul(out, ones[:], b2[TOPK * (w // 2) + k][:], start=False, stop=k == TOPK - 1)
                        last.then_inc(down, 1)

                ups(0)
                for w in range(NW):
                    if w + 1 < NW:
                        ups(w + 1)
                    downs(w)
                pe.wait_ge(act, NU * NW)
                for w in range(NW):
                    pe.wait_ge(xn_done, w // (NW // B) + 1)
                    for q in range(GT):
                        last = pe.transpose(s.bank[w][:, P * q:P * (q + 1)], s.xn[:, GT * w + q, :], s.ident[:])
                    last.then_inc(turned, 1)


def rotate(v, parts, bank, cos, sin, done):
    heads = W // HD
    x = bank[:].rearrange("p (h c) -> p h c", c=HD)
    first, second = (part[:].rearrange("p (h c) -> p h c", c=HD) for part in parts)
    v.tensor_tensor(first, x, bc(cos, 1, heads), ALU.mult).then_inc(done, 1)
    half = HD // 2
    for k in range(2):
        mine, other = slice(half * k, half * (k + 1)), slice(half * (1 - k), half * (2 - k))
        v.tensor_tensor(second[:, :, mine], x[:, :, other], bc(sin[:, mine], 1, heads), ALU.mult).then_inc(done, 1)


def phase_ternary(nc, m, io, s):
    ctx = ExitStack()
    NU = 2 * NT
    STEP = 2
    NS = NT // STEP
    with ctx:
        mm = Memory(nc, ctx, m)
        raw = mm.sb("raw", [P, NT, INNER])
        wk = mm.sb("wk", [P, INNER])
        wv = mm.sb("wv", [P, INNER])
        wb = mm.sb("wb", [P, NH])
        bb = mm.sb("bb", [P, NH])
        turn = [[mm.sb(f"rope_part{c}{n}", [P, W]) for n in range(2)] for c in range(2)]
        junk = mm.sb("abs_out", [P, W])
        acc = mm.sb("abs_sum", [P, 2, NU])
        tot = mm.sb("abs_total", [P, 2])
        thr = mm.sb("thr", [P, 2])
        ones = mm.sb("ones_sq", [P, P])
        la = mm.sb("log_alpha", [P, NH])
        lac = mm.sb("log_alpha_c", [P, IB])
        gap = mm.sb("gap", [P, P])
        le = mm.sb("le_full", [P, P])
        pos = mm.sb("pos1", [P, P])
        rev = mm.sb("rev", [P, 1])
        w_in = mm.sem("qk_w_in")
        rope_in = mm.sem("rope_in")
        small_in = mm.sem("small_in")
        chain = mm.sem("tern_chain")
        achain = mm.sem("tern_act_chain")
        ones_set = mm.sem("ones_set")
        b_ready = mm.sem("b_ready")
        z_ready = mm.sem("bz_ready")
        floored = mm.sem("floored")
        e_ready = mm.sem("be_ready")
        log_in = mm.sem("log_in")
        log_done = mm.sem("log_done")
        tables = mm.sem("att_tables")
        k_ready = mm.sem("k_ready")
        parts = mm.sem("rope_parts")
        k_done = mm.sem("k_done")
        k_abs = mm.sem("k_abs")
        av_ready = mm.sem("abs_v_ready")
        v_abs = mm.sem("v_abs")
        total_in = mm.sem("total_in")
        total = mm.sem("total")
        k_tern = mm.sem("k_tern")
        v_ready = mm.sem("v_ready")
        v_done = mm.sem("v_done")
        with nc.Block() as block:
            @block.sync
            def _(sp):
                for dst, src in ((wb, "L1_attn_WbT"), (wk, "L1_attn_WkT"), (wv, "L1_attn_WvT")):
                    sp.dma_start(dst[:], io[src]).then_inc(w_in, 16)
                for dst, src in ((s.cos, "c_cos"), (s.sin, "c_sin")):
                    sp.dma_start(dst[:], io[src]).then_inc(rope_in, 16)
                sp.dma_start(bb[:], io["L1_attn_bb"].partition_broadcast(P)).then_inc(small_in, 16)
                sp.dma_start(la[:], io["L1_attn_alpha_log"].rearrange("h a -> (h a)").partition_broadcast(P)).then_inc(small_in, 16)
                for k in range(2):
                    sp.dma_start(lac[HD * k:HD * (k + 1), :],
                                 io["alpha_log_by_parity"][k].partition_broadcast(HD)).then_inc(small_in, 16)
                for dst, src in ((gap, "c_gap"), (le, "c_le_full"), (pos, "c_pos1"), (rev, "c_rev")):
                    sp.dma_start(dst[:], io[src]).then_inc(small_in, 16)

            @block.tensor
            def _(pe):
                pe.wait_ge(w_in, 48)
                for t in range(NT):
                    last = pe.matmul(s.bank[7][:, NH * t:NH * (t + 1)], s.xnT[:, P * t:P * (t + 1)], wb[:], start=True, stop=True)
                last.then_inc(b_ready, 1)
                for n in range(NU):
                    t, c = n // 2, n % 2
                    tokens, cols = slice(P * t, P * (t + 1)), slice(W * c, W * (c + 1))
                    if n >= 4:
                        pe.wait_ge(parts, 3 * (n - 3))
                    pe.matmul(s.bank[n % 4][:], s.xnT[:, tokens], wk[:, cols], start=True, stop=True).then_inc(k_ready, 1)
                    if n >= 2:
                        pe.wait_ge(v_abs, n - 1)
                    pe.matmul(s.bank[4 + c][:], s.xnT[:, tokens], wv[:, cols], start=True, stop=True).then_inc(av_ready, 1)
                pe.wait_ge(ones_set, 1)
                pe.wait_ge(total_in, 1)
                pe.matmul(s.bank[6][:, 0:2], ones[:], tot[:], start=True, stop=True).then_inc(total, 1)
                pe.wait_ge(parts, 3 * NU)
                for n in range(NU):
                    t, c = n // 2, n % 2
                    if n >= 4:
                        pe.wait_ge(v_done, 2 * (n - 3))
                    pe.matmul(s.bank[n % 4][:], s.xnT[:, P * t:P * (t + 1)], wv[:, W * c:W * (c + 1)],
                              start=True, stop=True).then_inc(v_ready, 1)

            @block.gpsimd
            def _(g):
                for n in range(NU):
                    t, c = n // 2, n % 2
                    g.wait_ge(parts, 3 * n + 3)
                    g.tensor_tensor(raw[:, t, W * c:W * (c + 1)], turn[c][0][:], turn[c][1][:], ALU.add).then_inc(k_done, 1)

            @block.vector
            def _(v):
                link = Link(v, chain)
                v.memset(ones[:], 1.0).then_inc(ones_set, 1)
                v.wait_ge(rope_in, 32)
                for n in range(NU):
                    t, c = n // 2, n % 2
                    if n >= 2:
                        v.wait_ge(k_done, n - 1)
                    v.wait_ge(k_ready, n + 1)
                    rotate(v, turn[c], s.bank[n % 4], s.cos[:, t % TB, :], s.sin[:, t % TB, :], parts)
                    if n == 2:
                        v.wait_ge(b_ready, 1)
                        v.wait_ge(small_in, 128)
                        v.tensor_tensor(s.bk[:], s.bank[7][:, 0:NT * NH].rearrange("p (t h) -> p t h", h=NH), bc(bb[:], 1, NT),
                                        ALU.add).then_inc(z_ready, 1)
                        v.wait_ge(z_ready, 1)
                        for x in (s.bk, la, lac):
                            v.tensor_scalar(x[:], x[:], -87.0, None, ALU.max).then_inc(floored, 1)
                    if n == 5:
                        v.wait_ge(e_ready, 3)
                        for x in (s.bk, la, lac):
                            link(v.tensor_scalar(x[:], x[:], 1.0, None, ALU.add))
                            link(v.reciprocal(x[:], x[:]))
                        v.tensor_scalar(la[:], la[:], 1e-6, None, ALU.max).then_inc(log_in, 1)
                        v.tensor_scalar(lac[:], lac[:], 1e-6, None, ALU.max).then_inc(log_in, 1)
                    if n == NU - 1:
                        v.wait_ge(tables, NH + IB + 1)
                        v.tensor_tensor(s.dd[:], s.dd[:], bc(le[:], 1, NH), ALU.mult)

                v.wait_ge(k_abs, NU)
                v.wait_ge(v_abs, NU)
                v.tensor_reduce(tot[:], acc[:], AX_X, ALU.add).then_inc(total_in, 1)
                v.wait_ge(total, 1)
                link(v.tensor_scalar(thr[:], s.bank[6][:, 0:2], 1.0 / (N * INNER), None, ALU.mult))
                link(v.tensor_scalar(thr[:], thr[:], 0.01, 10.0, ALU.max, ALU.min))
                for k, out in enumerate((s.kt, s.vt)):
                    for n in range(NS):
                        rows = slice(STEP * n, STEP * (n + 1))
                        x, y = (z[:, rows, :].rearrange("p t c -> p (t c)") for z in (raw, out))
                        if k == 1:
                            v.wait_ge(v_done, 4 * STEP * (n + 1))
                        v.scalar_tensor_tensor(y, x, thr[:, k:k + 1], y, ALU.is_gt, ALU.mult).then_inc(k_tern, 1)

            @block.scalar
            def _(a):
                link = Link(a, achain)
                for n in range(NU):
                    t, c = n // 2, n % 2
                    if n == 4:
                        a.wait_ge(z_ready, 1)
                        a.wait_ge(floored, 3)
                        for x in (s.bk, la, lac):
                            a.activation(x[:], x[:], ACT.Exp, scale=-1.0).then_inc(e_ready, 1)
                    if n == 8:
                        a.wait_ge(log_in, 2)
                        a.activation(la[:], la[:], ACT.Ln).then_inc(log_done, 1)
                        a.activation(lac[:], lac[:], ACT.Ln).then_inc(log_done, 1)
                        a.wait_ge(log_done, 2)
                    if n > 8 and n % 2 == 0:
                        k = n // 2 - 5
                        for h in range(2 * k, min(2 * k + 2, NH)):
                            a.activation(s.dd[:, h, :], gap[:], ACT.Exp, scale=la[:, h:h + 1]).then_inc(tables, 1)
                        if k < IB:
                            a.activation(s.dt[:, k, :], pos[:], ACT.Exp, scale=lac[:, k:k + 1]).then_inc(tables, 1)
                        if k == IB:
                            a.activation(s.de[:], la[:], ACT.Exp, scale=rev[:]).then_inc(tables, 1)
                    a.wait_ge(av_ready, n + 1)
                    link(a.activation(junk[:], s.bank[4 + c][:], ACT.Abs, accum_out=acc[:, 1, n:n + 1]))
                    a.sem_inc(v_abs, 1)
                    a.wait_ge(k_done, n + 1)
                    x = raw[:, t, W * c:W * (c + 1)]
                    link(a.activation(s.kt[:, t, W * c:W * (c + 1)], x, ACT.Sign))
                    link(a.activation(x, x, ACT.Abs, accum_out=acc[:, 0, n:n + 1]))
                    a.sem_inc(k_abs, 1)
                for n in range(NU):
                    t, c = n // 2, n % 2
                    a.wait_ge(v_ready, n + 1)
                    a.activation(s.vt[:, t, W * c:W * (c + 1)], s.bank[n % 4][:], ACT.Sign).then_inc(v_done, 1)
                    a.wait_ge(k_tern, t // STEP + 1)
                    a.activation(raw[:, t, W * c:W * (c + 1)], s.bank[n % 4][:], ACT.Abs).then_inc(v_done, 1)


def phase_attend(nc, m, io, s):
    ctx = ExitStack()
    HB = IB // 2
    UH = 2 * HB
    UNITS = 4
    with ctx:
        mm = Memory(nc, ctx, m)
        wq = mm.sb("wq", [P, INNER])
        wo = mm.sb("wo1", [P, IB, D])
        xt = [mm.sb(f"x_tile{b}", [P, P]) for b in range(B)]
        part = [mm.sb(f"q_part{n}", [P, W]) for n in range(2)]
        qr = mm.sb("qr", [P, W])
        qbd = [mm.sb(f"q_by_head{c}", [P, HB, 2, P]) for c in range(2)]
        qd = [mm.sb(f"qd{c}", [P, HB, P]) for c in range(2)]
        k32 = mm.sb("k_fp32", [P, W])
        kf = [mm.sb(f"kf{c}", [P, HB, P]) for c in range(2)]
        kend = [mm.sb(f"k_end{c}", [P, UH, HD]) for c in range(2)]
        vb = [mm.sb(f"vb{c}", [P, UH, HD]) for c in range(2)]
        wT = [mm.sb(f"wT{c}", [P, UH, P]) for c in range(2)]
        oT = [mm.sb(f"o_feat{c}", [P, HB, P]) for c in range(2)]
        st = [mm.sb(f"att_state{b}", [P, IB, P]) for b in range(B)]
        c_in = mm.sem("att_in")
        init = mm.sem("att_init")
        xt_done = mm.sem("att_xt_done")
        q_ready = mm.sem("q_ready")
        q_parts = mm.sem("q_parts")
        qr_done = mm.sem("qr_done")
        q_turned = mm.sem("q_turned")
        k32_done = mm.sem("k32_done")
        qd_done = mm.sem("qd_done")
        qbd_done = mm.sem("q_by_head_done")
        kf_done = mm.sem("kf_done")
        vb_done = mm.sem("vb_done")
        k_turned = mm.sem("k_turned")
        kend_done = mm.sem("kend_done")
        scored = mm.sem("scored")
        w_done = mm.sem("w_done")
        o_ready = mm.sem("att_o_ready")
        oT_done = mm.sem("oT_done")
        s_ready = mm.sem("att_s_ready")
        s_done = mm.sem("att_s_done")
        f_ready = mm.sem("f_ready")
        f_done = mm.sem("f_done")

        def number(unit):
            i, b, c = unit
            return i * UNITS + (2 * b + c)

        def tile(unit):
            i, b, c = unit
            return i * B + b

        def after(unit):
            i, b, c = unit
            if c == 0:
                return i, b, 1
            return (i, 1, 0) if b == 0 else (i + 1, 0, 0)

        def over_units(eng, step):
            def tile_units(i, prev, last):
                for b in range(B):
                    for c in range(2):
                        unit = (i, b, c)
                        step(prev, unit, None if last and b + c == 2 else after(unit))
                        prev = unit

            step(None, None, (0, 0, 0))
            tile_units(0, None, False)
            with eng.Fori(0, TB - 2) as k:
                tile_units(k + 1, (k, 1, 1), False)
            tile_units(TB - 1, (TB - 2, 1, 1), True)
            step((TB - 1, 1, 1), None, None)

        def later(eng, sem, value):
            if not (isinstance(value, int) and value <= 0):
                eng.wait_ge(sem, value)

        with nc.Block() as block:
            @block.sync
            def _(sp):
                sp.dma_start(wq[:], io["L1_attn_WqT"]).then_inc(c_in, 16)
                sp.dma_start(wo[:], io["L1_attn_WoT"].rearrange("(j p) d -> p j d", p=P)).then_inc(c_in, 16)

            @block.scalar
            def _(a):
                a.wait_ge(init, 2 * B)

                def step(prev, unit, nxt):
                    if nxt is not None:
                        n, c = number(nxt), nxt[2]
                        i, b, c = nxt
                        if c == 0:
                            a.activation(xt[b][:], s.xnT[:, bass.ds(i * P + b * T, P)], ACT.Copy).then_inc(xt_done, 1)
                        later(a, scored, n * 2 - 2)
                        a.activation(k32[:], s.kt[:, bass.ds(i + b * TB, 1), W * c:W * (c + 1)].rearrange("p a c -> p (a c)"),
                                     ACT.Copy).then_inc(k32_done, 1)
                    if prev is not None:
                        n, c = number(prev), prev[2]
                        a.wait_ge(o_ready, n + 1)
                        a.activation(oT[c][:].rearrange("p j t -> p (j t)"), s.bank[5][:], ACT.Copy).then_inc(oT_done, 1)
                    if nxt is not None:
                        n, c = number(nxt), nxt[2]
                        a.wait_ge(k_turned, n + 1)
                        a.activation(kf[c][:].rearrange("p j t -> p (j t)"), s.bank[2][:], ACT.Copy).then_inc(kf_done, 1)
                        a.wait_ge(q_turned, n + 1)
                        for k in range(2):
                            rows = slice(HD * k, HD * (k + 1))
                            a.activation(qbd[c][rows, :, k, :], s.bank[1][rows, :].rearrange("p (j t) -> p j t", t=P),
                                         ACT.Copy).then_inc(qbd_done, 1)
                    if prev is not None and prev[2] == 1:
                        i, b, c = prev
                        a.wait_ge(f_ready, tile(prev) + 1)
                        a.activation(s.s1[:, bass.ds(i + b * TB, 1), :].rearrange("p a d -> p (a d)"), s.bank[7][:, 0:D],
                                     ACT.Copy).then_inc(f_done, 1)

                over_units(a, step)

            @block.gpsimd
            def _(g):
                def step(prev, unit, nxt):
                    if nxt is None:
                        return
                    i, b, c = nxt
                    n = number(nxt)
                    later(g, s_ready, n - 1)
                    beta = s.bk[:, bass.ds(i + b * TB, 1), UH * c:UH * (c + 1)].rearrange("p a h -> p (a h)")
                    g.tensor_tensor(vb[c][:], s.vt[:, bass.ds(i + b * TB, 1), W * c:W * (c + 1)].rearrange("p a (h c) -> p (a h) c", c=HD),
                                    bc(beta, 2, HD), ALU.mult).then_inc(vb_done, 1)

                over_units(g, step)

            @block.vector
            def _(v):
                for b in range(B):
                    v.memset(st[b][:], 0.0).then_inc(init, 1)
                for c in range(2):
                    v.memset(qbd[c][:], 0.0).then_inc(init, 1)
                v.wait_ge(init, 2 * B)

                def step(prev, unit, nxt):
                    if unit is not None:
                        n, c = number(unit), unit[2]
                        v.wait_ge(qbd_done, n * 2 + 2)
                        v.tensor_tensor(qd[c][:], s.bank[1][:].rearrange("p (j t) -> p j t", t=P), s.dt[:, HB * c:HB * (c + 1), :],
                                        ALU.mult).then_inc(qd_done, 1)
                        for k in range(2):
                            v.wait_ge(scored, n * 2 + (k + 1))
                            v.tensor_tensor(wT[c][:, 4 * k:4 * (k + 1), :], s.bank[3 + k][:].rearrange("p (h t) -> p h t", t=P),
                                            s.dd[:, UH * c + 4 * k:UH * c + 4 * (k + 1), :], ALU.mult).then_inc(w_done, 1)
                    if nxt is not None:
                        n, c = number(nxt), nxt[2]
                        v.wait_ge(q_ready, n + 1)
                        later(v, qr_done, n)
                        i, b, c = nxt
                        cos, sin = (table[:, bass.ds(i, 1), :].rearrange("p a c -> p (a c)") for table in (s.cos, s.sin))
                        rotate(v, part, s.bank[0], cos, sin, q_parts)
                        v.wait_ge(q_parts, n * 3 + 3)
                        v.tensor_tensor(qr[:], part[0][:], part[1][:], ALU.add).then_inc(qr_done, 1)
                    if prev is not None:
                        i, b, c = prev
                        n = number(prev)
                        v.wait_ge(s_ready, n + 1)
                        later(v, s_done, n * UH)
                        for j in range(HB):
                            for k in range(2):
                                rows, cols = slice(HD * k, HD * (k + 1)), slice(HD * k, HD * (k + 1))
                                block_ = st[b][rows, HB * c + j, cols]
                                v.scalar_tensor_tensor(block_, block_, s.dt[rows, HB * c + j, P - 1:P],
                                                       s.bank[6][rows, P * j + HD * k:P * j + HD * (k + 1)], ALU.mult, ALU.add).then_inc(s_done, 1)
                    if nxt is not None:
                        i, b, c = nxt
                        v.tensor_tensor(kend[c][:], s.kt[:, bass.ds(i + b * TB, 1), W * c:W * (c + 1)].rearrange("p a (h c) -> p (a h) c", c=HD),
                                        bc(s.de[:, UH * c:UH * (c + 1)], 2, HD), ALU.mult).then_inc(kend_done, 1)
                over_units(v, step)

            @block.tensor
            def _(pe):
                pe.wait_ge(c_in, 32)
                pe.wait_ge(init, 2 * B)

                def turn_queries(nxt):
                    n = number(nxt)
                    pe.wait_ge(qr_done, n + 1)
                    for j in range(HB):
                        last = pe.transpose(s.bank[1][:, P * j:P * (j + 1)], qr[:, P * j:P * (j + 1)], s.ident[:])
                    last.then_inc(q_turned, 1)

                def step(prev, unit, nxt):
                    if unit is not None:
                        n, c = number(unit), unit[2]
                        pe.wait_ge(kf_done, n + 1)
                        pe.wait_ge(qbd_done, n * 2 + 2)
                        later(pe, w_done, n * 2)
                        for j in range(HB):
                            last = pe.matmul(s.bank[3 + j // 2][:, 2 * P * (j % 2):2 * P * (j % 2 + 1)], kf[c][:, j, :],
                                             qbd[c][:, j].rearrange("p k t -> p (k t)"), start=True, stop=True)
                            if j % 2 == 1:
                                last.then_inc(scored, 1)
                    if nxt is not None:
                        n, c = number(nxt), nxt[2]
                        later(pe, q_parts, n * 3)
                        pe.wait_ge(xt_done, tile(nxt) + 1)
                        pe.matmul(s.bank[0][:], xt[nxt[1]][:], wq[:, W * c:W * (c + 1)], start=True, stop=True).then_inc(q_ready, 1)
                        pe.wait_ge(k32_done, n + 1)
                        later(pe, kf_done, n)
                        for j in range(HB):
                            last = pe.transpose(s.bank[2][:, P * j:P * (j + 1)], k32[:, P * j:P * (j + 1)], s.ident[:])
                        last.then_inc(k_turned, 1)
                        if unit is None:
                            turn_queries(nxt)
                    if prev is not None:
                        n, c = number(prev), prev[2]
                        pe.wait_ge(oT_done, n + 1)
                        if c == 0:
                            later(pe, f_done, tile(prev))
                        for j in range(HB):
                            last = pe.matmul(s.bank[7][:, 0:D], oT[c][:, j, :], wo[:, HB * c + j, :],
                                             start=c == 0 and j == 0, stop=c == 1 and j == HB - 1)
                        if c == 1:
                            last.then_inc(f_ready, 1)
                    if unit is not None:
                        i, b, c = unit
                        n = number(unit)
                        pe.wait_ge(qd_done, n + 1)
                        later(pe, oT_done, n)
                        later(pe, s_done, (n - UNITS + 1) * UH)
                        pe.wait_ge(vb_done, n + 1)
                        pe.wait_ge(w_done, n * 2 + 2)
                        for j in range(HB):
                            if j == HB - 1 and nxt is not None:
                                turn_queries(nxt)
                            pe.matmul(s.bank[5][:, P * j:P * (j + 1)], st[b][:, HB * c + j, :], qd[c][:, j, :], start=True, stop=False)
                            for k in range(2):
                                last = pe.matmul(s.bank[5][HD * k:HD * (k + 1), P * j:P * (j + 1)], vb[c][:, 2 * j + k, :],
                                                 wT[c][:, 2 * j + k, :], start=False, stop=True)
                        last.then_inc(o_ready, 1)
                        pe.wait_ge(kend_done, n + 1)
                        later(pe, s_done, n * UH)
                        for j in range(HB):
                            pair = slice(2 * j, 2 * j + 2)
                            last = pe.matmul(s.bank[6][:, P * j:P * (j + 1)], kend[c][:, pair, :].rearrange("p h c -> p (h c)"),
                                             vb[c][:, pair, :].rearrange("p h c -> p (h c)"), start=True, stop=True)
                        last.then_inc(s_ready, 1)

                over_units(pe, step)


def phase_keys(nc, m, io, s):
    Q = 2 * PH
    EB = NE // P
    ctx = ExitStack()
    with ctx:
        mm = Memory(nc, ctx, m)
        w = mm.sb("wq_bn", [P, Q, P])
        wt = mm.sb("wq_bn_t", [P, Q, P])
        keys = mm.sb("keys", [P, Q, NK])
        bn = mm.sb("bn", [P, 2, Q])
        down = mm.sb("down_t", [P, NE])
        ones = mm.sb("ones_k", [P, P])
        mrow = mm.sb("mean_row", [P, D])
        mcol = mm.sb("mean_col", [P, 1])
        xc = mm.sb("x_centred", [P, NT, D])
        cov = mm.sb("cov", [P, D])
        wc = mm.sb("w_cov_w", [P, Q, P])
        mv = mm.sb("mean_var", [P, 2, Q])
        offset_keys = mm.sb("offset_keys", [P, Q, NK])
        k_in = mm.sem("keys_in")
        chain = mm.sem("keys_chain")
        ones_done = mm.sem("ones_done")
        row_ready = mm.sem("row_ready")
        centred = mm.sem("centred")
        cov_ready = mm.sem("cov_ready")
        cov_done = mm.sem("cov_done")
        wc_ready = mm.sem("wc_ready")
        wc_done = mm.sem("wc_done")
        mv_ready = mm.sem("mv_ready")
        var_ready = mm.sem("bn_var")
        std_ready = mm.sem("bn_std")
        scaled = mm.sem("keys_scaled")
        m_ready = mm.sem("m_ready")
        h_ready = mm.sem("down_ready")
        h_done = mm.sem("down_done")
        with nc.Block() as block:
            @block.sync
            def _(sp):
                sp.dma_start(w[:].rearrange("p q d -> p (q d)"), io["L1_ffn_w_q"]).then_inc(k_in, 16)
                sp.dma_start(wt[:], io["w_q_by_key_feature"].rearrange("(q d) m -> d q m", d=P)).then_inc(k_in, 16)
                sp.dma_start(keys[:], io["keys_by_feature"]).then_inc(k_in, 16)
                sp.dma_start(bn[:], io["bn_by_feature"]).then_inc(k_in, 16)
                sp.dma_start(down[:], io["down_by_feature"]).then_inc(k_in, 16)
                sp.dma_start(s.up[:], io["L1_ffn_up_embed"].rearrange("(j p) d -> p j d", p=P)).then_inc(k_in, 16)

            @block.tensor
            def _(pe):
                pe.wait_ge(ones_done, 1)
                for t in range(NT):
                    last = pe.matmul(s.bank[0][:, 0:D], ones[:], s.xn[:, t, :], start=t == 0, stop=t == NT - 1)
                last.then_inc(row_ready, 1)
                pe.wait_ge(centred, 1)
                for t in range(NT):
                    last = pe.matmul(s.bank[1][:, 0:D], xc[:, t, :], xc[:, t, :], start=t == 0, stop=t == NT - 1)
                last.then_inc(cov_ready, 1)
                pe.wait_ge(cov_done, 1)
                pe.wait_ge(k_in, 96)
                for q in range(4):
                    pe.matmul(s.bank[4 + q][:], cov[:], w[:, 4 * q:4 * q + 4, :].rearrange("p q d -> p (q d)"), start=True,
                              stop=True).then_inc(wc_ready, 1)
                for q in range(Q):
                    pe.matmul(s.bank[2][:, q:q + 1], w[:, q, :], mcol[:], start=True, stop=True)
                pe.wait_ge(wc_done, 4)
                for q in range(Q):
                    last = pe.matmul(s.bank[2][:, Q + q:Q + q + 1], wc[:, q, :], ones[:, 0:1], start=True, stop=True)
                last.then_inc(mv_ready, 1)
                for j in range(EB):
                    for c in range(NW):
                        n = NW * j + c
                        if n >= 4:
                            pe.wait_ge(h_done, n - 3)
                        pe.matmul(s.bank[4 + n % 4][:], down[:, P * j:P * (j + 1)], s.xnT[:, W * c:W * (c + 1)], start=True,
                                  stop=True).then_inc(h_ready, 1)
                pe.wait_ge(scaled, 2)
                for q in range(Q):
                    pe.matmul(s.bank[0][:, NK * q:NK * (q + 1)], wt[:, q, :], wc[:, q, 0:NK], start=True, stop=True)
                pe.matmul(s.bank[1][:], ones[:], offset_keys[:].rearrange("p q k -> p (q k)"), start=True, stop=True).then_inc(m_ready, 1)

            @block.vector
            def _(v):
                link = Link(v, chain)
                v.memset(ones[:], 1.0).then_inc(ones_done, 1)
                link(v.tensor_reduce(mcol[:], s.xnT[:], AX_X, ALU.add))
                link(v.tensor_scalar(mcol[:], mcol[:], 1.0 / N, None, ALU.mult))
                v.wait_ge(row_ready, 1)
                link(v.tensor_scalar(mrow[:], s.bank[0][:, 0:D], 1.0 / N, None, ALU.mult))
                v.tensor_tensor(xc[:], s.xn[:], bc(mrow[:], 1, NT), ALU.subtract).then_inc(centred, 1)
                v.wait_ge(cov_ready, 1)
                v.tensor_scalar(cov[:], s.bank[1][:, 0:D], 1.0 / N, None, ALU.mult).then_inc(cov_done, 1)
                v.wait_ge(k_in, 96)
                for q in range(4):
                    v.wait_ge(wc_ready, q + 1)
                    v.tensor_tensor(wc[:, 4 * q:4 * q + 4, :], w[:, 4 * q:4 * q + 4, :],
                                    s.bank[4 + q][:].rearrange("p (q d) -> p q d", d=P), ALU.mult).then_inc(wc_done, 1)
                v.wait_ge(mv_ready, 1)
                link(v.tensor_copy(mv[:], s.bank[2][:, 0:2 * Q].rearrange("p (k q) -> p k q", k=2)))
                mean, var = mv[:, 0, :], mv[:, 1, :]
                v.tensor_scalar(var, var, LN_EPS, None, ALU.add).then_inc(var_ready, 1)
                v.wait_ge(std_ready, 1)
                link(v.reciprocal(var, var))
                link(v.tensor_tensor(var, var, bn[:, 0, :], ALU.mult))
                v.tensor_tensor(wc[:, :, 0:NK], keys[:], bc(var, 2, NK), ALU.mult).then_inc(scaled, 1)
                link(v.tensor_tensor(mean, mean, var, ALU.mult))
                link(v.tensor_tensor(mean, bn[:, 1, :], mean, ALU.subtract))
                v.tensor_tensor(offset_keys[:], keys[:], bc(mean, 2, NK), ALU.mult).then_inc(scaled, 1)
                v.wait_ge(m_ready, 1)
                v.tensor_copy(s.keymat[:], s.bank[0][:])
                v.tensor_copy(s.keyrow[:], s.bank[1][:])

            @block.scalar
            def _(a):
                root(a, var_ready, 1, mv[:, 1, :], std_ready)
                for n in range(EB * NW):
                    a.wait_ge(h_ready, n + 1)
                    a.activation(s.act[:, n // NW, W * (n % NW):W * (n % NW + 1)], s.bank[4 + n % 4][:],
                                 ACT.Gelu_apprx_tanh).then_inc(h_done, 1)


def phase_product_keys(nc, m, io, s, out):
    Q = 2 * PH
    EB = NE // P
    RING = 4
    GROUP = 4
    ctx = ExitStack()
    with ctx:
        mm = Memory(nc, ctx, m)
        xt = mm.sb("x_tile", [P, P])
        sim = [mm.sb(f"sim{u}", [P, Q, NK]) for u in range(2)]
        top = mm.sb("top8", [P, Q, PK])
        comb = mm.sb("comb", [P, PH, PK * PK])
        best = [mm.sb(f"best{u}", [P, PH, PK]) for u in range(2)]
        neg_max = [mm.sb(f"neg_max{u}", [P, PH]) for u in range(2)]
        rel = mm.sb("rel", [P, PH, PK])
        rz = mm.sb("recip_z", [P, PH])
        diag = [mm.sb(f"diag_recip_z{u}", [P, PH, P]) for u in range(2)]
        sums = [mm.sb(f"sums{r}", [P, NK, NK]) for r in range(RING)]
        soft = [mm.sb(f"soft{r}", [P, NE]) for r in range(RING)]
        sel = [mm.sb(f"selected{r}", [P, NE]) for r in range(RING)]
        wgt = mm.sb("weighted", [P, EB, P])
        pk = mm.sb("pk_out", [P, NT, D])
        idle = mm.sb("idle", [P, 1])
        xt_done = mm.sem("xt_done")
        sim_ready = mm.sem("sim_ready")
        sim_done = mm.sem("sim_done")
        top_done = mm.sem("top_done")
        comb_done = mm.sem("comb_done")
        best_done = mm.sem("best_done")
        rel_done = mm.sem("rel_done")
        rexp_done = mm.sem("rexp_done")
        z_done = mm.sem("z_done")
        rz_done = mm.sem("rz_done")
        diag_done = mm.sem("diag_done")
        sums_done = mm.sem("sums_done")
        soft_done = mm.sem("soft_done")
        sel_done = mm.sem("sel_done")
        head_in = mm.sem("head_in")
        wgt_done = mm.sem("wgt_done")
        out_ready = mm.sem("pk_out_ready")
        out_kept = mm.sem("pk_out_kept")
        silu_done = mm.sem("pk_silu_done")
        gated = mm.sem("pk_gated")
        res_done = mm.sem("res_done")
        stored = mm.sem("stored")
        out_v = out.rearrange("b (c p) d -> p (b c) d", p=P)

        def over_tiles(eng, steps):
            steps(None, 1, None, 0)
            steps(0, 0, None, 1)
            with eng.Fori(0, NT // 2 - 1) as i:
                for k in range(2):
                    n = i * 2 + 1 + k
                    steps(n, 1 - k, n - 1, n + 1)
            steps(NT - 1, 1, NT - 2, None)
            steps(None, 0, NT - 1, None)

        def at(n, size):
            return bass.ds(n * size, size)

        def ring_free(eng, sem, n, h):
            if not (isinstance(n, int) and n * PH + h < RING):
                eng.wait_ge(sem, n * PH + (h - RING + 1))

        with nc.Block() as block:
            @block.sync
            def _(sp):
                for k in range(NT // GROUP):
                    sp.wait_ge(res_done, k + 1)
                    rows = slice(GROUP * k, GROUP * (k + 1))
                    sp.dma_start(out_v[:, rows, :], pk[:, rows, :]).then_inc(stored, 16)
                sp.wait_ge(stored, 16 * NT // GROUP)

            @block.gpsimd
            def _(g):
                def steps(n, u, prev, nxt):
                    if n is not None:
                        g.wait_ge(sim_done, n + 1)
                        for h in range(PH):
                            ring_free(g, sel_done, n, h)
                            g.tensor_tensor(sums[h % RING][:], bc(sim[u][:, h, :], 2, NK), bc(sim[u][:, PH + h, :], 1, NK), ALU.add).then_inc(sums_done, 1)
                    if nxt is not None:
                        g.wait_ge(top_done, nxt + 1)
                        row, col = top[:, 0:PH, :], top[:, PH:Q, :]
                        g.tensor_tensor(comb[:].rearrange("p h (a b) -> p h a b", a=PK), bc(row, 3, PK), bc(col, 2, PK), ALU.add).then_inc(comb_done, 1)

                over_tiles(g, steps)
                for k in range(NT // GROUP):
                    g.wait_ge(gated, k + 1)
                    rows = slice(GROUP * k, GROUP * (k + 1))
                    g.tensor_tensor(pk[:, rows, :], pk[:, rows, :], s.x[:, rows, :], ALU.add).then_inc(res_done, 1)

            @block.tensor
            def _(pe):
                def steps(n, u, prev, nxt):
                    ct = s.bank[2 + 2 * u:4 + 2 * u]
                    for h in range(PH):
                        if h == 0 and nxt is not None:
                            pe.wait_ge(xt_done, nxt + 1)
                            pe.matmul(s.bank[0][:], xt[:], s.keymat[:], start=True, stop=True).then_inc(sim_ready, 1)
                        if n is not None:
                            if h == 0:
                                pe.wait_ge(diag_done, n + 1)
                            pe.wait_ge(sel_done, n * PH + (h + 1))
                            for j in range(EB):
                                last = pe.matmul(ct[j // 4][:, P * (j % 4):P * (j % 4 + 1)], sel[h % RING][:, P * j:P * (j + 1)], diag[u][:, h, :],
                                                 start=h == 0 and j % 4 == 0, stop=h == PH - 1, skip_group_check=True)
                            last.then_inc(head_in, 1)
                        if h == 3 and prev is not None:
                            pe.wait_ge(wgt_done, prev * 2 + 2)
                            if not (isinstance(prev, int) and prev == 0):
                                pe.wait_ge(out_kept, prev)
                            for j in range(EB):
                                last = pe.matmul(s.bank[6][:, 0:D], wgt[:, j, :], s.up[:, j, :], start=j == 0, stop=j == EB - 1)
                            last.then_inc(out_ready, 1)

                over_tiles(pe, steps)

            @block.scalar
            def _(a):
                def steps(n, u, prev, nxt):
                    for h in range(PH):
                        r = h % RING
                        if n is not None:
                            a.wait_ge(sums_done, n * PH + (h + 1))
                            ring_free(a, sel_done, n, h)
                            a.activation(soft[r][:], sums[r][:].rearrange("p i j -> p (i j)"), ACT.Exp, bias=neg_max[u][:, h:h + 1]).then_inc(soft_done, 1)
                        if nxt is not None:
                            if h == 0:
                                if not (isinstance(nxt, int) and nxt == 0):
                                    a.wait_ge(sim_ready, nxt)
                                a.activation(xt[:], s.xnT[:, at(nxt, P)], ACT.Copy).then_inc(xt_done, 1)
                            if h == 7:
                                a.wait_ge(rel_done, nxt + 1)
                                a.activation(rel[:], rel[:], ACT.Exp).then_inc(rexp_done, 1)
                        if h == 1 and n is not None:
                            a.wait_ge(rz_done, n + 1)
                            for k in range(PH):
                                last = a.activation(diag[u][:, k, :], s.ident[:], ACT.Copy, scale=rz[:, k:k + 1])
                            last.then_inc(diag_done, 1)
                        if h == 6 and prev is not None:
                            a.wait_ge(out_ready, prev + 1)
                            a.activation(pk[:, at(prev, 1), :].rearrange("p a d -> p (a d)"), s.bank[6][:, 0:D], ACT.Copy).then_inc(out_kept, 1)

                over_tiles(a, steps)
                a.wait_ge(out_kept, NT)
                for k in range(NT // GROUP):
                    rows = slice(GROUP * k, GROUP * (k + 1))
                    a.activation(pk[:, rows, :], pk[:, rows, :], ACT.Silu).then_inc(silu_done, 1)

            @block.vector
            def _(v):
                def steps(n, u, prev, nxt):
                    w = 1 - u
                    for h in range(PH):
                        r = h % RING
                        if n is not None:
                            v.wait_ge(soft_done, n * PH + (h + 1))
                            ring_free(v, head_in, n, h)
                            v.scalar_tensor_tensor(sel[r][:], sums[r][:].rearrange("p i j -> p (i j)"), best[u][:, h, PK - 1:PK], soft[r][:],
                                                   ALU.is_ge, ALU.mult).then_inc(sel_done, 1)
                        if h == 1 and prev is not None:
                            v.wait_ge(head_in, prev * PH + PH)
                            if not (isinstance(prev, int) and prev == 0):
                                v.wait_ge(out_ready, prev)
                            for k in range(2):
                                v.tensor_tensor(wgt[:, 4 * k:4 * k + 4, :], s.bank[2 + 2 * w + k][:].rearrange("p (j t) -> p j t", t=P),
                                                s.act[:, 4 * k:4 * k + 4, at(prev, P)], ALU.mult).then_inc(wgt_done, 1)
                        if nxt is not None:
                            if h == 4:
                                v.wait_ge(sim_ready, nxt + 1)
                                v.tensor_tensor(sim[w][:].rearrange("p q k -> p (q k)"), s.bank[0][:], s.keyrow[:], ALU.add).then_inc(sim_done, 1)
                                v.wait_ge(sim_done, nxt + 1)
                                v.memset(idle[:], 0.0)
                                for q in range(Q):
                                    ins = v.max(top[:, q, :], sim[w][:, q, :])
                                ins.then_inc(top_done, 1)
                            if h == 5:
                                v.wait_ge(comb_done, nxt + 1)
                                v.memset(idle[:], 0.0)
                                for k in range(PH):
                                    ins = v.max(best[w][:, k, :], comb[:, k, :])
                                ins.then_inc(best_done, 1)
                            if h == 6:
                                v.wait_ge(best_done, nxt + 1)
                                v.tensor_scalar(neg_max[w][:], best[w][:, :, 0], -1.0, None, ALU.mult)
                                v.tensor_tensor(rel[:], best[w][:], bc(best[w][:, :, 0], 2, PK), ALU.subtract).then_inc(rel_done, 1)
                            if h == 7:
                                v.wait_ge(rexp_done, nxt + 1)
                                v.tensor_reduce(rz[:], rel[:], AX_X, ALU.add).then_inc(z_done, 1)
                                v.wait_ge(z_done, nxt + 1)
                                v.reciprocal(rz[:], rz[:]).then_inc(rz_done, 1)

                over_tiles(v, steps)
                for k in range(NT // GROUP):
                    v.wait_ge(silu_done, k + 1)
                    rows = slice(GROUP * k, GROUP * (k + 1))
                    v.tensor_tensor(pk[:, rows, :], pk[:, rows, :], s.s1[:, rows, :], ALU.mult).then_inc(gated, 1)


class Shared:
    pass


def clear(nc, semaphores):
    with nc.Block() as block:
        @block.sync
        def _(sp):
            for semaphore in semaphores:
                sp.sem_clear(semaphore)


def build(nc, io, out):
    ctx = ExitStack()
    with ctx:
        m = Memory(nc, ctx)
        s = Shared()
        s.x = m.sb("x", [P, NT, D])
        s.xn = m.sb("xn", [P, NT, D])
        s.xnT = m.sb("xnT", [P, N])
        s.ident = m.sb("ident", [P, P])
        s.bank = [m.ps(f"bank{i}", [P, W]) for i in range(8)]
        with ExitStack() as block0:
            m0 = Memory(nc, block0)
            sems = Memory(nc, block0)
            s.s0 = m0.sb("s0", [P, NT, D])
            s.g0 = m0.sb("g0", [P, NT, D])
            with ExitStack() as attn:
                m1 = Memory(nc, attn)
                s.gate = m1.sb("gate", [P, NT, H * VD])
                s.o = m1.sb("o", [P, NT, H * VD])
                with ExitStack() as scan:
                    m2 = Memory(nc, scan)
                    s.kqv_w = m2.sb("kqv_w", [P, 4 * P])
                    s.conv_w = m2.sb("conv_w", [P, 4, CONV])
                    s.le = m2.sb("le", [P, P])
                    s.gt = m2.sb("gt", [P, P])
                    s.levels = m2.sb("levels", [P, LEVELS, P])
                    s.own = m2.sb("own", [P, H])
                    s.hT = m2.sb("hT", [P, N])
                    s.kqv = [m2.sb(f"kqv{j}", [P, N]) for j in range(4)]
                    s.rs = [m2.sb(f"rs{j}", [P, N]) for j in range(2)]
                    s.g = m2.sb("g", [P, NT, H])
                    s.beta = m2.sb("beta", [P, NT, H])
                    phase_norm(nc, sems, io, s)
                    phase_project(nc, sems, io, s)
                    phase_delta(nc, sems, io, s)
                phase_encode(nc, sems, io, s)
            phase_experts(nc, sems, io, s)
            clear(nc, sems.used)
        with ExitStack() as block1:
            m1 = Memory(nc, block1)
            s.s1 = m1.sb("s1", [P, NT, D])
            with ExitStack() as attn:
                m2 = Memory(nc, attn)
                s.cos = m2.sb("cos", [P, TB, HD])
                s.sin = m2.sb("sin", [P, TB, HD])
                s.kt = m2.sb("k_tern", [P, NT, INNER], BF16)
                s.vt = m2.sb("v_tern", [P, NT, INNER], BF16)
                s.bk = m2.sb("beta_k", [P, NT, NH])
                s.dd = m2.sb("dd", [P, NH, P])
                s.dt = m2.sb("decay_t", [P, IB, P])
                s.de = m2.sb("decay_e", [P, NH])
                phase_ternary(nc, m, io, s)
                phase_attend(nc, m, io, s)
            m3 = Memory(nc, block1)
            s.act = m3.sb("act_t", [P, NE // P, N])
            s.up = m3.sb("up", [P, NE // P, D])
            s.keymat = m3.sb("keymat", [P, 2 * PH * NK])
            s.keyrow = m3.sb("keyrow", [P, 2 * PH * NK])
            phase_keys(nc, m, io, s)
            phase_product_keys(nc, m, io, s, out)


def constants():
    f = np.float32
    i = np.arange(P)
    row, col = i[:, None], i[None, :]
    same = row // C == col // C
    levels = [(row // (2 << n) == col // (2 << n)) & ((row >> n) % 2 == 0) & ((col >> n) % 2 == 1) for n in range(LEVELS)]
    inv = (f(1) / f(10000.0) ** (np.arange(0, HD, 2, dtype=f) / f(HD))).astype(f)
    angle = (np.arange(T, dtype=f)[:, None] * inv[None, :]).astype(f)

    def by_tile(x):
        return np.ascontiguousarray(x.astype(f).reshape(TB, P, HD).transpose(1, 0, 2))

    cos, sin = np.cos(angle), np.sin(angle)
    return {
        "c_ident": np.eye(P, dtype=f),
        "c_head_ones": (row // KD == col // KD).astype(f),
        "c_own": (row // KD == np.arange(H)[None, :]).astype(f),
        "c_le": ((row <= col) & same).astype(f),
        "c_gt": ((row > col) & same).astype(f),
        "c_levels": np.stack(levels, 1).astype(f),
        "c_cos": by_tile(np.concatenate([cos, cos], 1)),
        "c_sin": by_tile(np.concatenate([-sin, sin], 1)),
        "c_gap": np.maximum(col - row, 0).astype(f),
        "c_le_full": (row <= col).astype(f),
        "c_pos1": np.tile((i + 1).astype(f), (P, 1)),
        "c_rev": (P - 1 - i).astype(f)[:, None],
    }


_AS_THEY_ARE = ["L0_attn_x", "L0_attn_ln1_g", "L0_attn_ln1_b", "L0_attn_ln2_g", "L0_attn_ln2_b", "L0_attn_rms_in_w", "L0_attn_Wq",
                "L0_attn_Wk", "L0_attn_Wv", "L0_attn_conv_q_w", "L0_attn_conv_k_w", "L0_attn_conv_v_w", "L0_attn_Wa",
                "L0_attn_dt_bias", "L0_attn_A_log", "L0_attn_Wb", "L0_attn_Wg", "L0_attn_o_norm_w", "L0_attn_Wo", "L0_attn_W2",
                "L0_attn_b2", "L0_ffn_W1", "L0_ffn_W2", "L0_ffn_b2", "L0_ffn_Wr", "L0_ffn_br", "L0_ffn_gamma", "L0_ffn_beta",
                "L1_attn_bb", "L1_attn_alpha_log", "L1_ffn_w_q", "L1_ffn_up_embed"]


def laid_out(x):
    return {
        "b1_by_feature": x["L0_ffn_b1"].reshape(E, FB, P).transpose(0, 2, 1),
        "L1_attn_WqT": x["L1_attn_Wq"].T,
        "L1_attn_WkT": x["L1_attn_Wk"].T,
        "L1_attn_WvT": x["L1_attn_Wv"].T,
        "L1_attn_WbT": x["L1_attn_Wb"].T,
        "L1_attn_WoT": x["L1_attn_Wo"].T,
        "alpha_log_by_parity": x["L1_attn_alpha_log"].reshape(IB, 2).T,
        "w_q_by_key_feature": x["L1_ffn_w_q"].T,
        "keys_by_feature": x["L1_ffn_keys"].transpose(3, 2, 0, 1).reshape(P, 2 * PH, NK),
        "bn_by_feature": np.stack([x["L1_ffn_bn_gamma"].reshape(2 * PH, P).T, x["L1_ffn_bn_beta"].reshape(2 * PH, P).T], 1),
        "down_by_feature": x["L1_ffn_down_embed"].T,
    }


def kernel(**inputs):
    import concourse.bacc as _bacc
    from concourse.bass_utils import run_bass_kernel_spmd as _run

    nc = _bacc.Bacc("TRN2", target_bir_lowering=False, num_devices=1)
    given = {k: np.asarray(v) for k, v in inputs.items()}
    arrays = {k: given[k] for k in _AS_THEY_ARE} | laid_out(given) | constants()
    io = {}
    for name in arrays:
        arrays[name] = np.ascontiguousarray(arrays[name])
        io[name] = nc.dram_tensor(name, arrays[name].shape, mybir.dt.from_np(arrays[name].dtype), kind="ExternalInput").ap()
    out = nc.dram_tensor("out", (B, T, D), F32, kind="ExternalOutput").ap()
    build(nc, io, out)
    r = _run(nc, [arrays], core_ids=[0])
    return r.results[0]["out"]
```
